# Optimizing a Trainium2 kernel written in Bass

```python
import numpy as np
import jax
import jax.numpy as jnp

def _softmax(x, axis=-1):
    return jax.nn.softmax(x, axis=axis)

def _gelu(x):
    return jax.nn.gelu(x, approximate=True)

def _silu(x):
    return jax.nn.silu(x)

def _sigmoid(x):
    return jax.nn.sigmoid(x)

def _layernorm(x, axis=-1, eps=1e-05):
    m = jnp.mean(x, axis=axis, keepdims=True)
    v = jnp.var(x, axis=axis, keepdims=True)
    return (x - m) / jnp.sqrt(v + eps)

def _scatter_add(tgt, idx, src, axis=0):
    return tgt.at[idx].add(src)

def _segment_sum(src, seg, n):
    return jax.ops.segment_sum(src, seg, n)
kernel_name = 'mk_flamingo_gated_d2_seqx_r8_5c645b'

def setup_inputs(seed: int=0):
    np.random.seed(seed)
    _w = jnp.asarray

    def _rec_inputs():
        import jax
        import jax.numpy as jnp
        _rk = jax.random.key(seed)
        x = -0.0002928 + 1 * jax.random.normal(jax.random.fold_in(_rk, 1), (4, 256, 128), jnp.float32)
        _lenS = 256 - jax.random.randint(jax.random.fold_in(_rk, 7), (4,), 0, max(1, 256 // 4) + 1, jnp.int32)
        _lenS2 = 256 - jax.random.randint(jax.random.fold_in(_rk, 8), (4,), 0, max(1, 256 // 4) + 1, jnp.int32)
        _ctx_1024P = jax.random.normal(jax.random.fold_in(_rk, 11), (4, 16, 128), jnp.float32)
        _ctx_1024c = jax.random.dirichlet(jax.random.fold_in(_rk, 511), 0.3 * jnp.ones((16,), jnp.float32), (4, 256))
        _ctx_1024t = jnp.einsum('bsk,bkd->bsd', _ctx_1024c, _ctx_1024P)
        _ctx_1024t = _ctx_1024t * jax.lax.rsqrt(jnp.mean(jnp.square(_ctx_1024t)) + 1e-12) * 0.953939
        ctx_1024 = -1.39393e-06 + 0.999914 * (_ctx_1024t + 0.3 * jax.random.normal(jax.random.fold_in(_rk, 611), (4, 256, 128), jnp.float32))
        _validS = jnp.arange(256)[None, :] < _lenS[:, None]
        _validS2 = jnp.arange(256)[None, :] < _lenS2[:, None]
        _causal = jnp.tril(jnp.ones((256, 256), dtype=bool))
        mask_Bx1xSxS2_ik1 = jnp.where(jnp.broadcast_to(_validS2[:, None, None, :], (4, 1, 256, 256)), 1, 0).astype(jnp.int32)
        _g = jax.random.normal(jax.random.fold_in(_rk, 9001), (2, 2), jnp.float32)
        _g = jnp.sign(_g) * jnp.maximum(jnp.abs(_g), 1.0) + (_g == 0) * 1.0
        g_xattn = _g[0]
        g_ffn = _g[1]
        return (x, ctx_1024, mask_Bx1xSxS2_ik1, g_xattn, g_ffn)
    x, ctx_1024, mask_Bx1xSxS2_ik1, g_xattn, g_ffn = _rec_inputs()

    def _L0_xattn_setup():
        import jax, jax.numpy as jnp
        import numpy as np
        B, S, E, H = (2, 256, 128, 16)
        D = E // H
        key = jax.random.key(seed)
        ks = jax.random.split(key, 14)
        inp = {'query': jax.random.normal(ks[0], (B, S, E), jnp.float32), 'key': jax.random.normal(ks[1], (B, S, E), jnp.float32), 'value': jax.random.normal(ks[2], (B, S, E), jnp.float32), 'adj': jax.random.normal(ks[3], (S, S), jnp.float32), 'mask': jax.random.randint(ks[4], (B, 1, S, S), 0, 2, jnp.int32)}
        sc = 1.0 / np.sqrt(E)
        inp['Wq'] = jax.random.normal(ks[5], (E, E), jnp.float32) * sc
        inp['bq'] = jax.random.normal(ks[6], (E,), jnp.float32) * sc
        inp['Wk'] = jax.random.normal(ks[7], (E, E), jnp.float32) * sc
        inp['bk'] = jax.random.normal(ks[8], (E,), jnp.float32) * sc
        inp['Wv'] = jax.random.normal(ks[9], (E, E), jnp.float32) * sc
        inp['bv'] = jax.random.normal(ks[10], (E,), jnp.float32) * sc
        inp['Wo'] = jax.random.normal(ks[11], (E, E), jnp.float32) * sc
        inp['bo'] = jax.random.normal(ks[12], (E,), jnp.float32) * sc
        return inp
    _L0_xattn_all = _L0_xattn_setup()
    _L0_xattn_in = {k: v for k, v in _L0_xattn_all.items() if k in ('adj', 'Wq', 'bq', 'Wk', 'bk', 'Wv', 'bv', 'Wo', 'bo')}
    del _L0_xattn_all

    def _L0_ffn_setup():
        import jax, jax.numpy as jnp
        import numpy as np
        E = 16
        G = 4
        EPG = E // G
        K = 4
        TOPK_GROUP = 2
        PER_GROUP_K = K // TOPK_GROUP

        def _route(xf, router_w, correction_bias):
            S = xf.shape[0]
            logits = xf @ router_w.T
            scores = jax.nn.sigmoid(logits)
            sb = scores + correction_bias
            grp_top = jax.lax.top_k(sb.reshape(S, G, EPG), PER_GROUP_K)[0]
            group_scores = grp_top.sum(axis=-1)
            _, group_idx = jax.lax.top_k(group_scores, TOPK_GROUP)
            group_mask = jnp.zeros((S, G), sb.dtype).at[jnp.arange(S)[:, None], group_idx].set(1.0)
            score_mask = jnp.broadcast_to(group_mask[:, :, None], (S, G, EPG)).reshape(S, E)
            masked = jnp.where(score_mask > 0, sb, -jnp.inf)
            _, topk_idx = jax.lax.top_k(masked, K)
            w = jnp.take_along_axis(scores, topk_idx, axis=1)
            w = w / (w.sum(axis=-1, keepdims=True) + 1e-20)
            return (topk_idx, w, scores)
        key = jax.random.key(seed)
        ks = jax.random.split(key, 9)
        B, T, C, H, HS = (2, 128, 128, 32, 256)
        std = 0.02
        return {'x': jax.random.normal(ks[0], (B, T, C), jnp.float32), 'router_w': jax.random.normal(ks[1], (E, C), jnp.float32) * std, 'correction_bias': jnp.zeros((E,), jnp.float32), 'gate_w': jax.random.normal(ks[2], (E, C, H), jnp.float32) * std, 'up_w': jax.random.normal(ks[3], (E, C, H), jnp.float32) * std, 'down_w': jax.random.normal(ks[4], (E, H, C), jnp.float32) * std, 'shared_gate_w': jax.random.normal(ks[5], (HS, C), jnp.float32) * std, 'shared_up_w': jax.random.normal(ks[6], (HS, C), jnp.float32) * std, 'shared_down_w': jax.random.normal(ks[7], (C, HS), jnp.float32) * std}
    _L0_ffn_all = _L0_ffn_setup()
    _L0_ffn_in = {k: v for k, v in _L0_ffn_all.items() if k in ('router_w', 'correction_bias', 'gate_w', 'up_w', 'down_w', 'shared_gate_w', 'shared_up_w', 'shared_down_w')}
    del _L0_ffn_all

    def _L1_xattn_setup():
        import jax, jax.numpy as jnp
        import numpy as np
        HEADS = 8
        DIM_HEAD = 64
        SCALE = 8.0
        EPS = 1e-05

        def layer_norm(x, g, b):
            mu = jnp.mean(x, axis=-1, keepdims=True)
            var = jnp.mean((x - mu) ** 2, axis=-1, keepdims=True)
            return (x - mu) * jax.lax.rsqrt(var + EPS) * g + b
        key = jax.random.key(seed)
        ks = jax.random.split(key, 6)
        b, n, dim = (4, 512, 128)
        inner = HEADS * DIM_HEAD
        return {'x': jax.random.normal(ks[0], (b, n, dim), jnp.float32), 'context': jax.random.normal(ks[1], (b, n, dim), jnp.float32), 'Wq': jax.random.normal(ks[2], (dim, inner), jnp.float32) * 0.03, 'Wkv': jax.random.normal(ks[3], (dim, 2 * inner), jnp.float32) * 0.03, 'null_kv': jax.random.normal(ks[4], (2, DIM_HEAD), jnp.float32), 'ln_q_g': jnp.ones((inner,), jnp.float32), 'ln_q_b': jnp.zeros((inner,), jnp.float32), 'ln_out_g': jnp.ones((inner,), jnp.float32), 'ln_out_b': jnp.zeros((inner,), jnp.float32), 'Wout': jax.random.normal(ks[5], (inner, dim), jnp.float32) * 0.03}
    _L1_xattn_all = _L1_xattn_setup()
    _L1_xattn_in = {k: v for k, v in _L1_xattn_all.items() if k in ('Wq', 'Wkv', 'null_kv', 'ln_q_g', 'ln_q_b', 'ln_out_g', 'ln_out_b', 'Wout')}
    del _L1_xattn_all

    def _L1_ffn_setup():
        import jax, jax.numpy as jnp
        import numpy as np
        D_MODEL = 128
        key = jax.random.key(seed)
        k_x, k_w, k_a1, k_a2 = jax.random.split(key, 4)
        x = jax.random.normal(k_x, (4, 256, D_MODEL), dtype=jnp.float32)
        weight = jax.random.normal(k_w, (D_MODEL, D_MODEL), dtype=jnp.float32) * 0.02
        aux_weight1 = jax.random.normal(k_a1, (D_MODEL, D_MODEL), dtype=jnp.float32) * 0.02
        aux_weight2 = jax.random.normal(k_a2, (D_MODEL, D_MODEL), dtype=jnp.float32) * 0.02
        bias = jnp.zeros((D_MODEL,), dtype=jnp.float32)
        return {'x': x, 'weight': weight, 'aux_weight1': aux_weight1, 'aux_weight2': aux_weight2, 'bias': bias}
    _L1_ffn_all = _L1_ffn_setup()
    _L1_ffn_in = {k: v for k, v in _L1_ffn_all.items() if k in ('weight', 'aux_weight1', 'aux_weight2', 'bias')}
    del _L1_ffn_all
    return {'x': x, 'ctx_1024': ctx_1024, 'mask_Bx1xSxS2_ik1': mask_Bx1xSxS2_ik1, 'g_xattn': g_xattn, 'g_ffn': g_ffn, 'L0_xattn_adj': _L0_xattn_in['adj'], 'L0_xattn_Wq': _L0_xattn_in['Wq'], 'L0_xattn_bq': _L0_xattn_in['bq'], 'L0_xattn_Wk': _L0_xattn_in['Wk'], 'L0_xattn_bk': _L0_xattn_in['bk'], 'L0_xattn_Wv': _L0_xattn_in['Wv'], 'L0_xattn_bv': _L0_xattn_in['bv'], 'L0_xattn_Wo': _L0_xattn_in['Wo'], 'L0_xattn_bo': _L0_xattn_in['bo'], 'L0_ffn_router_w': _L0_ffn_in['router_w'], 'L0_ffn_correction_bias': _L0_ffn_in['correction_bias'], 'L0_ffn_gate_w': _L0_ffn_in['gate_w'], 'L0_ffn_up_w': _L0_ffn_in['up_w'], 'L0_ffn_down_w': _L0_ffn_in['down_w'], 'L0_ffn_shared_gate_w': _L0_ffn_in['shared_gate_w'], 'L0_ffn_shared_up_w': _L0_ffn_in['shared_up_w'], 'L0_ffn_shared_down_w': _L0_ffn_in['shared_down_w'], 'L1_xattn_Wq': _L1_xattn_in['Wq'], 'L1_xattn_Wkv': _L1_xattn_in['Wkv'], 'L1_xattn_null_kv': _L1_xattn_in['null_kv'], 'L1_xattn_ln_q_g': _L1_xattn_in['ln_q_g'], 'L1_xattn_ln_q_b': _L1_xattn_in['ln_q_b'], 'L1_xattn_ln_out_g': _L1_xattn_in['ln_out_g'], 'L1_xattn_ln_out_b': _L1_xattn_in['ln_out_b'], 'L1_xattn_Wout': _L1_xattn_in['Wout'], 'L1_ffn_weight': _L1_ffn_in['weight'], 'L1_ffn_aux_weight1': _L1_ffn_in['aux_weight1'], 'L1_ffn_aux_weight2': _L1_ffn_in['aux_weight2'], 'L1_ffn_bias': _L1_ffn_in['bias']}

def reference(x, ctx_1024, mask_Bx1xSxS2_ik1, g_xattn, g_ffn, L0_xattn_adj, L0_xattn_Wq, L0_xattn_bq, L0_xattn_Wk, L0_xattn_bk, L0_xattn_Wv, L0_xattn_bv, L0_xattn_Wo, L0_xattn_bo, L0_ffn_router_w, L0_ffn_correction_bias, L0_ffn_gate_w, L0_ffn_up_w, L0_ffn_down_w, L0_ffn_shared_gate_w, L0_ffn_shared_up_w, L0_ffn_shared_down_w, L1_xattn_Wq, L1_xattn_Wkv, L1_xattn_null_kv, L1_xattn_ln_q_g, L1_xattn_ln_q_b, L1_xattn_ln_out_g, L1_xattn_ln_out_b, L1_xattn_Wout, L1_ffn_weight, L1_ffn_aux_weight1, L1_ffn_aux_weight2, L1_ffn_bias):
    import jax
    import jax.numpy as jnp

    def _L0_xattn_ref(query, key, value, adj, mask, Wq, bq, Wk, bk, Wv, bv, Wo, bo):
        import jax, jax.numpy as jnp
        import numpy as np
        B, S, E, H = (2, 256, 128, 16)
        D = E // H
        b, s, _ = query.shape

        def heads(x, W, bias):
            y = jnp.einsum('bse,ef->bsf', x, W.T) + bias
            return y.reshape(b, s, H, D).transpose(0, 2, 1, 3)
        Q = heads(query, Wq, bq)
        K = heads(key, Wk, bk)
        V = heads(value, Wv, bv)
        scores = jnp.einsum('bhqd,bhkd->bhqk', Q, K) / jnp.sqrt(jnp.float32(D))
        scores = scores + adj[None, None, :, :]
        scores = jnp.where(mask == 0, jnp.float32(-jnp.inf), scores)
        weights = jax.nn.softmax(scores, axis=-1)
        out = jnp.einsum('bhqk,bhkd->bhqd', weights, V)
        out = out.transpose(0, 2, 1, 3).reshape(b, s, E)
        return jnp.einsum('bse,ef->bsf', out, Wo.T) + bo

    def _L0_ffn_ref(x, router_w, correction_bias, gate_w, up_w, down_w, shared_gate_w, shared_up_w, shared_down_w):
        import jax, jax.numpy as jnp
        import numpy as np
        E = 16
        G = 4
        EPG = E // G
        K = 4
        TOPK_GROUP = 2
        PER_GROUP_K = K // TOPK_GROUP

        def _route(xf, router_w, correction_bias):
            S = xf.shape[0]
            logits = xf @ router_w.T
            scores = jax.nn.sigmoid(logits)
            sb = scores + correction_bias
            grp_top = jax.lax.top_k(sb.reshape(S, G, EPG), PER_GROUP_K)[0]
            group_scores = grp_top.sum(axis=-1)
            _, group_idx = jax.lax.top_k(group_scores, TOPK_GROUP)
            group_mask = jnp.zeros((S, G), sb.dtype).at[jnp.arange(S)[:, None], group_idx].set(1.0)
            score_mask = jnp.broadcast_to(group_mask[:, :, None], (S, G, EPG)).reshape(S, E)
            masked = jnp.where(score_mask > 0, sb, -jnp.inf)
            _, topk_idx = jax.lax.top_k(masked, K)
            w = jnp.take_along_axis(scores, topk_idx, axis=1)
            w = w / (w.sum(axis=-1, keepdims=True) + 1e-20)
            return (topk_idx, w, scores)
        B, T, C = x.shape
        S = B * T
        xf = x.reshape(S, C)
        sg = xf @ shared_gate_w.T
        su = xf @ shared_up_w.T
        shared_out = jax.nn.silu(sg) * su @ shared_down_w.T
        topk_idx, w, _scores = _route(xf, router_w, correction_bias)
        combine = jnp.zeros((S, E), xf.dtype).at[jnp.arange(S)[:, None], topk_idx].add(w)
        g = jnp.einsum('sc,ech->esh', xf, gate_w)
        u = jnp.einsum('sc,ech->esh', xf, up_w)
        h = jax.nn.silu(g) * u
        hw = h * combine.T[:, :, None]
        routed = jnp.einsum('esh,ehc->sc', hw, down_w)
        return (shared_out + routed).reshape(B, T, C)

    def _L1_xattn_ref(x, context, Wq, Wkv, null_kv, ln_q_g, ln_q_b, ln_out_g, ln_out_b, Wout):
        import jax, jax.numpy as jnp
        import numpy as np
        HEADS = 8
        DIM_HEAD = 64
        SCALE = 8.0
        EPS = 1e-05

        def layer_norm(x, g, b):
            mu = jnp.mean(x, axis=-1, keepdims=True)
            var = jnp.mean((x - mu) ** 2, axis=-1, keepdims=True)
            return (x - mu) * jax.lax.rsqrt(var + EPS) * g + b
        b, n, _ = x.shape
        m = context.shape[1]
        h, d = (HEADS, DIM_HEAD)
        q = x @ Wq
        kv = context @ Wkv
        k, v = jnp.split(kv, 2, axis=-1)
        q = layer_norm(q, ln_q_g, ln_q_b)
        split = lambda t: t.reshape(t.shape[0], t.shape[1], h, d).transpose(0, 2, 1, 3)
        q, k, v = (split(q), split(k), split(v))
        nk = jnp.broadcast_to(null_kv[0], (b, h, 1, d))
        nv = jnp.broadcast_to(null_kv[1], (b, h, 1, d))
        k = jnp.concatenate([nk, k], axis=2)
        v = jnp.concatenate([nv, v], axis=2)
        q = jax.nn.softmax(q, axis=-1) * SCALE
        k = jax.nn.softmax(k, axis=2)
        ctx = jnp.einsum('bhnd,bhne->bhde', k, v)
        out = jnp.einsum('bhnd,bhde->bhne', q, ctx)
        out = out.transpose(0, 2, 1, 3).reshape(b, n, h * d)
        out = layer_norm(out, ln_out_g, ln_out_b)
        return out @ Wout

    def _L1_ffn_ref(x, weight, aux_weight1, aux_weight2, bias):
        import jax, jax.numpy as jnp
        import numpy as np
        D_MODEL = 128
        h = jnp.einsum('btc,cd->btd', x, weight)
        h = jnp.einsum('btc,cd->btd', h, aux_weight1)
        h = jnp.einsum('btc,cd->btd', h, aux_weight2)
        return jnp.tanh(h + bias)
    x = x + jnp.tanh(g_xattn[0]) * _L0_xattn_ref(_layernorm(x, axis=-1), ctx_1024, ctx_1024, L0_xattn_adj, mask_Bx1xSxS2_ik1, L0_xattn_Wq, L0_xattn_bq, L0_xattn_Wk, L0_xattn_bk, L0_xattn_Wv, L0_xattn_bv, L0_xattn_Wo, L0_xattn_bo)
    x = x + jnp.tanh(g_ffn[0]) * _L0_ffn_ref(_layernorm(x, axis=-1), L0_ffn_router_w, L0_ffn_correction_bias, L0_ffn_gate_w, L0_ffn_up_w, L0_ffn_down_w, L0_ffn_shared_gate_w, L0_ffn_shared_up_w, L0_ffn_shared_down_w)
    x = x + jnp.tanh(g_xattn[1]) * _L1_xattn_ref(_layernorm(x, axis=-1), ctx_1024, L1_xattn_Wq, L1_xattn_Wkv, L1_xattn_null_kv, L1_xattn_ln_q_g, L1_xattn_ln_q_b, L1_xattn_ln_out_g, L1_xattn_ln_out_b, L1_xattn_Wout)
    x = x + jnp.tanh(g_ffn[1]) * _L1_ffn_ref(_layernorm(x, axis=-1), L1_ffn_weight, L1_ffn_aux_weight1, L1_ffn_aux_weight2, L1_ffn_bias)
    return x

_drawn_inputs = setup_inputs


def setup_inputs(seed=0):
    import zlib

    import numpy as np

    out = dict(_drawn_inputs(seed))
    spreads = {'g_ffn': (-1.0, 0.6),
     'L0_ffn_correction_bias': (0.0, 0.8),
     'L1_xattn_ln_q_g': (1.0, 0.6),
     'L1_xattn_ln_q_b': (0.0, 2.0),
     'L1_xattn_ln_out_g': (1.0, 0.2),
     'L1_xattn_ln_out_b': (0.0, 0.514),
     'L1_ffn_bias': (0.0, 0.8)}
    factors = {'L0_xattn_bq': 4.095,
     'L0_xattn_bk': 64.0,
     'L0_ffn_router_w': 8.0,
     'L0_ffn_gate_w': 8.0,
     'L0_ffn_up_w': 8.0,
     'L0_ffn_down_w': 8.0,
     'L0_ffn_shared_gate_w': 8.0,
     'L0_ffn_shared_up_w': 8.0,
     'L0_ffn_shared_down_w': 8.0,
     'L1_xattn_Wq': 4.346,
     'L1_xattn_null_kv': 2.725,
     'L1_ffn_weight': 7.755,
     'L1_ffn_aux_weight1': 7.562,
     'L1_ffn_aux_weight2': 7.659}
    for name, (base, spread) in spreads.items():
        noise = np.random.default_rng([zlib.crc32(name.encode()), seed]).standard_normal(out[name].shape)
        drawn = base * np.exp(spread * noise) if base else spread * noise
        out[name] = jnp.asarray(drawn.astype(out[name].dtype))
    for name, factor in factors.items():
        out[name] = (out[name] * factor).astype(out[name].dtype)
    return out
```

```python
from contextlib import ExitStack

import concourse.bass as bass
from concourse import mybir

F32 = mybir.dt.float32
BF16 = mybir.dt.bfloat16
I32 = mybir.dt.int32
ALU = mybir.AluOpType
ACT = mybir.ActivationFunctionType
AX = mybir.AxisListType

P = 128
B, S, E = 4, 256, 128
N = B * S
NT = N // P
HALF = N // 2
HT = NT // 2
H0, D0 = 16, 8
C = S // P
TERMS = [(0, 0), (0, 1), (1, 0), (0, 2), (1, 1), (2, 0)]
KROWS = len(TERMS) * D0
SLOTS = H0 // 2
GH = 8
LAG = 2 * GH
NEG = -1.0e30
EXP0, HID = 16, 32
RC = EXP0 * HID // P
SC = 256 // P
HC = RC + SC
TOPG, TOPK = 2, 4
H1, D1 = 8, 64
I1 = H1 * D1
PR = I1 // P
SCALE1 = 8.0
EPS = 1e-5
SENT = -2.0e38
STRUCK = 1.0e38


def build(nc, A, out):
    ctx = ExitStack()
    with ctx:
        def sb(name, shape, dt=F32):
            return ctx.enter_context(nc.sbuf_tensor(name, shape, dt))

        def sem(name):
            return ctx.enter_context(nc.semaphore(name))

        banks = [ctx.enter_context(nc.psum_tensor(f"bank{i}", [P, 512], F32)) for i in range(8)]
        bankS = banks[0:3]
        bankT = banks[3:6]
        bankO, bankM = banks[6], banks[7]

        x = sb("x", [P, NT, E])
        ctxT = sb("ctxT", [P, N])
        w_kT, w_vT, w_qT, w_oT = (sb(n, [P, E]) for n in ("w_kT", "w_vT", "w_qT", "w_oT"))
        bq_col, bk_col = sb("bq_col", [P, 1]), sb("bk_col", [P, 1])
        bv_row, bo_row = sb("bv_row", [P, E]), sb("bo_row", [P, E])
        gates = sb("gates", [P, 4])
        ident = sb("ident", [P, P])
        adj = sb("adj", [P, C, S])
        adjT = sb("adjT", [P, C, S])
        mask = sb("mask", [P, 2, C, S], I32)
        maskT = sb("maskT", [P, B, C, S], I32)
        w_router = sb("w_router", [P, EXP0])
        cb_row = sb("cb_row", [P, EXP0])
        w_gate = sb("w_gate", [P, HC, P])
        w_up = sb("w_up", [P, HC, P])
        w_down = sb("w_down", [P, HC, E])
        expand = sb("expand", [EXP0, RC, P])
        tri = sb("tri", [P, 4, 4])
        w1q = sb("w1q", [P, I1])
        w1kv = sb("w1kv", [P, 2 * I1])
        w1out = sb("w1out", [P, PR, E])
        nullk = sb("nullk", [P, 1])
        nullv = sb("nullv", [P, D1])
        lnq_g, lnq_b = sb("lnq_g", [P, I1]), sb("lnq_b", [P, I1])
        lno_g, lno_b = sb("lno_g", [P, PR]), sb("lno_b", [P, PR])
        fw_T, fa1_T, fa2 = sb("fw_T", [P, E]), sb("fa1_T", [P, E]), sb("fa2", [P, E])
        fb_row = sb("fb_row", [P, E])

        tg = sb("tg", [P, 4])
        identb = sb("identb", [P, P], BF16)
        half_neg = sb("half_neg", [P, 8])
        stats = sb("stats", [P, NT, 6])
        mv = sb("mv", [P, NT, 2])
        vare = sb("vare", [P, NT])
        rstd = sb("rstd", [P, NT])
        xn = sb("xn", [P, NT, E])
        xnT = sb("xnT", [P, N])
        kf = sb("kf", [P, N])
        kr = sb("kr", [P, N])
        kparts = sb("kparts", [P, 3, N], BF16)
        qf = sb("qf", [P, N])
        qr = sb("qr", [P, N])
        qparts = sb("qparts", [P, 3, N], BF16)
        qst = sb("qst", [P, SLOTS, N], BF16)
        kst = sb("kst", [P, SLOTS, N], BF16)
        vaug = sb("vaug", [P, NT, H0, D0 + 1])
        adjm = sb("adjm", [P, B, C, S], BF16)
        adjmT = maskT[:, :, :, :].bitcast(F32)
        mx = sb("mx", [P, 2, 2, C, GH // 2])
        mrow = sb("mrow", [2 * C * GH // 2, 2, P], BF16)
        sc_t = sb("sc_t", [P, 3, C * S])
        et = sb("et", [P, 4, C, S])
        orec = sb("orec", [P, C, H0])
        attn = sb("attn", [P, C, E])
        attnT = sb("attnT", [P, C, P])
        tgbo = sb("tgbo", [P, E])

        kmx = sb("kmx", [P, B, PR])
        kE = kf[:, :].rearrange("p (r n) -> p r n", r=2)
        ksum = sb("ksum", [P, B, PR])
        ek0 = sb("ek0", [P, B, PR])
        kden = sb("kden", [P, B, PR])
        krec = sb("krec", [P, B, PR])
        kEn = sb("kEn", [P, NT, I1])
        v1 = sb("v1", [P, NT, I1])
        early = et[:, :, :, :].rearrange("p r c s -> p (r c s)")
        nkv = early[:, 0:B * PR * D1].rearrange("p (n e) -> p n e", e=D1)
        ctx_t = early[:, B * PR * D1:2 * B * PR * D1].rearrange("p (n e) -> p n e", e=D1)
        ctx_bd = sb("ctx_bd", [P, B * PR, 2 * (D1 + 1)])

        w3 = sb("w3", [P, E])
        fa12 = sb("fa12", [P, E])
        wq_mean = sb("wq_mean", [P, 1])
        wq_c = w1q
        wq_cT = sb("wq_cT", [P, PR, P])
        wq_g = lnq_g
        gram = sb("gram", [P, P])
        wo_g = sb("wo_g", [P, PR, E])
        wo_c = wo_g
        ones_mean = sb("ones_mean", [P, P])
        lnb_bc = sb("lnb_bc", [P, PR, P])
        tgbw = sb("tgbw", [P, E])

        sil = qf[:, :].rearrange("p (r n) -> p r n", r=2)
        hid = kEn[:, 0:HC, :]
        elog = sb("elog", [P, HT * EXP0])
        score = sb("score", [P, HT, EXP0])
        biased = sb("biased", [P, HT * 4, 4])
        pairs = sb("pairs", [P, HT * 4, 6])
        gscore = sb("gscore", [P, HT, 4])
        gcmp = sb("gcmp", [P, HT, 4, 4])
        geq = sb("geq", [P, HT, 4, 4])
        grank = sb("grank", [P, HT * 4])
        gpen = sb("gpen", [P, HT * 4])
        cand = sb("cand", [P, HT, EXP0 + 4])
        best8 = sb("best8", [P, HT, 8])
        struck = sb("struck", [P, HT, EXP0 + 4])
        wts = sb("wts", [P, HT, EXP0])
        wsum = sb("wsum", [P, HT])
        wrec = sb("wrec", [P, HT])
        combT = sb("combT", [EXP0, HALF])

        qvar = sb("qvar", [P, NT])
        qrstd = sb("qrstd", [P, NT])
        junk = sb("junk", [P, E])
        late = v1[:, :, :].rearrange("p (k r) n -> p k r n", k=4)
        z = late[:, 0].rearrange("p r (h d) -> p r h d", h=H1)
        zmx = sb("zmx", [P, 2, H1])
        zs = late[:, 1].rearrange("p r (h d) -> p r h d", h=H1)
        qE = late[:, 2]
        qET = late[:, 3].rearrange("p r (c m) -> p r c m", c=PR)
        osum = sb("osum", [P, 2, H1])
        on = kf[:, :].rearrange("p (r n) -> p r n", r=2)
        onT = kr[:, :].rearrange("p (r c m) -> p r c m", r=2, c=PR)
        ostat = sb("ostat", [P, NT, 6])
        omv = sb("omv", [P, NT, 2])
        ove = sb("ove", [P, NT])
        orstd = sb("orstd", [P, NT])
        fh = sb("fh", [P, HT, E])
        ft = fh

        k_scr = nc.dram_tensor("k_scr", [3, P, N], BF16, kind="Internal").ap()
        q_scr = nc.dram_tensor("q_scr", [3, P, N], BF16, kind="Internal").ap()

        ld = {n: sem(f"ld_{n}") for n in ("x", "kv", "q", "small", "adj", "mask", "moe", "l1", "ffn", "id")}
        ld_maskq = [sem(f"ld_maskq{i}") for i in range(2)]
        own_dve, own_act, own_pool = sem("own_dve"), sem("own_act"), sem("own_pool")
        identb_ok, gates_ok, consts_ok = sem("identb_ok"), sem("gates_ok"), sem("consts_ok")
        kproj, vproj, qproj = sem("kproj"), sem("vproj"), sem("qproj")
        kf_ok, k1_ok, kparts_ok = sem("kf_ok"), sem("k1_ok"), sem("kparts_ok")
        qf_ok, qparts_ok = sem("qf_ok"), sem("qparts_ok")
        kspill, qspill, kst_ld, qst_ld = sem("kspill"), sem("qspill"), sem("kst_ld"), sem("qst_ld")
        kones = sem("kones")
        vaug_ok = sem("vaug_ok")
        adjm_ok, adjmT_ok = sem("adjm_ok"), sem("adjmT_ok")
        xbias_ok = sem("xbias_ok")
        ln_var = [sem(f"ln_var{i}") for i in range(4)]
        ln_rstd = [sem(f"ln_rstd{i}") for i in range(4)]
        ln_xn = [sem(f"ln_xn{i}") for i in range(4)]
        ln_tp = [sem(f"ln_tp{i}") for i in range(4)]
        ln_xT = [sem(f"ln_xT{i}") for i in range(4)]
        fa12_mm, fa12_ok, w3_mm, w3_ok = sem("fa12_mm"), sem("fa12_ok"), sem("w3_mm"), sem("w3_ok")
        wqc_ok, wqT_mm, wqT_ok, gram_mm, gram_ok = (sem(n) for n in ("wqc_ok", "wqT_mm", "wqT_ok", "gram_mm", "gram_ok"))
        wog_ok, wmean_mm, woc_ok, lnb_ok, bw_mm, bw_ok = (sem(n) for n in ("wog_ok", "wmean_mm", "woc_ok", "lnb_ok", "bw_mm", "bw_ok"))
        k1mm, k1max, k1exp, k1tp, k1n, v1mm, v1_ok = (sem(n) for n in ("k1mm", "k1max", "k1exp", "k1tp", "k1n", "v1mm", "v1_ok"))
        ek_ok, c1mm, c1read, ctx_ok = sem("ek_ok"), sem("c1mm"), sem("c1read"), sem("ctx_ok")
        s_mm, s_max, m_tp, m_row = (sem(n) for n in ("s_mm", "s_max", "m_tp", "m_row"))
        m_ld = [sem(f"m_ld{i}") for i in range(2)]
        t_mm, t_add, t_exp, pv_mm = (sem(n) for n in ("t_mm", "t_add", "t_exp", "pv_mm"))
        o_norm, a_tp, a_T, a_mm, x1_ok = (sem(n) for n in ("o_norm", "a_tp", "a_T", "a_mm", "x1_ok"))
        r_mm, r_exp, w_ok, w_tp, w_T, g_mm, sil_ok, c_mm, hid_ok, d_mm, x2_ok = (
            sem(n) for n in ("r_mm", "r_exp", "w_ok", "w_tp", "w_T", "g_mm", "sil_ok", "c_mm", "hid_ok", "d_mm", "x2_ok"))
        q_mm, y_mm, qv_ok, qr_ok, z_ok, zs_ok, qe_ok, e_tp, e_T, o_mm, on_ok, n_tp, n_T, ov_ok, or_ok, p_mm, x3_ok = (
            sem(n) for n in ("q_mm", "y_mm", "qv_ok", "qr_ok", "z_ok", "zs_ok", "qe_ok", "e_tp", "e_T", "o_mm",
                             "on_ok", "n_tp", "n_T", "ov_ok", "or_ok", "p_mm", "x3_ok"))
        xbias3 = sem("xbias3")
        f_mm, fh_ok, ft_ok, x4_ok, stored = (sem(n) for n in ("f_mm", "fh_ok", "ft_ok", "x4_ok", "stored"))

        def load(eng, group, dst, src):
            eng.dma_start(dst, src).then_inc(ld[group], 16)

        def loaded(eng, group):
            eng.wait_ge(ld[group], 16 * LOADS[group])

        LOADS = dict(x=1, kv=3, q=2, small=5, adj=2, mask=1, moe=10, l1=9, ffn=4, id=1)

        def head(i):
            b, h = divmod(i, H0)
            return b, h, h // 2, 64 * (h % 2)

        block = ctx.enter_context(nc.Block())

        @block.sync
        def _(sp):
            load(sp, "kv", ctxT[:, :], A["ctxT"])
            load(sp, "kv", w_kT[:, :], A["wkT"])
            load(sp, "x", x[:, :, :], A["x"])
            load(sp, "kv", w_vT[:, :], A["wvT"])
            load(sp, "q", w_qT[:, :], A["wqT"])
            load(sp, "q", w_oT[:, :], A["woT"])
            load(sp, "l1", w1kv[:, :], A["w1kv"])
            load(sp, "l1", w1q[:, :], A["w1q"])
            load(sp, "l1", w1out[:, :, :], A["w1out"])
            load(sp, "l1", nullk[:, :], A["nullk"])
            load(sp, "l1", nullv[:, :], A["nullv"])
            load(sp, "l1", lnq_g[:, :], A["lnq_g"])
            load(sp, "l1", lnq_b[:, :], A["lnq_b"])
            load(sp, "l1", lno_g[:, :], A["lno_g"])
            load(sp, "l1", lno_b[:, :], A["lno_b"])
            load(sp, "ffn", fw_T[:, :], A["fwT"])
            load(sp, "ffn", fa1_T[:, :], A["fa1T"])
            load(sp, "ffn", fa2[:, :], A["fa2"])
            load(sp, "ffn", fb_row[:, :], A["fb"])
            load(sp, "adj", adj[:, :, :], A["adj"])
            for b in range(2):
                sp.dma_start(mask[:, b, :, :], A["mask"][:, b]).then_inc(ld_maskq[b % 2], 16)
            load(sp, "adj", adjT[:, :, :], A["adjT"])
            load(sp, "mask", maskT[:, :, :, :], A["maskT"])

            def restack(parts, scr, stack, ready, spill, landed, which):
                sp.wait_ge(ready, 2)
                sp.dma_start(scr.rearrange("c p n -> p c n"), parts[:, :, :]).then_inc(spill, 16)
                sp.wait_ge(spill, 16)
                for c, term in enumerate(TERMS):
                    rows = scr[term[which]].rearrange("(s two d) n -> two d s n", two=2, d=D0)
                    for par in range(2):
                        r0 = 64 * par + c * D0
                        sp.dma_start(stack[r0:r0 + D0, :, :], rows[par]).then_inc(landed, 16)

            sp.wait_ge(kones, 1)
            restack(kparts, k_scr, kst, kparts_ok, kspill, kst_ld, 1)
            restack(qparts, q_scr, qst, qparts_ok, qspill, qst_ld, 0)
            load(sp, "moe", w_router[:, :], A["router_w"])
            load(sp, "moe", cb_row[:, :], A["cb"])
            load(sp, "moe", expand[:, :, :], A["expand"])
            load(sp, "moe", tri[:, :, :], A["tri"])
            load(sp, "moe", w_gate[:, 0:RC, :], A["gate_w"])
            load(sp, "moe", w_gate[:, RC:HC, :], A["sgate_w"])
            load(sp, "moe", w_up[:, 0:RC, :], A["up_w"])
            load(sp, "moe", w_up[:, RC:HC, :], A["sup_w"])
            load(sp, "moe", w_down[:, 0:RC, :], A["down_w"])
            load(sp, "moe", w_down[:, RC:HC, :], A["sdown_w"])
            for b in range(2, B):
                sp.wait_ge(adjm_ok, b - 1)
                sp.dma_start(mask[:, b % 2, :, :], A["mask"][:, b]).then_inc(ld_maskq[b % 2], 16)
            for g in range(2 * B):
                b, s0 = g // 2, (g % 2) * GH // 2
                sp.wait_ge(m_row, g + 1)
                for par in range(2):
                    for qc in range(C):
                        r0 = (par * C + qc) * GH // 2
                        t0 = b * S + qc * P
                        sp.dma_start(qst[64 * par + KROWS:64 * par + KROWS + 1, s0:s0 + GH // 2, t0:t0 + P],
                                     mrow[r0:r0 + GH // 2, g % 2, :]).then_inc(m_ld[g % 2], 16)
            for t in range(NT):
                sp.wait_ge(x4_ok, t // HT + 1)
                sp.dma_start(out[t], x[:, t, :]).then_inc(stored, 16)
            sp.wait_ge(stored, 16 * NT)

        @block.gpsimd
        def _(pool):
            steps = [0]

            def link(ins):
                steps[0] += 1
                ins.then_inc(own_pool, 1)
                pool.wait_ge(own_pool, steps[0])

            link(nc.gpsimd.memset(kst[32:64, :, :], 1.0))
            link(nc.gpsimd.memset(kst[96:128, :, :], 1.0))
            nc.gpsimd.memset(half_neg[:, :], -0.5).then_inc(kones, 1)
            pool.wait_ge(kones, 1)
            link(nc.gpsimd.memset(ones_mean[:, :], 1.0 / I1))
            nc.gpsimd.memset(vaug[:, :, :, D0:D0 + 1], 1.0).then_inc(consts_ok, 1)
            loaded(pool, "id")
            nc.gpsimd.tensor_copy(identb[:, :], ident[:, :]).then_inc(identb_ok, 1)

            def ln_power(i, half):
                t0 = half * HT
                pool.wait_ge(ln_var[i], half + 1)
                link(nc.gpsimd.tensor_scalar(vare[:, t0:t0 + HT], mv[:, t0:t0 + HT, 1], EPS, None, ALU.add))
                nc.gpsimd.tensor_tensor(rstd[:, t0:t0 + HT], vare[:, t0:t0 + HT], half_neg[:, 0:HT],
                                        ALU.pow).then_inc(ln_rstd[i], 1)

            for half in range(2):
                ln_power(0, half)
            for half in range(2):
                cols = slice(half * HALF, (half + 1) * HALF)
                pool.wait_ge(k1_ok, half + 1)
                link(nc.gpsimd.tensor_tensor(kr[:, cols], kf[:, cols], kparts[:, 0, cols], ALU.subtract))
                link(nc.gpsimd.tensor_copy(kparts[:, 1, cols], kr[:, cols]))
                nc.gpsimd.tensor_tensor(kparts[:, 2, cols], kr[:, cols], kparts[:, 1, cols],
                                        ALU.subtract).then_inc(kparts_ok, 1)
            pool.wait_ge(gates_ok, 1)
            link(nc.gpsimd.tensor_scalar(tgbo[:, :], bo_row[:, :], tg[:, 0:1], None, ALU.mult))
            pool.wait_ge(ln_xn[0], 2)
            nc.gpsimd.tensor_tensor(x[:, :, :], x[:, :, :],
                                    tgbo[:, :].unsqueeze(1).to_broadcast([P, NT, E]), ALU.add).then_inc(xbias_ok, 1)
            link(nc.gpsimd.memset(ctx_bd[:, :, :], 0.0))
            link(nc.gpsimd.memset(ctx_bd[0:D1, :, D1:D1 + 1], 1.0))
            link(nc.gpsimd.memset(ctx_bd[D1:P, :, 2 * D1 + 1:2 * D1 + 2], 1.0))
            nc.gpsimd.memset(cand[:, :, EXP0:EXP0 + 4], SENT).then_inc(consts_ok, 1)
            loaded(pool, "l1")
            for half in range(2):
                ln_power(1, half)
            for half in range(2):
                ln_power(2, half)
                pool.wait_ge(bw_ok, 1)
                pool.wait_ge(ln_xn[2], half + 1)
                t0 = half * HT
                nc.gpsimd.tensor_tensor(x[:, t0:t0 + HT, :], x[:, t0:t0 + HT, :],
                                        tgbw[:, :].unsqueeze(1).to_broadcast([P, HT, E]), ALU.add).then_inc(xbias3, 1)
                for k in range(HT + 1):
                    if k < HT:
                        t = t0 + k
                        pool.wait_ge(qv_ok, t + 1)
                        link(nc.gpsimd.tensor_scalar(qvar[:, t:t + 1], qvar[:, t:t + 1], EPS, None, ALU.add))
                        nc.gpsimd.tensor_tensor(qrstd[:, t:t + 1], qvar[:, t:t + 1], half_neg[:, 0:1],
                                                ALU.pow).then_inc(qr_ok, 1)
                        pool.wait_ge(z_ok, t + 1)
                        if t >= 2:
                            pool.wait_ge(qe_ok, t - 1)
                        nc.gpsimd.tensor_tensor(zs[:, t % 2, :, :], z[:, t % 2, :, :],
                                                zmx[:, t % 2, :].unsqueeze(2).to_broadcast([P, H1, D1]),
                                                ALU.subtract).then_inc(zs_ok, 1)
                    if k >= 1:
                        t = t0 + k - 1
                        pool.wait_ge(ov_ok, t + 1)
                        link(nc.gpsimd.tensor_scalar(ove[:, t:t + 1], omv[:, t, 1:2], EPS, None, ALU.add))
                        link(nc.gpsimd.tensor_tensor(orstd[:, t:t + 1], ove[:, t:t + 1], half_neg[:, 0:1], ALU.pow))
                        nc.gpsimd.tensor_scalar(orstd[:, t:t + 1], orstd[:, t:t + 1], tg[:, 1:2], None,
                                                ALU.mult).then_inc(or_ok, 1)
            for half in range(2):
                ln_power(3, half)

        def k1_evac(act, u):
            c, half = divmod(u, 2)
            act.wait_ge(k1tp, u + 1)
            nc.scalar.copy(kEn[:, half * HT:(half + 1) * HT, c * P:(c + 1) * P],
                           banks[6 + u % 2][:, :].rearrange("p (t c) -> p t c", t=HT)).then_inc(k1n, 1)

        @block.scalar
        def _(act):
            steps = [0]

            def link(ins):
                steps[0] += 1
                ins.then_inc(own_act, 1)
                act.wait_ge(own_act, steps[0])

            def ln_evac(i, half, bank):
                act.wait_ge(ln_tp[i], half + 1)
                nc.scalar.copy(xnT[:, half * HALF:(half + 1) * HALF], bank[:, :]).then_inc(ln_xT[i], 1)

            load(act, "id", ident[:, :], A["ident"])
            load(act, "small", bq_col[:, :], A["bq"])
            load(act, "small", bk_col[:, :], A["bk"])
            load(act, "small", bv_row[:, :], A["bv"])
            load(act, "small", bo_row[:, :], A["bo"])
            load(act, "small", gates[:, :], A["gates"])
            loaded(act, "small")
            nc.scalar.activation(tg[:, :], gates[:, :], ACT.Tanh).then_inc(gates_ok, 1)
            for half in range(2):
                cols = slice(half * HALF, (half + 1) * HALF)
                act.wait_ge(kproj, half + 1)
                link(nc.scalar.activation(kf[:, cols], bankT[half][:, :], ACT.Identity, bias=bk_col[:, :]))
                nc.scalar.copy(kparts[:, 0, cols], kf[:, cols]).then_inc(k1_ok, 1)
            for half in range(2):
                ln_evac(0, half, [bankS[2], bankT[2]][half])
            for half in range(2):
                cols = slice(half * HALF, (half + 1) * HALF)
                act.wait_ge(qf_ok, 2 * half + 1)
                nc.scalar.copy(qparts[:, 0, cols], qf[:, cols]).then_inc(qf_ok, 1)
            for u in range(2 * PR):
                c, half = divmod(u, 2)
                bank = banks[u % 4]
                if u == 0:
                    act.wait_ge(kparts_ok, 2)
                if u >= 2:
                    act.wait_ge(k1tp, u - 1)
                act.wait_ge(k1max, u + 1)
                for k in range(2):
                    b = 2 * half + k
                    nc.scalar.activation(kE[:, u % 2, k * S:(k + 1) * S], bank[:, k * S:(k + 1) * S], ACT.Exp,
                                         bias=kmx[:, b, c:c + 1], accum_out=ksum[:, b, c:c + 1])
                    last = nc.scalar.activation(ek0[:, b, c:c + 1], nullk[:, :], ACT.Exp, bias=kmx[:, b, c:c + 1])
                last.then_inc(k1exp, 1)
                if u >= 1:
                    k1_evac(act, u - 1)
            k1_evac(act, 2 * PR - 1)
            for i in range(B * H0 + LAG + 6):
                g = i // GH
                if i % GH == 3 and 1 <= g <= 2 * B:
                    act.wait_ge(m_tp, g)
                    if g >= 3:
                        act.wait_ge(m_ld[(g - 1) % 2], 64 * ((g - 1) // 2))
                    nc.scalar.mul(mrow[:, (g - 1) % 2, :], bankM[0:16, 0:P], -1.0).then_inc(m_row, 1)
                j = i - LAG
                if 0 <= j < B * H0:
                    act.wait_ge(t_add, j + 1)
                    if j >= 4:
                        act.wait_ge(pv_mm, j - 3)
                    nc.scalar.activation(et[:, j % 4, :, :].rearrange("p c s -> p (c s)"), sc_t[:, j % 3, :],
                                         ACT.Exp).then_inc(t_exp, 1)
                if j >= H0 and j % H0 == 4:
                    b = j // H0 - 1
                    act.wait_ge(a_tp, b + 1)
                    nc.scalar.copy(attnT[:, :, :].rearrange("p c s -> p (c s)"), bankM[:, 0:S]).then_inc(a_T, 1)
            for half in range(2):
                ln_evac(1, half, banks[0])
                act.wait_ge(r_mm, half + 1)
                if half:
                    act.wait_ge(w_ok, half)
                nc.scalar.activation(elog[:, :], banks[1][:, 0:HT * EXP0], ACT.Exp, scale=-1.0).then_inc(r_exp, 1)
                for c in range(HC):
                    u = half * HC + c
                    act.wait_ge(g_mm, u + 1)
                    if u >= 2:
                        act.wait_ge(hid_ok, u - 1)
                    nc.scalar.activation(sil[:, u % 2, :], banks[2 + 2 * (u % 2)][:, :], ACT.Silu).then_inc(sil_ok, 1)
                    if c == 0:
                        act.wait_ge(w_tp, half + 1)
                        nc.scalar.copy(combT[:, :], banks[1][0:EXP0, :]).then_inc(w_T, 1)
            for half in range(2):
                ln_evac(2, half, banks[0])
                for k in range(HT + 1):
                    if k < HT:
                        t = half * HT + k
                        act.wait_ge(zs_ok, t + 1)
                        if t >= 2:
                            act.wait_ge(e_tp, t - 1)
                        nc.scalar.activation(qE[:, t % 2, :], zs[:, t % 2, :, :].rearrange("p h d -> p (h d)"),
                                             ACT.Exp).then_inc(qe_ok, 1)
                        act.wait_ge(e_tp, t + 1)
                        nc.scalar.copy(qET[:, t % 2, :, :].rearrange("p c s -> p (c s)"), banks[3][:, :]).then_inc(e_T, 1)
                    if k >= 1:
                        t = half * HT + k - 1
                        act.wait_ge(n_tp, t + 1)
                        nc.scalar.copy(onT[:, t % 2, :, :].rearrange("p c s -> p (c s)"), banks[6][:, :]).then_inc(n_T, 1)
            for half in range(2):
                ln_evac(3, half, banks[0])
                act.wait_ge(fh_ok, half + 1)
                nc.scalar.activation(ft[:, :, :].rearrange("p t e -> p (t e)"), fh[:, :, :].rearrange("p t e -> p (t e)"),
                                     ACT.Tanh).then_inc(ft_ok, 1)

        @block.vector
        def _(dve):
            steps = [0]

            def link(ins):
                steps[0] += 1
                ins.then_inc(own_dve, 1)
                dve.wait_ge(own_dve, steps[0])

            def ln_stats(i, half):
                ts = range(half * HT, (half + 1) * HT)
                for t in ts:
                    last = nc.vector.bn_stats(stats[:, t, :], x[:, t, :])
                link(last)
                for t in ts:
                    last = nc.vector.bn_aggr(mv[:, t, :], stats[:, t, :])
                last.then_inc(ln_var[i], 1)

            def ln_apply(i, half):
                ts = range(half * HT, (half + 1) * HT)
                dve.wait_ge(ln_rstd[i], half + 1)
                if i:
                    dve.wait_ge(ln_tp[i - 1], half + 1)
                for t in ts:
                    last = nc.vector.tensor_scalar(xn[:, t, :], x[:, t, :], mv[:, t, 0:1], rstd[:, t:t + 1],
                                                   ALU.subtract, ALU.mult)
                last.then_inc(ln_xn[i], 1)

            loaded(dve, "x")
            ln_stats(0, 0)
            ln_stats(0, 1)
            dve.wait_ge(vproj, 2)
            dve.wait_ge(consts_ok, 1)
            loaded(dve, "small")
            for half in range(2):
                last = nc.vector.tensor_tensor(
                    vaug[:, half * HT:(half + 1) * HT, :, 0:D0],
                    bankS[half][:, :].rearrange("p (t h d) -> p t h d", t=HT, h=H0),
                    bv_row[:, :].rearrange("p (h d) -> p h d", h=H0).unsqueeze(1).to_broadcast([P, HT, H0, D0]), ALU.add)
            last.then_inc(vaug_ok, 1)
            ln_apply(0, 0)
            ln_apply(0, 1)
            for half in range(2):
                cols = slice(half * HALF, (half + 1) * HALF)
                dve.wait_ge(qproj, half + 1)
                nc.vector.tensor_scalar(qf[:, cols], [bankO, bankM][half][:, :], bq_col[:, :], float(D0) ** -0.5,
                                        ALU.add, ALU.mult).then_inc(qf_ok, 1)
                dve.wait_ge(qf_ok, 2 * half + 2)
                link(nc.vector.tensor_tensor(qr[:, cols], qf[:, cols], qparts[:, 0, cols], ALU.subtract))
                link(nc.vector.tensor_copy(qparts[:, 1, cols], qr[:, cols]))
                nc.vector.tensor_tensor(qparts[:, 2, cols], qr[:, cols], qparts[:, 1, cols],
                                        ALU.subtract).then_inc(qparts_ok, 1)
            loaded(dve, "l1")
            link(nc.vector.reduce_sum(wq_mean[:, :], w1q[:, :], AX.X))
            link(nc.vector.tensor_scalar(wq_mean[:, :], wq_mean[:, :], 1.0 / I1, None, ALU.mult))
            link(nc.vector.tensor_scalar(wq_c[:, :], w1q[:, :], wq_mean[:, :], None, ALU.subtract))
            nc.vector.tensor_tensor(wq_g[:, :], wq_c[:, :], lnq_g[:, :], ALU.mult).then_inc(wqc_ok, 1)
            for c in range(PR):
                nc.vector.tensor_scalar(wo_g[:, c, :], w1out[:, c, :], lno_g[:, c:c + 1], None, ALU.mult)
            last = nc.vector.tensor_copy(lnb_bc[:, :, :], lno_b[:, :].unsqueeze(2).to_broadcast([P, PR, P]))
            last.then_inc(wog_ok, 1)
            loaded(dve, "adj")
            loaded(dve, "mask")

            def masks(b):
                dve.wait_ge(ld_maskq[b % 2], 16 * (b // 2 + 1))
                addend = mask[:, b % 2, :, :].bitcast(F32)
                link(nc.vector.tensor_scalar(addend, mask[:, b % 2, :, :], 0.0, NEG, ALU.is_equal, ALU.mult))
                nc.vector.tensor_tensor(adjm[:, b, :, :], addend, adj[:, :, :], ALU.add).then_inc(adjm_ok, 1)
                link(nc.vector.tensor_scalar(adjmT[:, b], maskT[:, b, :, :], 0.0, NEG, ALU.is_equal, ALU.mult))
                nc.vector.tensor_tensor(adjmT[:, b], adjmT[:, b], adjT[:, :, :], ALU.add).then_inc(adjmT_ok, 1)

            masks(0)
            for u in range(2 * PR):
                c, half = divmod(u, 2)
                dve.wait_ge(k1mm, u + 1)
                link(nc.vector.tensor_reduce(kmx[:, 2 * half:2 * half + 2, c],
                                             banks[u % 4][:, :].rearrange("p (b s) -> p b s", b=2),
                                             AX.X, ALU.max))
                nc.vector.tensor_scalar(kmx[:, 2 * half:2 * half + 2, c], kmx[:, 2 * half:2 * half + 2, c],
                                        nullk[:, :], -1.0, ALU.max, ALU.mult).then_inc(k1max, 1)
                dve.wait_ge(v1mm, u + 1)
                nc.vector.tensor_copy(v1[:, u, :], banks[4 + u % 2][:, :]).then_inc(v1_ok, 1)
                if u == 0:
                    dve.wait_ge(fa12_mm, 1)
                    nc.vector.tensor_copy(fa12[:, :], banks[6][:, 0:E]).then_inc(fa12_ok, 1)
                if u == 1:
                    dve.wait_ge(wqT_mm, 1)
                    nc.vector.tensor_copy(wq_cT[:, :, :].rearrange("p c e -> p (c e)"), banks[7][:, :]).then_inc(wqT_ok, 1)
            dve.wait_ge(k1exp, 2 * PR)
            link(nc.vector.tensor_tensor(kden[:, :, :], ksum[:, :, :], ek0[:, :, :], ALU.add))
            link(nc.vector.reciprocal(krec[:, :, :], kden[:, :, :]))
            link(nc.vector.tensor_tensor(nkv[:, :, :], nullv[:, :].unsqueeze(1).to_broadcast([P, B * PR, D1]),
                                         ek0[:, :, :].rearrange("p b c -> p (b c)").unsqueeze(2).to_broadcast([P, B * PR, D1]),
                                         ALU.mult))
            for b in range(B):
                dve.wait_ge(c1mm, b + 1)
                pr = slice(b * PR, (b + 1) * PR)
                src = banks[b][:, :].rearrange("p (c e) -> p c e", c=PR)
                nc.vector.tensor_tensor(ctx_t[0:D1, pr, :], src[0:D1, :, 0:D1], nkv[0:D1, pr, :], ALU.add)
                nc.vector.tensor_tensor(ctx_t[D1:P, pr, :], src[D1:P, :, D1:P], nkv[D1:P, pr, :],
                                        ALU.add).then_inc(c1read, 1)
            dve.wait_ge(c1read, B)
            dve.wait_ge(consts_ok, 2)
            kb = krec[:, :, :].rearrange("p b c -> p (b c)").unsqueeze(2).to_broadcast([P, B * PR, D1])
            nc.vector.tensor_tensor(ctx_bd[0:D1, :, 0:D1], ctx_t[0:D1, :, :], kb[0:D1], ALU.mult)
            nc.vector.tensor_tensor(ctx_bd[D1:P, :, D1 + 1:2 * D1 + 1], ctx_t[D1:P, :, :], kb[D1:P],
                                    ALU.mult).then_inc(ctx_ok, 1)
            dve.wait_ge(w3_mm, 1)
            nc.vector.tensor_copy(w3[:, :], banks[5][:, 0:E]).then_inc(w3_ok, 1)
            dve.wait_ge(gram_mm, 1)
            nc.vector.tensor_scalar(gram[:, :], banks[6][:, 0:P], 1.0 / I1, None, ALU.mult).then_inc(gram_ok, 1)
            dve.wait_ge(wmean_mm, 1)
            nc.vector.tensor_tensor(wo_c[:, :, :], wo_g[:, :, :],
                                    banks[7][:, 0:E].unsqueeze(1).to_broadcast([P, PR, E]), ALU.subtract)
            dve.wait_ge(gates_ok, 1)
            nc.vector.tensor_scalar(tgbw[:, :], banks[7][:, E:2 * E], tg[:, 1:2], None, ALU.mult).then_inc(bw_ok, 1)

            for i in range(B * H0 + LAG + 8):
                if i < B * H0:
                    b, h, s, p0 = head(i)
                    g = i // GH
                    dve.wait_ge(s_mm, i + 1)
                    if g >= 2 and i % GH == 0:
                        dve.wait_ge(m_tp, g - 1)
                    nc.vector.tensor_reduce(mx[:, g % 2, h % 2, :, s % (GH // 2)],
                                            bankS[i % 3][:, :].rearrange("p (c s) -> p c s", c=C),
                                            AX.X, ALU.max).then_inc(s_max, 1)
                j = i - LAG
                if 0 <= j < B * H0:
                    dve.wait_ge(t_mm, j + 1)
                    if j >= 3:
                        dve.wait_ge(t_exp, j - 2)
                    nc.vector.tensor_tensor(sc_t[:, j % 3, :], bankT[j % 3][:, :],
                                            adjmT[:, j // H0].rearrange("p c s -> p (c s)"),
                                            ALU.add).then_inc(t_add, 1)
                if i < 4 * (B - 1) and i % 4 == 1:
                    masks(i // 4 + 1)
                if j >= H0 and j % H0 == 1:
                    b = j // H0 - 1
                    dve.wait_ge(pv_mm, (b + 1) * H0)
                    o = bankO[:, 0:C * H0 * (D0 + 1)].rearrange("p (c h d) -> p c h d", c=C, h=H0)
                    link(nc.vector.reciprocal(orec[:, :, :], o[:, :, :, D0]))
                    nc.vector.tensor_tensor(attn[:, :, :].rearrange("p c (h d) -> p c h d", h=H0), o[:, :, :, 0:D0],
                                            orec[:, :, :].unsqueeze(3).to_broadcast([P, C, H0, D0]),
                                            ALU.mult).then_inc(o_norm, 1)
                if j >= H0 and j % H0 == 6:
                    b = j // H0 - 1
                    dve.wait_ge(a_mm, b + 1)
                    dve.wait_ge(xbias_ok, 1)
                    nc.vector.scalar_tensor_tensor(
                        x[:, C * b:C * (b + 1), :], bankM[:, S:2 * S].rearrange("p (c e) -> p c e", c=C), tg[:, 0:1],
                        x[:, C * b:C * (b + 1), :], ALU.mult, ALU.add).then_inc(x1_ok, 1)
            dve.wait_ge(x1_ok, B)
            for half in range(2):
                ln_stats(1, half)
                ln_apply(1, half)
                dve.wait_ge(r_exp, half + 1)
                link(nc.vector.tensor_scalar(elog[:, :], elog[:, :], 1.0, None, ALU.add))
                link(nc.vector.reciprocal(score[:, :, :].rearrange("p t e -> p (t e)"), elog[:, :]))
                if half == 0:
                    loaded(dve, "moe")
                link(nc.vector.tensor_tensor(biased[:, :, :].rearrange("p (t g) e -> p t (g e)", t=HT), score[:, :, :],
                                             cb_row[:, :].unsqueeze(1).to_broadcast([P, HT, EXP0]), ALU.add))
                nc.vector.tensor_tensor(pairs[:, :, 0:3], biased[:, :, 0:3], biased[:, :, 1:4], ALU.add)
                nc.vector.tensor_tensor(pairs[:, :, 3:5], biased[:, :, 0:2], biased[:, :, 2:4], ALU.add)
                link(nc.vector.tensor_tensor(pairs[:, :, 5:6], biased[:, :, 0:1], biased[:, :, 3:4], ALU.add))
                link(nc.vector.tensor_reduce(gscore[:, :, :].rearrange("p t g -> p (t g)"), pairs[:, :, :], AX.X, ALU.max))
                other = gscore[:, :, :].unsqueeze(2).to_broadcast([P, HT, 4, 4])
                mine = gscore[:, :, :].unsqueeze(3).to_broadcast([P, HT, 4, 4])
                nc.vector.tensor_tensor(gcmp[:, :, :, :], other, mine, ALU.is_gt)
                link(nc.vector.tensor_tensor(geq[:, :, :, :], other, mine, ALU.is_equal))
                link(nc.vector.tensor_tensor(geq[:, :, :, :], geq[:, :, :, :],
                                             tri[:, :, :].unsqueeze(1).to_broadcast([P, HT, 4, 4]), ALU.mult))
                link(nc.vector.tensor_tensor(gcmp[:, :, :, :], gcmp[:, :, :, :], geq[:, :, :, :], ALU.add))
                link(nc.vector.reduce_sum(grank[:, :], gcmp[:, :, :, :].rearrange("p t g h -> p (t g) h"), AX.X))
                link(nc.vector.tensor_scalar(gpen[:, :], grank[:, :], float(TOPG), NEG, ALU.is_ge, ALU.mult))
                link(nc.vector.tensor_tensor(cand[:, :, 0:EXP0].rearrange("p t (g e) -> p t g e", g=4),
                                             biased[:, :, :].rearrange("p (t g) e -> p t g e", t=HT),
                                             gpen[:, :].rearrange("p (t g) -> p t g", t=HT).unsqueeze(3).to_broadcast([P, HT, 4, 4]),
                                             ALU.add))
                for t in range(HT):
                    last = nc.vector.max(best8[:, t, :], cand[:, t, 0:EXP0])
                link(last)
                link(nc.vector.memset(best8[:, :, TOPK:8], SENT))
                for t in range(HT):
                    last = nc.vector.match_replace(struck[:, t, :], best8[:, t, :], cand[:, t, :], STRUCK)
                link(last)
                link(nc.vector.tensor_scalar(wts[:, :, :], struck[:, :, 0:EXP0], STRUCK, None, ALU.is_equal))
                link(nc.vector.tensor_tensor(wts[:, :, :], wts[:, :, :], score[:, :, :], ALU.mult))
                link(nc.vector.reduce_sum(wsum[:, :], wts[:, :, :], AX.X))
                link(nc.vector.tensor_scalar(wsum[:, :], wsum[:, :], 1e-20, None, ALU.add))
                link(nc.vector.reciprocal(wrec[:, :], wsum[:, :]))
                nc.vector.tensor_tensor(wts[:, :, :], wts[:, :, :], wrec[:, :].unsqueeze(2).to_broadcast([P, HT, EXP0]),
                                        ALU.mult).then_inc(w_ok, 1)
                for c in range(HC):
                    u = half * HC + c
                    dve.wait_ge(sil_ok, u + 1)
                    if half:
                        dve.wait_ge(d_mm, half)
                    first = nc.vector.tensor_tensor(hid[:, c, :], sil[:, u % 2, :], banks[3 + 2 * (u % 2)][:, :], ALU.mult)
                    if c < RC:
                        link(first)
                        dve.wait_ge(c_mm, half * RC + c + 1)
                        first = nc.vector.tensor_tensor(hid[:, c, :], hid[:, c, :], banks[6][:, :], ALU.mult)
                    first.then_inc(hid_ok, 1)
                dve.wait_ge(d_mm, half + 1)
                t0 = half * HT
                link(nc.vector.scalar_tensor_tensor(x[:, t0:t0 + HT, :], banks[7][:, :].rearrange("p (t e) -> p t e", t=HT),
                                                    tg[:, 2:3], x[:, t0:t0 + HT, :], ALU.mult, ALU.add))
            for half in range(2):
                ln_stats(2, half)
                ln_apply(2, half)
                t0 = half * HT
                for k in range(HT + 2):
                    if k < HT:
                        t = t0 + k
                        dve.wait_ge(y_mm, t + 1)
                        nc.vector.tensor_tensor_reduce(out=junk[:, :], in0=banks[1][:, 0:P], in1=xn[:, t, :], scale=1.0,
                                                       scalar=0.0, op0=ALU.mult, op1=ALU.add,
                                                       accum_out=qvar[:, t:t + 1]).then_inc(qv_ok, 1)
                        dve.wait_ge(qr_ok, t + 1)
                        dve.wait_ge(q_mm, t + 1)
                        if t >= 2:
                            dve.wait_ge(zs_ok, t - 1)
                        link(nc.vector.scalar_tensor_tensor(z[:, t % 2, :, :].rearrange("p h d -> p (h d)"), banks[2][:, :],
                                                            qrstd[:, t:t + 1], lnq_b[:, :], ALU.mult, ALU.add))
                        nc.vector.tensor_reduce(zmx[:, t % 2, :], z[:, t % 2, :, :], AX.X, ALU.max).then_inc(z_ok, 1)
                    if 1 <= k <= HT:
                        t = t0 + k - 1
                        dve.wait_ge(o_mm, t + 1)
                        for q in range(2):
                            o = banks[4 + q][:, 0:4 * (D1 + 1)].rearrange("p (h e) -> p h e", h=4)
                            last = nc.vector.tensor_scalar(osum[:, t % 2, 4 * q:4 * q + 4], o[:, :, D1], 1.0 / SCALE1, None, ALU.mult)
                        link(last)
                        link(nc.vector.reciprocal(osum[:, t % 2, :], osum[:, t % 2, :]))
                        if t >= 2:
                            dve.wait_ge(n_tp, t - 1)
                        for q in range(2):
                            o = banks[4 + q][:, 0:4 * (D1 + 1)].rearrange("p (h e) -> p h e", h=4)
                            last = nc.vector.tensor_tensor(
                                on[:, t % 2, q * 256:(q + 1) * 256].rearrange("p (h e) -> p h e", h=4), o[:, :, 0:D1],
                                osum[:, t % 2, 4 * q:4 * q + 4].unsqueeze(2).to_broadcast([P, 4, D1]), ALU.mult)
                        last.then_inc(on_ok, 1)
                        dve.wait_ge(on_ok, t + 1)
                        link(nc.vector.bn_stats(ostat[:, t, :], on[:, t % 2, :]))
                        nc.vector.bn_aggr(omv[:, t, :], ostat[:, t, :]).then_inc(ov_ok, 1)
                    if k >= 2:
                        t = t0 + k - 2
                        dve.wait_ge(p_mm, t + 1)
                        dve.wait_ge(or_ok, t + 1)
                        dve.wait_ge(xbias3, half + 1)
                        nc.vector.scalar_tensor_tensor(x[:, t, :], banks[7][:, 0:E], orstd[:, t:t + 1], x[:, t, :],
                                                       ALU.mult, ALU.add).then_inc(x3_ok, 1)
            dve.wait_ge(x3_ok, NT)
            for half in range(2):
                ln_stats(3, half)
                ln_apply(3, half)
                t0 = half * HT
                dve.wait_ge(f_mm, half + 1)
                nc.vector.tensor_tensor(fh[:, :, :], banks[1][:, :].rearrange("p (t e) -> p t e", t=HT),
                                        fb_row[:, :].unsqueeze(1).to_broadcast([P, HT, E]), ALU.add).then_inc(fh_ok, 1)
                dve.wait_ge(ft_ok, half + 1)
                nc.vector.scalar_tensor_tensor(x[:, t0:t0 + HT, :], ft[:, :, :], tg[:, 3:4], x[:, t0:t0 + HT, :],
                                               ALU.mult, ALU.add).then_inc(x4_ok, 1)

        @block.tensor
        def _(pe):
            mm = nc.tensor.matmul

            def ln_transpose(i, half, bank):
                pe.wait_ge(ln_xn[i], half + 1)
                for k in range(HT):
                    last = nc.tensor.transpose(bank[:, k * P:(k + 1) * P], xn[:, half * HT + k, :], ident[:, :])
                last.then_inc(ln_tp[i], 1)

            loaded(pe, "kv")
            for half in range(2):
                mm(bankT[half][:, :], w_kT[:, :], ctxT[:, half * HALF:(half + 1) * HALF],
                   start=True, stop=True).then_inc(kproj, 1)
            for t in range(NT):
                last = mm(bankS[t // HT][:, (t % HT) * E:(t % HT + 1) * E], ctxT[:, t * P:(t + 1) * P], w_vT[:, :],
                          start=True, stop=True)
                if t % HT == HT - 1:
                    last.then_inc(vproj, 1)
            loaded(pe, "id")
            for half in range(2):
                ln_transpose(0, half, [bankS[2], bankT[2]][half])
            loaded(pe, "q")
            for half in range(2):
                pe.wait_ge(ln_xT[0], half + 1)
                mm([bankO, bankM][half][:, :], w_qT[:, :], xnT[:, half * HALF:(half + 1) * HALF],
                   start=True, stop=True).then_inc(qproj, 1)
            loaded(pe, "l1")
            loaded(pe, "ffn")
            pe.wait_ge(vaug_ok, 1)
            pe.wait_ge(k1_ok, 2)
            pe.wait_ge(ln_xT[0], 2)

            def k1_transpose(u):
                pe.wait_ge(k1exp, u + 1)
                if u >= 2:
                    pe.wait_ge(k1n, u - 1)
                elif u == 0:
                    pe.wait_ge(fa12_ok, 1)
                else:
                    pe.wait_ge(wqT_ok, 1)
                for k in range(4):
                    last = nc.tensor.transpose(banks[6 + u % 2][:, k * P:(k + 1) * P], kE[:, u % 2, k * P:(k + 1) * P],
                                               ident[:, :])
                last.then_inc(k1tp, 1)

            for u in range(2 * PR):
                c, half = divmod(u, 2)
                if u >= 4:
                    pe.wait_ge(k1exp, u - 3)
                mm(banks[u % 4][:, :], w1kv[:, c * P:(c + 1) * P], ctxT[:, half * HALF:(half + 1) * HALF],
                   start=True, stop=True).then_inc(k1mm, 1)
                if u >= 2:
                    pe.wait_ge(v1_ok, u - 1)
                mm(banks[4 + u % 2][:, :], ctxT[:, u * P:(u + 1) * P], w1kv[:, I1:2 * I1],
                   start=True, stop=True).then_inc(v1mm, 1)
                if u == 0:
                    pe.wait_ge(qf_ok, 4)
                    mm(banks[6][:, 0:E], fa1_T[:, :], fa2[:, :], start=True, stop=True).then_inc(fa12_mm, 1)
                    pe.wait_ge(wqc_ok, 1)
                    for k in range(PR):
                        last = nc.tensor.transpose(banks[7][:, k * P:(k + 1) * P], wq_c[:, k * P:(k + 1) * P], ident[:, :])
                    last.then_inc(wqT_mm, 1)
                if u >= 1:
                    k1_transpose(u - 1)
            k1_transpose(2 * PR - 1)
            pe.wait_ge(k1n, 2 * PR)
            pe.wait_ge(v1_ok, 2 * PR)
            for b in range(B):
                for c in range(PR):
                    for k in range(C):
                        t = b * C + k
                        last = mm(banks[b][:, c * P:(c + 1) * P], kEn[:, t, c * P:(c + 1) * P],
                                  v1[:, t, c * P:(c + 1) * P], start=(k == 0), stop=(k == C - 1))
                last.then_inc(c1mm, 1)
            mm(banks[5][:, 0:E], fw_T[:, :], fa12[:, :], start=True, stop=True).then_inc(w3_mm, 1)
            for c in range(PR):
                last = mm(banks[6][:, 0:P], wq_cT[:, c, :], wq_cT[:, c, :], start=(c == 0), stop=(c == PR - 1))
            last.then_inc(gram_mm, 1)
            pe.wait_ge(wog_ok, 1)
            for c in range(PR):
                mm(banks[7][:, 0:E], ones_mean[:, :], wo_g[:, c, :], start=(c == 0), stop=(c == PR - 1))
            for c in range(PR):
                last = mm(banks[7][:, E:2 * E], lnb_bc[:, c, :], w1out[:, c, :], start=(c == 0), stop=(c == PR - 1))
            last.then_inc(wmean_mm, 1)

            pe.wait_ge(c1read, B)
            pe.wait_ge(bw_ok, 1)
            pe.wait_ge(identb_ok, 1)
            pe.wait_ge(kst_ld, 16 * 2 * len(TERMS))
            pe.wait_ge(qst_ld, 16 * 2 * len(TERMS))

            def values(j):
                b, h, s, p0 = head(j)
                pe.wait_ge(t_exp, j + 1)
                if j % H0 == 0 and b:
                    pe.wait_ge(o_norm, b)
                for qc in range(C):
                    col = (qc * H0 + h) * (D0 + 1)
                    for kc in range(C):
                        last = mm(bankO[:, col:col + D0 + 1], et[:, j % 4, kc, qc * P:(qc + 1) * P],
                                  vaug[:, b * C + kc, h, :], start=(kc == 0), stop=(kc == C - 1))
                last.then_inc(pv_mm, 1)

            for i in range(B * H0 + LAG + 7):
                g = i // GH
                if i % GH == 1 and 1 <= g <= 2 * B:
                    pe.wait_ge(s_max, g * GH)
                    if g >= 2:
                        pe.wait_ge(m_row, g - 1)
                    if g >= 6 and g % 2 == 0:
                        pe.wait_ge(x1_ok, g // 2 - 2)
                    nc.tensor.transpose(bankM[0:16, 0:P],
                                        mx[:, (g - 1) % 2, :, :, :].rearrange("p a c s -> p (a c s)"),
                                        ident[:, :]).then_inc(m_tp, 1)
                if i < B * H0:
                    b, h, s, p0 = head(i)
                    if i >= 3:
                        pe.wait_ge(s_max, i - 2)
                    if h == 0:
                        pe.wait_ge(adjm_ok, b + 1)
                    mm(bankS[i % 3][:, :], identb[:, :], adjm[:, b, :, :].rearrange("p c s -> p (c s)"),
                       start=True, stop=False)
                    for qc in range(C):
                        last = mm(bankS[i % 3][:, qc * S:(qc + 1) * S],
                                  qst[p0:p0 + KROWS, s, b * S + qc * P:b * S + (qc + 1) * P],
                                  kst[p0:p0 + KROWS, s, b * S:(b + 1) * S], start=False, stop=(qc == C - 1))
                    last.then_inc(s_mm, 1)
                j = i - LAG
                if 0 <= j < B * H0:
                    b, h, s, p0 = head(j)
                    if j >= 3:
                        pe.wait_ge(t_add, j - 2)
                    if j % GH == 0:
                        pe.wait_ge(m_ld[j // GH % 2], 64 * (j // GH // 2 + 1))
                    if h == 0:
                        pe.wait_ge(adjmT_ok, b + 1)
                    for kc in range(C):
                        last = mm(bankT[j % 3][:, kc * S:(kc + 1) * S],
                                  kst[p0:p0 + KROWS + 1, s, b * S + kc * P:b * S + (kc + 1) * P],
                                  qst[p0:p0 + KROWS + 1, s, b * S:(b + 1) * S], start=True, stop=True)
                    last.then_inc(t_mm, 1)
                if 0 <= j - 1 < B * H0:
                    values(j - 1)
                if j >= H0 and j % H0 == 3:
                    b = j // H0 - 1
                    pe.wait_ge(o_norm, b + 1)
                    pe.wait_ge(m_row, min(2 * B, (i - 3) // GH))
                    for qc in range(C):
                        last = nc.tensor.transpose(bankM[:, qc * P:(qc + 1) * P], attn[:, qc, :], ident[:, :])
                    last.then_inc(a_tp, 1)
                if j >= H0 and j % H0 == 5:
                    b = j // H0 - 1
                    pe.wait_ge(a_T, b + 1)
                    for qc in range(C):
                        last = mm(bankM[:, S + qc * E:S + (qc + 1) * E], attnT[:, qc, :], w_oT[:, :], start=True, stop=True)
                    last.then_inc(a_mm, 1)
            pe.wait_ge(x1_ok, B)
            loaded(pe, "moe")
            for half in range(2):
                ln_transpose(1, half, banks[0])
                pe.wait_ge(ln_xT[1], half + 1)
                cols = slice(half * HALF, (half + 1) * HALF)
                if half:
                    pe.wait_ge(w_T, half)
                for k in range(HT):
                    last = mm(banks[1][:, k * EXP0:(k + 1) * EXP0], xnT[:, half * HALF + k * P:half * HALF + (k + 1) * P],
                              w_router[:, :], start=True, stop=True)
                last.then_inc(r_mm, 1)
                for c in range(HC + 1):
                    if c < HC:
                        u = half * HC + c
                        if u >= 2:
                            pe.wait_ge(hid_ok, u - 1)
                        mm(banks[2 + 2 * (u % 2)][:, :], w_gate[:, c, :], xnT[:, cols], start=True, stop=True)
                        mm(banks[3 + 2 * (u % 2)][:, :], w_up[:, c, :], xnT[:, cols], start=True, stop=True).then_inc(g_mm, 1)
                    if c == 1:
                        pe.wait_ge(w_ok, half + 1)
                        for k in range(HT):
                            last = nc.tensor.transpose(banks[1][0:EXP0, k * P:(k + 1) * P], wts[:, k, :], ident[:, :])
                        last.then_inc(w_tp, 1)
                        pe.wait_ge(w_T, half + 1)
                    if 1 <= c <= RC:
                        if half * RC + c - 1 >= 1:
                            n = half * RC + c - 1
                            pe.wait_ge(hid_ok, (n - 1) // RC * HC + (n - 1) % RC + 1)
                        mm(banks[6][:, :], expand[:, c - 1, :], combT[:, :], start=True, stop=True).then_inc(c_mm, 1)
                pe.wait_ge(hid_ok, (half + 1) * HC)
                if half:
                    pe.wait_ge(ln_var[1], 2)
                for k in range(HT):
                    for c in range(HC):
                        last = mm(banks[7][:, k * E:(k + 1) * E], hid[:, c, k * P:(k + 1) * P], w_down[:, c, :],
                                  start=(c == 0), stop=(c == HC - 1))
                last.then_inc(d_mm, 1)
            pe.wait_ge(ctx_ok, 1)
            for half in range(2):
                ln_transpose(2, half, banks[0])
                pe.wait_ge(ln_xT[2], half + 1)
                for k in range(HT + 2):
                    if k < HT:
                        t = half * HT + k
                        if t:
                            pe.wait_ge(qv_ok, t)
                            pe.wait_ge(z_ok, t)
                        mm(banks[1][:, 0:P], xnT[:, t * P:(t + 1) * P], gram[:, :], start=True, stop=True).then_inc(y_mm, 1)
                        mm(banks[2][:, :], xnT[:, t * P:(t + 1) * P], wq_g[:, :], start=True, stop=True).then_inc(q_mm, 1)
                    if 1 <= k <= HT:
                        t = half * HT + k - 1
                        if t:
                            pe.wait_ge(on_ok, t)
                        pe.wait_ge(e_T, t + 1)
                        for c in range(PR):
                            col = (c % 2) * 2 * (D1 + 1)
                            last = mm(banks[4 + c // 2][:, col:col + 2 * (D1 + 1)], qET[:, t % 2, c, :],
                                      ctx_bd[:, t // C * PR + c, :], start=True, stop=True)
                        last.then_inc(o_mm, 1)
                    if k < HT:
                        t = half * HT + k
                        pe.wait_ge(qe_ok, t + 1)
                        for c in range(PR):
                            last = nc.tensor.transpose(banks[3][:, c * P:(c + 1) * P], qE[:, t % 2, c * P:(c + 1) * P], ident[:, :])
                        last.then_inc(e_tp, 1)
                    if 1 <= k <= HT:
                        t = half * HT + k - 1
                        pe.wait_ge(on_ok, t + 1)
                        if t:
                            pe.wait_ge(n_T, t)
                        for c in range(PR):
                            last = nc.tensor.transpose(banks[6][:, c * P:(c + 1) * P], on[:, t % 2, c * P:(c + 1) * P], ident[:, :])
                        last.then_inc(n_tp, 1)
                        pe.wait_ge(n_T, t + 1)
                        if t:
                            pe.wait_ge(x3_ok, t)
                        for c in range(PR):
                            last = mm(banks[7][:, 0:E], onT[:, t % 2, c, :], wo_c[:, c, :], start=(c == 0), stop=(c == PR - 1))
                        last.then_inc(p_mm, 1)
            pe.wait_ge(w3_ok, 1)
            for half in range(2):
                ln_transpose(3, half, banks[0])
                pe.wait_ge(ln_xT[3], half + 1)
                if half:
                    pe.wait_ge(fh_ok, half)
                for k in range(HT):
                    last = mm(banks[1][:, k * E:(k + 1) * E], xnT[:, half * HALF + k * P:half * HALF + (k + 1) * P],
                              w3[:, :], start=True, stop=True)
                last.then_inc(f_mm, 1)


def kernel(**inputs):
    import numpy as np
    import concourse.bacc as bacc
    from concourse.bass_utils import run_bass_kernel_spmd as run

    I = {k: np.asarray(v) for k, v in inputs.items()}

    def rows(v):
        return np.broadcast_to(v.reshape(1, -1), (P, v.size))

    def tiles(v):
        return v.reshape(-1, P, v.shape[-1]).transpose(1, 0, 2)

    mask = I["mask_Bx1xSxS2_ik1"][:, 0]
    lay = {
        "x": tiles(I["x"].reshape(N, E)),
        "ctxT": I["ctx_1024"].reshape(N, E).T,
        "wkT": I["L0_xattn_Wk"].T, "wvT": I["L0_xattn_Wv"].T, "wqT": I["L0_xattn_Wq"].T, "woT": I["L0_xattn_Wo"].T,
        "bq": I["L0_xattn_bq"].reshape(P, 1), "bk": I["L0_xattn_bk"].reshape(P, 1),
        "bv": rows(I["L0_xattn_bv"]), "bo": rows(I["L0_xattn_bo"]),
        "gates": rows(np.concatenate([I["g_xattn"], I["g_ffn"]])),
        "ident": np.eye(P, dtype=np.float32),
        "tri": np.broadcast_to(np.tril(np.ones((4, 4), np.float32), -1), (P, 4, 4)),
        "expand": np.repeat(np.eye(EXP0, dtype=np.float32), HID, 1).reshape(EXP0, RC, P),
        "adj": tiles(I["L0_xattn_adj"]), "adjT": tiles(I["L0_xattn_adj"].T),
        "mask": mask.reshape(B, C, P, S).transpose(2, 0, 1, 3),
        "maskT": mask.transpose(0, 2, 1).reshape(B, C, P, S).transpose(2, 0, 1, 3),
        "router_w": I["L0_ffn_router_w"].T, "cb": rows(I["L0_ffn_correction_bias"]),
        "gate_w": I["L0_ffn_gate_w"].transpose(1, 0, 2).reshape(P, RC, P),
        "up_w": I["L0_ffn_up_w"].transpose(1, 0, 2).reshape(P, RC, P),
        "down_w": tiles(I["L0_ffn_down_w"].reshape(EXP0 * HID, E)),
        "sgate_w": I["L0_ffn_shared_gate_w"].T.reshape(P, SC, P), "sup_w": I["L0_ffn_shared_up_w"].T.reshape(P, SC, P),
        "sdown_w": tiles(I["L0_ffn_shared_down_w"].T),
        "w1q": I["L1_xattn_Wq"], "w1kv": I["L1_xattn_Wkv"], "w1out": tiles(I["L1_xattn_Wout"]),
        "nullk": np.concatenate([I["L1_xattn_null_kv"][0]] * 2).reshape(P, 1), "nullv": rows(I["L1_xattn_null_kv"][1]),
        "lnq_g": rows(I["L1_xattn_ln_q_g"]), "lnq_b": rows(I["L1_xattn_ln_q_b"]),
        "lno_g": I["L1_xattn_ln_out_g"].reshape(PR, P).T, "lno_b": I["L1_xattn_ln_out_b"].reshape(PR, P).T,
        "fwT": I["L1_ffn_weight"].T, "fa1T": I["L1_ffn_aux_weight1"].T, "fa2": I["L1_ffn_aux_weight2"],
        "fb": rows(I["L1_ffn_bias"]),
    }
    nc = bacc.Bacc("TRN2", target_bir_lowering=False, num_devices=1)
    arrays, A = {}, {}
    for name, a in lay.items():
        a = np.ascontiguousarray(a)
        arrays[f"in_{name}"] = a
        A[name] = nc.dram_tensor(f"in_{name}", a.shape, mybir.dt.from_np(a.dtype), kind="ExternalInput").ap()
    out = nc.dram_tensor("out", (NT, P, E), F32, kind="ExternalOutput").ap()
    build(nc, A, out)
    r = run(nc, [arrays], core_ids=[0])
    return r.results[0]["out"].reshape(B, S, E)
```

```python
from contextlib import ExitStack

import concourse.bass as bass
from concourse import mybir

F32 = mybir.dt.float32
BF16 = mybir.dt.bfloat16
I32 = mybir.dt.int32
ALU = mybir.AluOpType
ACT = mybir.ActivationFunctionType
AX = mybir.AxisListType

P = 128
B, S, E = 4, 256, 128
N = B * S
NT = N // P
HALF = N // 2
HT = NT // 2
H0, D0 = 16, 8
C = S // P
TERMS = [(0, 0), (0, 1), (0, 2), (1, 0), (1, 1), (2, 0)]
Q_RUNS = [(0, 1, 3), (1, 1, 2), (2, 1, 1)]
K_RUNS = [(0, 3, 1), (0, 2, 1), (0, 1, 1)]
KROWS = len(TERMS) * D0
SLOTS = H0 // 2
SH = 4
GH = 8
LAG = 2 * GH
NEG = -1.0e30
EXP0, HID = 16, 32
RC = EXP0 * HID // P
SC = 256 // P
HC = RC + SC
TOPG, TOPK = 2, 4
H1, D1 = 8, 64
I1 = H1 * D1
PR = I1 // P
SCALE1 = 8.0
EPS = 1e-5
AW = D0 + 1
GU = [RC, RC + 1, 0, 1, 2, 3]
STEPS = B * H0 + LAG
SIDE = 35

STAGES = {
    2: [("out_tp0", "X"), ("out_tp1", "Y")],
    3: [("attn_tp", "M")],
    4: [("attn_proj", "M")],
    6: [("tp1", "X")],
    7: [("logits", "M"), ("gu0", "X")],
    8: [("gu1", "Y")],
    9: [("gu2", "X")],
    10: [("gu3", "Y"), ("wts_tp", "M")],
    11: [("comb0", "M")],
    12: [("gu4", "Y")],
    13: [("gu5", "X")],
    14: [("comb1", "M")],
    15: [("down", "M")],
    17: [("tp2", "X")],
    18: [("gram", "M")],
    19: [("q0", "O")],
    20: [("q1", "X")],
    22: [("e_tp0", "O")],
    23: [("oa0", "Y"), ("ob0", "O")],
    24: [("n_tp0", "O")],
    26: [("e_tp1", "O")],
    27: [("oa1", "X"), ("ob1", "O")],
    28: [("n_tp1", "O")],
    30: [("proj1", "Y")],
    32: [("tp3", "O")],
    33: [("ffn", "Y")],
}


def offsets(i):
    return [(b, i - H0 * (b + 2)) for b in range(B) if 0 <= i - H0 * (b + 2) < SIDE]


def bank_turns():
    turns, filled = {}, dict.fromkeys("OMXY", 0)

    def take(stage, key, bank):
        turns[stage, key] = (bank, filled[bank])
        filled[bank] += 1

    for i in range(H0 * (B + 1) + SIDE):
        if i % GH == 1 and 1 <= i // GH <= 2 * B:
            take("max_tp", i // GH - 1, "M")
        j = i - LAG
        if j >= SH + 1 and (j - SH - 1) % SH == 0 and (j - SH - 1) // SH < B * H0 // SH:
            take("values", (j - SH - 1) // SH, "O")
        for b, o in offsets(i):
            for stage, bank in STAGES.get(o, []):
                take(stage, b, bank)
    return turns


SENT = -2.0e38
STRUCK = 1.0e38


def build(nc, A, out):
    ctx = ExitStack()
    with ctx:
        def sb(name, shape, dt=F32):
            return ctx.enter_context(nc.sbuf_tensor(name, shape, dt))

        def sem(name):
            return ctx.enter_context(nc.semaphore(name))

        banks = [ctx.enter_context(nc.psum_tensor(f"bank{i}", [P, 512], F32)) for i in range(8)]
        bankS = banks[6:8]
        bankT = banks[0:2]
        shared = dict(zip("OMXY", banks[2:6]))

        x = sb("x", [P, NT, E])
        ctxT = sb("ctxT", [P, N])
        w_kT, w_vT, w_qT, w_oT = (sb(n, [P, E]) for n in ("w_kT", "w_vT", "w_qT", "w_oT"))
        bq_col, bk_col = sb("bq_col", [P, 1]), sb("bk_col", [P, 1])
        bv_row, bo_row = sb("bv_row", [P, E]), sb("bo_row", [P, E])
        gates = sb("gates", [P, 4])
        ident = sb("ident", [P, P])
        identb = sb("identb", [P, P], BF16)
        adj = sb("adj", [P, C, S])
        adjT = sb("adjT", [P, C, S])
        mask = sb("mask", [P, 2, C, S], I32)
        maskT = sb("maskT", [P, B, C, S], I32)
        w_router = sb("w_router", [P, EXP0])
        cb_row = sb("cb_row", [P, EXP0])
        w_gate = sb("w_gate", [P, HC, P])
        w_up = sb("w_up", [P, HC, P])
        w_down = sb("w_down", [P, HC, E])
        expand = sb("expand", [EXP0, RC, P])
        tri = sb("tri", [P, 4, 4])
        w1q = sb("w1q", [P, I1])
        w1kv = sb("w1kv", [P, 2 * I1])
        w1out = sb("w1out", [P, PR, E])
        nullk = sb("nullk", [P, 1])
        nullv = sb("nullv", [P, D1])
        lnq_g, lnq_b = sb("lnq_g", [P, I1]), sb("lnq_b", [P, I1])
        lno_g, lno_b = sb("lno_g", [P, PR]), sb("lno_b", [P, PR])
        fw_T, fa1_T, fa2 = sb("fw_T", [P, E]), sb("fa1_T", [P, E]), sb("fa2", [P, E])
        fb_row = sb("fb_row", [P, E])

        tg = sb("tg", [P, 4])
        tg_half = sb("tg_half", [P, 1])
        half_neg = sb("half_neg", [P, 8])
        stats = sb("stats", [P, NT, 6])
        mv = sb("mv", [P, NT, 2])
        vare = sb("vare", [P, NT])
        rstd = sb("rstd", [P, NT])
        xn = sb("xn", [P, NT, E])
        xnT = sb("xnT", [P, N])
        kf = sb("kf", [P, N])
        kr = sb("kr", [P, N])
        kparts = sb("kparts", [P, 3, N], BF16)
        qf = sb("qf", [P, N])
        qr = sb("qr", [P, N])
        qparts = sb("qparts", [P, 3, N], BF16)
        qst = sb("qst", [P, SLOTS, N], BF16)
        kst = sb("kst", [P, SLOTS, N], BF16)
        vaug = sb("vaug", [P, NT, H0 * AW + 32 - AW])
        vheads = vaug[:, :, 0:H0 * AW].rearrange("p t (h w) -> p t h w", h=H0)
        adjm = sb("adjm", [P, B, C, S], BF16)
        adjmT = maskT[:, :, :, :].bitcast(F32)
        mx = sb("mx", [P, 2, 2, C, GH // 2])
        mrow = sb("mrow", [2 * C * GH // 2, 2, P], BF16)
        sc_t = sb("sc_t", [P, 2, C * S])
        et = sb("et", [P, 2 * SH, C, S])
        outT = qr[:, :].rearrange("p (n s) -> p n s", n=SH)
        orec = sb("orec", [P, C, H0])
        attn = sb("attn", [P, C, E])
        attnT = sb("attnT", [P, C * P])
        tgbo = sb("tgbo", [P, E])

        kmx = sb("kmx", [P, B, PR])
        ksum = sb("ksum", [P, B, PR])
        ek0 = sb("ek0", [P, B, PR])
        kden = sb("kden", [P, B, PR])
        krec = sb("krec", [P, B, PR])
        kEn = sb("kEn", [P, NT, I1])
        v1 = sb("v1", [P, NT, I1])
        early = et[:, :, :, :].rearrange("p r c s -> p (r c s)")
        nkv = early[:, 0:B * PR * D1].rearrange("p (n e) -> p n e", e=D1)
        kE = early[:, 2 * B * PR * D1:2 * B * PR * D1 + N].rearrange("p (r n) -> p r n", r=2)
        ctx_t = early[:, B * PR * D1:2 * B * PR * D1].rearrange("p (n e) -> p n e", e=D1)
        ctx_bd = sb("ctx_bd", [P, B * PR, 2 * (D1 + 1)])
        w3 = sb("w3", [P, E])
        fa12 = sb("fa12", [P, E])
        wq_mean = sb("wq_mean", [P, 1])
        wq_c = w1q
        wq_cT = sb("wq_cT", [P, PR * P])
        wq_g = lnq_g
        gram = sb("gram", [P, P])
        wo_g = sb("wo_g", [P, PR, E])
        wo_c = wo_g
        ones_mean = sb("ones_mean", [P, P])
        lnb_bc = sb("lnb_bc", [P, PR, P])
        tgbw = sb("tgbw", [P, E])

        spent = kEn[:, :, :].rearrange("p t n -> p (t n)")
        hid = spent[:, 0:HC * S].rearrange("p (c s) -> p c s", c=HC)
        sil = spent[:, HC * S:(HC + 2) * S].rearrange("p (r s) -> p r s", r=2)
        up = spent[:, (HC + 2) * S:(HC + 4) * S].rearrange("p (r s) -> p r s", r=2)
        th = spent[:, (HC + 4) * S:(HC + 6) * S].rearrange("p (r s) -> p r s", r=2)
        TB = C
        elog = sb("elog", [P, TB * EXP0])
        score = sb("score", [P, TB, EXP0])
        biased = sb("biased", [P, TB * 4, 4])
        pairs = sb("pairs", [P, TB * 4, 6])
        gscore = sb("gscore", [P, TB, 4])
        gcmp = sb("gcmp", [P, TB, 4, 4])
        geq = sb("geq", [P, TB, 4, 4])
        grank = sb("grank", [P, TB * 4])
        gpen = sb("gpen", [P, TB * 4])
        cand = sb("cand", [P, TB, EXP0 + 4])
        best8 = sb("best8", [P, TB, 8])
        struck = sb("struck", [P, TB, EXP0 + 4])
        wts = sb("wts", [P, TB, EXP0])
        wsum = sb("wsum", [P, TB])
        wrec = sb("wrec", [P, TB])
        combT = sb("combT", [EXP0, S])

        qvar = sb("qvar", [P, NT])
        qrstd = sb("qrstd", [P, NT])
        junk = sb("junk", [P, E])
        late = v1[:, :, :].rearrange("p (k r) n -> p k r n", k=4)
        z = late[:, 0].rearrange("p r (h d) -> p r h d", h=H1)
        zmx = sb("zmx", [P, 2, H1])
        zs = late[:, 1].rearrange("p r (h d) -> p r h d", h=H1)
        qE = late[:, 2]
        qET = late[:, 3].rearrange("p r (c m) -> p r c m", c=PR)
        osum = sb("osum", [P, 2, H1])
        on = kf[:, :].rearrange("p (r n) -> p r n", r=2)
        onT = kr[:, :].rearrange("p (r c m) -> p r c m", r=2, c=PR)
        ostat = sb("ostat", [P, NT, 6])
        omv = sb("omv", [P, NT, 2])
        ove = sb("ove", [P, NT])
        orstd = sb("orstd", [P, NT])
        fh = qf[:, 0:C * E].rearrange("p (t e) -> p t e", t=C)

        k_scr = nc.dram_tensor("k_scr", [2, 3, D0 * SLOTS, N], BF16, kind="Internal").ap()
        q_scr = nc.dram_tensor("q_scr", [2, 3, D0 * SLOTS, N], BF16, kind="Internal").ap()

        LOADS = dict(x=1, ctx=1, wk=1, w1k=1, w1v=1, wv=1, wq=2, small=5, adj=2, mask=1, moe=10, l1=7, ffn=4, id=2,
                     ones=1)
        ld = {n: sem(f"ld_{n}") for n in LOADS}
        ld_maskq = [sem(f"ld_maskq{i}") for i in range(2)]

        def load(eng, group, dst, src):
            eng.dma_start(dst, src).then_inc(ld[group], 16)

        def loaded(eng, *groups):
            for group in groups:
                eng.wait_ge(ld[group], 16 * LOADS[group])

        own_dve, own_act, own_pool = sem("own_dve"), sem("own_act"), sem("own_pool")
        gates_ok, nullk_ld, consts_ok = sem("gates_ok"), sem("nullk_ld"), sem("consts_ok")
        kproj, vproj, qproj = sem("kproj"), sem("vproj"), sem("qproj")
        k1_ok, kparts_ok, qf_ok, qparts_ok = (sem(n) for n in ("k1_ok", "kparts_ok", "qf_ok", "qparts_ok"))
        kspill, qspill, kst_ld = sem("kspill"), sem("qspill"), sem("kst_ld")
        qst_ld = [sem(f"qst_ld{i}") for i in range(2)]
        vaug_ok, adjm_ok, adjmT_ok, xbias_ok = sem("vaug_ok"), sem("adjm_ok"), sem("adjmT_ok"), sem("xbias_ok")
        tp0, xT0 = sem("tp0"), sem("xT0")
        ln_var = [sem(f"ln_var{i}") for i in range(4)]
        ln_rstd = [sem(f"ln_rstd{i}") for i in range(4)]
        ln_xn = [sem(f"ln_xn{i}") for i in range(4)]
        fa12_mm, fa12_ok, w3_mm, w3_ok = sem("fa12_mm"), sem("fa12_ok"), sem("w3_mm"), sem("w3_ok")
        wqm_ok, wqc_ok, wqg_ok, wqT_mm, wqT_ok = (sem(n) for n in ("wqm_ok", "wqc_ok", "wqg_ok", "wqT_mm", "wqT_ok"))
        gram_mm, gram_ok, wog_ok, lnb_ok, wmean_mm, bw_ok = (
            sem(n) for n in ("gram_mm", "gram_ok", "wog_ok", "lnb_ok", "wmean_mm", "bw_ok"))
        k1mm, k1max, k1exp, k1tp, k1n, v1mm, v1_ok = (sem(n) for n in ("k1mm", "k1max", "k1exp", "k1tp", "k1n", "v1mm", "v1_ok"))
        c1mm, c1read, ctx_ok = sem("c1mm"), sem("c1read"), sem("ctx_ok")
        s_mm, s_max, t_mm, t_add, t_exp = (sem(n) for n in ("s_mm", "s_max", "t_mm", "t_add", "t_exp"))
        m_ld = [sem(f"m_ld{i}") for i in range(2)]
        o_norm = sem("o_norm")
        filled = {k: sem(f"filled_{k}") for k in "OMXY"}
        read = {k: sem(f"read_{k}") for k in "OMXY"}
        r_exp, th_ok, hid_ok, comb_ok, w_ok = (sem(n) for n in ("r_exp", "th_ok", "hid_ok", "comb_ok", "w_ok"))
        qr_ok, z_ok, zs_ok, qe_ok, on_ok, ov_ok, or_ok, xb3_ok = (
            sem(n) for n in ("qr_ok", "z_ok", "zs_ok", "qe_ok", "on_ok", "ov_ok", "or_ok", "xb3_ok"))
        ft_ok, x4_ok, stored = sem("ft_ok"), sem("x4_ok"), sem("stored")

        turns = bank_turns()

        def bank_of(stage, key):
            return shared[turns[stage, key][0]]

        def take_bank(pe, stage, key):
            name, turn = turns[stage, key]
            if turn:
                pe.wait_ge(read[name], turn)
            return shared[name]

        def fill(ins, stage, key):
            ins.then_inc(filled[turns[stage, key][0]], 1)

        def wait_filled(eng, stage, key):
            name, turn = turns[stage, key]
            eng.wait_ge(filled[name], turn + 1)

        def done_reading(ins, stage, key):
            ins.then_inc(read[turns[stage, key][0]], 1)

        def wait_read(eng, stage, key):
            name, turn = turns[stage, key]
            eng.wait_ge(read[name], turn + 1)

        def head(i):
            b, h = divmod(i, H0)
            return b, h, h // 2, 64 * (h % 2)

        def tiles_of(b):
            return slice(b * C, (b + 1) * C)

        def toks(b):
            return slice(b * S, (b + 1) * S)

        def v_set(i):
            j = i - LAG - SH - 1
            return j // SH if j >= 0 and j % SH == 0 and j // SH < B * H0 // SH else None

        def gu_at(o):
            for stage, _ in STAGES.get(o, []):
                if stage[:2] == "gu":
                    return int(stage[2])
            return None

        ALL_STEPS = range(H0 * (B + 1) + SIDE)
        block = ctx.enter_context(nc.Block())

        @block.sync
        def _(sp):
            load(sp, "ctx", ctxT[:, :], A["ctxT"])
            load(sp, "wk", w_kT[:, :], A["wkT"])
            load(sp, "w1k", w1kv[:, 0:I1], A["w1kv"][:, 0:I1])
            load(sp, "wv", w_vT[:, :], A["wvT"])
            load(sp, "w1v", w1kv[:, I1:2 * I1], A["w1kv"][:, I1:2 * I1])
            load(sp, "wq", w_qT[:, :], A["wqT"])
            load(sp, "wq", w_oT[:, :], A["woT"])
            load(sp, "ones", kst[KROWS:KROWS + 65:64, :, :], A["ones"])
            load(sp, "l1", w1q[:, :], A["w1q"])
            load(sp, "l1", w1out[:, :, :], A["w1out"])
            load(sp, "l1", nullv[:, :], A["nullv"])
            load(sp, "l1", lnq_g[:, :], A["lnq_g"])
            load(sp, "l1", lnq_b[:, :], A["lnq_b"])
            load(sp, "l1", lno_g[:, :], A["lno_g"])
            load(sp, "l1", lno_b[:, :], A["lno_b"])
            load(sp, "ffn", fw_T[:, :], A["fwT"])
            load(sp, "ffn", fa1_T[:, :], A["fa1T"])
            load(sp, "ffn", fa2[:, :], A["fa2"])
            load(sp, "ffn", fb_row[:, :], A["fb"])
            load(sp, "adj", adj[:, :, :], A["adj"])
            for b in range(2):
                sp.dma_start(mask[:, b, :, :], A["mask"][:, b]).then_inc(ld_maskq[b % 2], 16)
            load(sp, "adj", adjT[:, :, :], A["adjT"])
            load(sp, "mask", maskT[:, :, :, :], A["maskT"])

            def spill(parts, scr, half, ready, spilled):
                cols = slice(half * HALF, (half + 1) * HALF)
                sp.wait_ge(ready, half + 1)
                for c in range(3):
                    sp.dma_start(scr[:, c, :, cols], parts[:, c, cols]).then_inc(spilled, 16)

            def restack(scr, stack, cols, landed, runs):
                for par in range(2):
                    term = 0
                    for part, count, repeats in runs:
                        r0 = 64 * par + term * D0
                        rows = count * repeats * D0
                        src = scr[par, part:part + count, :, cols].rearrange("c (d s) n -> (c d) s n", d=D0)
                        if repeats > 1:
                            src = src.unsqueeze(0).to_broadcast([repeats, D0, SLOTS, cols.stop - cols.start])
                        sp.dma_start(stack[r0:r0 + rows, :, cols], src).then_inc(landed, 16)
                        term += count * repeats

            spill(kparts, k_scr, 0, kparts_ok, kspill)
            spill(kparts, k_scr, 1, kparts_ok, kspill)
            sp.wait_ge(kspill, 16 * 6)
            restack(k_scr, kst, slice(0, N), kst_ld, K_RUNS)
            for half in range(2):
                spill(qparts, q_scr, half, qparts_ok, qspill)
                sp.wait_ge(qspill, 16 * 3 * (half + 1))
                restack(q_scr, qst, slice(half * HALF, (half + 1) * HALF), qst_ld[half], Q_RUNS)
            load(sp, "moe", w_router[:, :], A["router_w"])
            load(sp, "moe", cb_row[:, :], A["cb"])
            load(sp, "moe", expand[:, :, :], A["expand"])
            load(sp, "moe", tri[:, :, :], A["tri"])
            load(sp, "moe", w_gate[:, 0:RC, :], A["gate_w"])
            load(sp, "moe", w_gate[:, RC:HC, :], A["sgate_w"])
            load(sp, "moe", w_up[:, 0:RC, :], A["up_w"])
            load(sp, "moe", w_up[:, RC:HC, :], A["sup_w"])
            load(sp, "moe", w_down[:, 0:RC, :], A["down_w"])
            load(sp, "moe", w_down[:, RC:HC, :], A["sdown_w"])
            for g in range(2 * B):
                b, s0 = g // 2, (g % 2) * GH // 2
                wait_read(sp, "max_tp", g)
                for par in range(2):
                    for qc in range(C):
                        r0 = (par * C + qc) * GH // 2
                        t0 = b * S + qc * P
                        sp.dma_start(qst[64 * par + KROWS:64 * par + KROWS + 1, s0:s0 + GH // 2, t0:t0 + P],
                                     mrow[r0:r0 + GH // 2, g % 2, :]).then_inc(m_ld[g % 2], 16)
                if g in (1, 3):
                    nb = 2 + g // 2
                    sp.wait_ge(adjm_ok, nb - 1)
                    sp.dma_start(mask[:, nb % 2, :, :], A["mask"][:, nb]).then_inc(ld_maskq[nb % 2], 16)
            for b in range(B):
                sp.wait_ge(x4_ok, b + 1)
                sp.dma_start(out[:, tiles_of(b)], x[:, tiles_of(b), :]).then_inc(stored, 16)
            sp.wait_ge(stored, 16 * B)

        @block.gpsimd
        def _(pool):
            steps = [0]

            def link(ins):
                steps[0] += 1
                ins.then_inc(own_pool, 1)
                pool.wait_ge(own_pool, steps[0])

            def power(dst, src, n, ready):
                nc.gpsimd.tensor_tensor(dst, src, half_neg[:, 0:n], ALU.pow).then_inc(ready, 1)

            link(nc.gpsimd.memset(half_neg[:, :], -0.5))
            for half in range(2):
                pool.wait_ge(ln_var[0], half + 1)
                power(rstd[:, half * HT:(half + 1) * HT], vare[:, half * HT:(half + 1) * HT], HT, ln_rstd[0])
            link(nc.gpsimd.memset(ones_mean[:, :], 1.0 / I1))
            nc.gpsimd.memset(vaug[:, :, :], 1.0).then_inc(consts_ok, 1)
            loaded(pool, "adj", "mask")
            pool.wait_ge(ld_maskq[0], 16)
            link(nc.gpsimd.tensor_scalar(mask[:, 0].bitcast(F32), mask[:, 0], 0.0, NEG, ALU.is_equal, ALU.mult))
            nc.gpsimd.tensor_tensor(adjm[:, 0], mask[:, 0].bitcast(F32), adj[:, :, :], ALU.add).then_inc(adjm_ok, 1)
            pool.wait_ge(wqm_ok, 1)
            nc.gpsimd.tensor_scalar(wq_c[:, :], w1q[:, :], wq_mean[:, :], None, ALU.subtract).then_inc(wqc_ok, 1)
            pool.wait_ge(wqc_ok, 1)
            nc.gpsimd.tensor_tensor(wq_g[:, :], wq_c[:, :], lnq_g[:, :], ALU.mult).then_inc(wqg_ok, 1)
            link(nc.gpsimd.tensor_scalar(adjmT[:, 0], maskT[:, 0], 0.0, NEG, ALU.is_equal, ALU.mult))
            nc.gpsimd.tensor_tensor(adjmT[:, 0], adjmT[:, 0], adjT[:, :, :], ALU.add).then_inc(adjmT_ok, 1)
            nc.gpsimd.tensor_tensor(wo_g[:, :, :], w1out[:, :, :], lno_g[:, :].unsqueeze(2).to_broadcast([P, PR, E]),
                                    ALU.mult).then_inc(wog_ok, 1)
            nc.gpsimd.tensor_copy(lnb_bc[:, :, :], lno_b[:, :].unsqueeze(2).to_broadcast([P, PR, P])).then_inc(lnb_ok, 1)
            pool.wait_ge(gates_ok, 1)
            loaded(pool, "small")
            link(nc.gpsimd.tensor_scalar(tgbo[:, :], bo_row[:, :], tg[:, 0:1], None, ALU.mult))
            pool.wait_ge(ln_xn[0], 2)
            nc.gpsimd.tensor_tensor(x[:, :, :], x[:, :, :],
                                    tgbo[:, :].unsqueeze(1).to_broadcast([P, NT, E]), ALU.add).then_inc(xbias_ok, 1)
            link(nc.gpsimd.memset(ctx_bd[:, :, :], 0.0))
            link(nc.gpsimd.memset(ctx_bd[0:D1, :, D1:D1 + 1], 1.0))
            link(nc.gpsimd.memset(ctx_bd[D1:P, :, 2 * D1 + 1:2 * D1 + 2], 1.0))
            nc.gpsimd.memset(cand[:, :, EXP0:EXP0 + 4], SENT).then_inc(consts_ok, 1)

            for i in ALL_STEPS:
                nb, k = i // H0 + 1, i % H0
                if nb < B and k in (1, 3, 11, 13):
                    if k == 1:
                        pool.wait_ge(ld_maskq[nb % 2], 16 * (nb // 2 + 1))
                        link(nc.gpsimd.tensor_scalar(mask[:, nb % 2].bitcast(F32), mask[:, nb % 2], 0.0, NEG,
                                                     ALU.is_equal, ALU.mult))
                    if k == 3:
                        nc.gpsimd.tensor_tensor(adjm[:, nb], mask[:, nb % 2].bitcast(F32), adj[:, :, :],
                                                ALU.add).then_inc(adjm_ok, 1)
                    if k == 11:
                        link(nc.gpsimd.tensor_scalar(adjmT[:, nb], maskT[:, nb], 0.0, NEG, ALU.is_equal, ALU.mult))
                    if k == 13:
                        nc.gpsimd.tensor_tensor(adjmT[:, nb], adjmT[:, nb], adjT[:, :, :], ALU.add).then_inc(adjmT_ok, 1)
                for b, o in offsets(i):
                    ts = tiles_of(b)
                    for norm, at in ((1, 4), (2, 15), (3, 30)):
                        if o == at:
                            pool.wait_ge(ln_var[norm], b + 1)
                            power(rstd[:, ts], vare[:, ts], C, ln_rstd[norm])
                    n = gu_at(o)
                    if n is not None:
                        wait_read(pool, f"gu{n}", b)
                        nc.gpsimd.tensor_tensor(hid[:, GU[n], :], sil[:, n % 2, :], up[:, n % 2, :],
                                                ALU.mult).then_inc(hid_ok, 1)
                    if o == 17:
                        pool.wait_ge(ln_xn[2], b + 1)
                        pool.wait_ge(bw_ok, 1)
                        nc.gpsimd.tensor_tensor(x[:, ts, :], x[:, ts, :], tgbw[:, :].unsqueeze(1).to_broadcast([P, C, E]),
                                                ALU.add).then_inc(xb3_ok, 1)
                    if o == 18:
                        wait_read(pool, "gram", b)
                        power(qrstd[:, ts], qvar[:, ts], C, qr_ok)
                    if o in (19, 20):
                        r = o - 19
                        pool.wait_ge(z_ok, C * b + r + 1)
                        nc.gpsimd.tensor_tensor(zs[:, r, :, :], z[:, r, :, :],
                                                zmx[:, r, :].unsqueeze(2).to_broadcast([P, H1, D1]),
                                                ALU.subtract).then_inc(zs_ok, 1)
                    if o == 27:
                        pool.wait_ge(ov_ok, b + 1)
                        link(nc.gpsimd.tensor_tensor(orstd[:, ts], ove[:, ts], half_neg[:, 0:C], ALU.pow))
                        nc.gpsimd.tensor_scalar(orstd[:, ts], orstd[:, ts], tg[:, 1:2], None, ALU.mult).then_inc(or_ok, 1)

        def k1_evac(act, u):
            c, half = divmod(u, 2)
            act.wait_ge(k1tp, u + 1)
            nc.scalar.copy(kEn[:, half * HT:(half + 1) * HT, c * P:(c + 1) * P],
                           banks[4 + u % 2][:, :].rearrange("p (t c) -> p t c", t=HT)).then_inc(k1n, 1)

        @block.scalar
        def _(act):
            steps = [0]

            def link(ins):
                steps[0] += 1
                ins.then_inc(own_act, 1)
                act.wait_ge(own_act, steps[0])

            def evac(dst, src, stage, b):
                wait_filled(act, stage, b)
                done_reading(nc.scalar.copy(dst, src), stage, b)

            load(act, "x", x[:, :, :], A["x"])
            load(act, "small", bk_col[:, :], A["bk"])
            load(act, "small", gates[:, :], A["gates"])
            load(act, "small", bq_col[:, :], A["bq"])
            load(act, "small", bv_row[:, :], A["bv"])
            load(act, "small", bo_row[:, :], A["bo"])
            load(act, "id", ident[:, :], A["ident"])
            load(act, "id", identb[:, :], A["identb"])
            act.dma_start(nullk[:, :], A["nullk"]).then_inc(nullk_ld, 16)
            loaded(act, "small")
            nc.scalar.activation(tg[:, :], gates[:, :], ACT.Tanh).then_inc(gates_ok, 1)
            for half in range(2):
                cols = slice(half * HALF, (half + 1) * HALF)
                act.wait_ge(kproj, half + 1)
                link(nc.scalar.activation(kf[:, cols], banks[4 + half][:, :], ACT.Identity, bias=bk_col[:, :]))
                nc.scalar.copy(kparts[:, 0, cols], kf[:, cols]).then_inc(k1_ok, 1)
            for half in range(2):
                act.wait_ge(tp0, half + 1)
                nc.scalar.copy(xnT[:, half * HALF:(half + 1) * HALF], banks[6 + half][:, :]).then_inc(xT0, 1)
            act.wait_ge(nullk_ld, 16)
            for u in range(2 * PR):
                c, half = divmod(u, 2)
                act.wait_ge(v1mm, u + 1)
                nc.scalar.copy(v1[:, u, :], banks[2 + u % 2][:, :]).then_inc(v1_ok, 1)
                if u >= 2:
                    act.wait_ge(k1tp, u - 1)
                act.wait_ge(k1max, u + 1)
                for k in range(2):
                    b = 2 * half + k
                    nc.scalar.activation(kE[:, u % 2, k * S:(k + 1) * S], banks[u % 2][:, k * S:(k + 1) * S], ACT.Exp,
                                         bias=kmx[:, b, c:c + 1], accum_out=ksum[:, b, c:c + 1])
                    last = nc.scalar.activation(ek0[:, b, c:c + 1], nullk[:, :], ACT.Exp, bias=kmx[:, b, c:c + 1])
                last.then_inc(k1exp, 1)
                if u >= 1:
                    k1_evac(act, u - 1)
            k1_evac(act, 2 * PR - 1)

            for i in ALL_STEPS:
                j = i - LAG
                if 0 <= j < B * H0:
                    act.wait_ge(t_add, j + 1)
                    if j >= 2 * SH:
                        wait_filled(act, "values", j // SH - 2)
                    nc.scalar.activation(et[:, j % (2 * SH), :, :].rearrange("p c s -> p (c s)"), sc_t[:, j % 2, :],
                                         ACT.Exp).then_inc(t_exp, 1)
                if i % GH == 1 and 1 <= i // GH <= 2 * B:
                    g = i // GH - 1
                    wait_filled(act, "max_tp", g)
                    if g >= 2:
                        act.wait_ge(m_ld[g % 2], 64 * (g // 2))
                    done_reading(nc.scalar.mul(mrow[:, g % 2, :], bank_of("max_tp", g)[0:16, 0:P], -1.0), "max_tp", g)
                n = v_set(i)
                if n is not None:
                    evac(outT[:, n % SH, :], bank_of("values", n)[:, 0:S], "values", n)
                for b, o in offsets(i):
                    if o == 3:
                        evac(attnT[:, :], bank_of("attn_tp", b)[:, 0:C * P], "attn_tp", b)
                    for norm, at in ((1, 6), (2, 17), (3, 32)):
                        if o == at:
                            evac(xnT[:, toks(b)], bank_of(f"tp{norm}", b)[:, 0:S], f"tp{norm}", b)
                    if o == 7:
                        wait_filled(act, "logits", b)
                        done_reading(nc.scalar.activation(elog[:, :], bank_of("logits", b)[:, 0:C * EXP0], ACT.Exp,
                                                          scale=-1.0), "logits", b)
                    k = gu_at(o)
                    if k is not None:
                        wait_filled(act, f"gu{k}", b)
                        gu = bank_of(f"gu{k}", b)
                        if b * HC + k >= 2:
                            act.wait_ge(hid_ok, b * HC + k - 1)
                        nc.scalar.copy(up[:, k % 2, :], gu[:, S:2 * S])
                        nc.scalar.activation(th[:, k % 2, :], gu[:, 0:S], ACT.Tanh, scale=0.5).then_inc(th_ok, 1)
                    if o == 10:
                        evac(combT[:, :], bank_of("wts_tp", b)[0:EXP0, 0:S], "wts_tp", b)
                    if o in (21, 22):
                        r = o - 21
                        act.wait_ge(zs_ok, C * b + r + 1)
                        nc.scalar.activation(qE[:, r, :], zs[:, r, :, :].rearrange("p h d -> p (h d)"),
                                             ACT.Exp).then_inc(qe_ok, 1)
                    if o in (22, 26):
                        r = (o - 22) // 4
                        evac(qET[:, r, :, :].rearrange("p c s -> p (c s)"), bank_of(f"e_tp{r}", b)[:, :], f"e_tp{r}", b)
                    if o in (24, 28):
                        r = (o - 24) // 4
                        evac(onT[:, r, :, :].rearrange("p c s -> p (c s)"), bank_of(f"n_tp{r}", b)[:, :], f"n_tp{r}", b)
                    if o == 34:
                        wait_read(act, "ffn", b)
                        nc.scalar.activation(fh[:, :, :].rearrange("p t e -> p (t e)"),
                                             fh[:, :, :].rearrange("p t e -> p (t e)"), ACT.Tanh).then_inc(ft_ok, 1)

        @block.vector
        def _(dve):
            steps = [0]

            def link(ins):
                steps[0] += 1
                ins.then_inc(own_dve, 1)
                dve.wait_ge(own_dve, steps[0])

            def ln_stats(i, ts):
                for t in range(ts.start, ts.stop):
                    last = nc.vector.bn_stats(stats[:, t, :], x[:, t, :])
                link(last)
                for t in range(ts.start, ts.stop):
                    last = nc.vector.bn_aggr(mv[:, t, :], stats[:, t, :])
                link(last)
                nc.vector.tensor_scalar(vare[:, ts], mv[:, ts, 1], EPS, None, ALU.add).then_inc(ln_var[i], 1)

            def ln_apply(i, ts, turn):
                dve.wait_ge(ln_rstd[i], turn + 1)
                for t in range(ts.start, ts.stop):
                    last = nc.vector.tensor_scalar(xn[:, t, :], x[:, t, :], mv[:, t, 0:1], rstd[:, t:t + 1],
                                                   ALU.subtract, ALU.mult)
                last.then_inc(ln_xn[i], 1)

            def k1_max(u):
                c, half = divmod(u, 2)
                dve.wait_ge(k1mm, u + 1)
                m = kmx[:, 2 * half:2 * half + 2, c]
                link(nc.vector.tensor_reduce(m, banks[u % 2][:, :].rearrange("p (b s) -> p b s", b=2), AX.X, ALU.max))
                nc.vector.tensor_scalar(m, m, nullk[:, :], -1.0, ALU.max, ALU.mult).then_inc(k1max, 1)

            def split(dst, full, rest, half, ready):
                cols = slice(half * HALF, (half + 1) * HALF)
                link(nc.vector.tensor_tensor(rest[:, cols], full[:, cols], dst[:, 0, cols], ALU.subtract))
                link(nc.vector.tensor_copy(dst[:, 1, cols], rest[:, cols]))
                nc.vector.tensor_tensor(dst[:, 2, cols], rest[:, cols], dst[:, 1, cols], ALU.subtract).then_inc(ready, 1)

            def k_split(half):
                dve.wait_ge(k1_ok, half + 1)
                split(kparts, kf, kr, half, kparts_ok)

            def q_split(half):
                cols = slice(half * HALF, (half + 1) * HALF)
                dve.wait_ge(qproj, half + 1)
                nc.vector.tensor_scalar(qf[:, cols], banks[6 + half][:, :], bq_col[:, :], float(D0) ** -0.5,
                                        ALU.add, ALU.mult).then_inc(qf_ok, 1)
                dve.wait_ge(qf_ok, half + 1)
                link(nc.vector.tensor_copy(qparts[:, 0, cols], qf[:, cols]))
                split(qparts, qf, qr, half, qparts_ok)

            def v_bias(half):
                dve.wait_ge(vproj, half + 1)
                nc.vector.tensor_tensor(
                    vheads[:, half * HT:(half + 1) * HT, :, 0:D0],
                    banks[6 + half][:, :].rearrange("p (t h d) -> p t h d", t=HT, h=H0),
                    bv_row[:, :].rearrange("p (h d) -> p h d", h=H0).unsqueeze(1).to_broadcast([P, HT, H0, D0]),
                    ALU.add).then_inc(vaug_ok, 1)

            loaded(dve, "x")
            for half in range(2):
                ln_stats(0, slice(half * HT, (half + 1) * HT))
            for half in range(2):
                ln_apply(0, slice(half * HT, (half + 1) * HT), half)
            dve.wait_ge(nullk_ld, 16)
            loaded(dve, "small")
            k1_max(0)
            k_split(0)
            k1_max(1)
            k_split(1)
            q_split(0)
            k1_max(2)
            loaded(dve, "l1")
            link(nc.vector.reduce_sum(wq_mean[:, :], w1q[:, :], AX.X))
            nc.vector.tensor_scalar(wq_mean[:, :], wq_mean[:, :], 1.0 / I1, None, ALU.mult).then_inc(wqm_ok, 1)
            q_split(1)
            k1_max(3)
            dve.wait_ge(gates_ok, 1)
            nc.vector.tensor_scalar(tg_half[:, :], tg[:, 2:3], 0.5, None, ALU.mult)
            k1_max(4)
            dve.wait_ge(consts_ok, 1)
            v_bias(0)
            k1_max(5)
            v_bias(1)
            k1_max(6)
            k1_max(7)

            def prepare(i):
                if i == 1:
                    dve.wait_ge(fa12_mm, 1)
                    nc.vector.tensor_copy(fa12[:, :], banks[4][:, 0:E]).then_inc(fa12_ok, 1)
                    dve.wait_ge(wqT_mm, 1)
                    nc.vector.tensor_copy(wq_cT[:, :], banks[5][:, :]).then_inc(wqT_ok, 1)
                if i == 2:
                    dve.wait_ge(k1exp, 2 * PR)
                    link(nc.vector.tensor_tensor(kden[:, :, :], ksum[:, :, :], ek0[:, :, :], ALU.add))
                    link(nc.vector.reciprocal(krec[:, :, :], kden[:, :, :]))
                    link(nc.vector.tensor_tensor(nkv[:, :, :], nullv[:, :].unsqueeze(1).to_broadcast([P, B * PR, D1]),
                                                 ek0[:, :, :].rearrange("p b c -> p (b c)").unsqueeze(2).to_broadcast([P, B * PR, D1]),
                                                 ALU.mult))
                if i == 3:
                    dve.wait_ge(w3_mm, 1)
                    nc.vector.tensor_copy(w3[:, :], banks[4][:, 0:E]).then_inc(w3_ok, 1)
                    dve.wait_ge(gram_mm, 1)
                    nc.vector.tensor_scalar(gram[:, :], banks[5][:, 0:P], 1.0 / I1, None, ALU.mult).then_inc(gram_ok, 1)
                if 4 <= i < 4 + B:
                    b = i - 4
                    dve.wait_ge(c1mm, b + 1)
                    pr = slice(b * PR, (b + 1) * PR)
                    src = banks[b][:, :].rearrange("p (c e) -> p c e", c=PR)
                    nc.vector.tensor_tensor(ctx_t[0:D1, pr, :], src[0:D1, :, 0:D1], nkv[0:D1, pr, :], ALU.add)
                    nc.vector.tensor_tensor(ctx_t[D1:P, pr, :], src[D1:P, :, D1:P], nkv[D1:P, pr, :],
                                            ALU.add).then_inc(c1read, 1)
                if i == 8:
                    dve.wait_ge(wmean_mm, 1)
                    nc.vector.tensor_tensor(wo_c[:, :, :], wo_g[:, :, :],
                                            banks[4][:, 0:E].unsqueeze(1).to_broadcast([P, PR, E]), ALU.subtract)
                    nc.vector.tensor_scalar(tgbw[:, :], banks[4][:, E:2 * E], tg[:, 1:2], None, ALU.mult).then_inc(bw_ok, 1)
                if i == 9:
                    dve.wait_ge(c1read, B)
                    dve.wait_ge(consts_ok, 2)
                    kb = krec[:, :, :].rearrange("p b c -> p (b c)").unsqueeze(2).to_broadcast([P, B * PR, D1])
                    nc.vector.tensor_tensor(ctx_bd[0:D1, :, 0:D1], ctx_t[0:D1, :, :], kb[0:D1], ALU.mult)
                    nc.vector.tensor_tensor(ctx_bd[D1:P, :, D1 + 1:2 * D1 + 1], ctx_t[D1:P, :, :], kb[D1:P],
                                            ALU.mult).then_inc(ctx_ok, 1)

            def route_groups(b):
                wait_read(dve, "logits", b)
                link(nc.vector.tensor_scalar(elog[:, :], elog[:, :], 1.0, None, ALU.add))
                link(nc.vector.reciprocal(score[:, :, :].rearrange("p t e -> p (t e)"), elog[:, :]))
                link(nc.vector.tensor_tensor(biased[:, :, :].rearrange("p (t g) e -> p t (g e)", t=TB), score[:, :, :],
                                             cb_row[:, :].unsqueeze(1).to_broadcast([P, TB, EXP0]), ALU.add))
                nc.vector.tensor_tensor(pairs[:, :, 0:3], biased[:, :, 0:3], biased[:, :, 1:4], ALU.add)
                nc.vector.tensor_tensor(pairs[:, :, 3:5], biased[:, :, 0:2], biased[:, :, 2:4], ALU.add)
                link(nc.vector.tensor_tensor(pairs[:, :, 5:6], biased[:, :, 0:1], biased[:, :, 3:4], ALU.add))
                link(nc.vector.tensor_reduce(gscore[:, :, :].rearrange("p t g -> p (t g)"), pairs[:, :, :], AX.X, ALU.max))
                other = gscore[:, :, :].unsqueeze(2).to_broadcast([P, TB, 4, 4])
                mine = gscore[:, :, :].unsqueeze(3).to_broadcast([P, TB, 4, 4])
                nc.vector.tensor_tensor(gcmp[:, :, :, :], other, mine, ALU.is_gt)
                link(nc.vector.tensor_tensor(geq[:, :, :, :], other, mine, ALU.is_equal))
                link(nc.vector.tensor_tensor(geq[:, :, :, :], geq[:, :, :, :],
                                             tri[:, :, :].unsqueeze(1).to_broadcast([P, TB, 4, 4]), ALU.mult))
                link(nc.vector.tensor_tensor(gcmp[:, :, :, :], gcmp[:, :, :, :], geq[:, :, :, :], ALU.add))
                link(nc.vector.reduce_sum(grank[:, :], gcmp[:, :, :, :].rearrange("p t g h -> p (t g) h"), AX.X))
                link(nc.vector.tensor_scalar(gpen[:, :], grank[:, :], float(TOPG), NEG, ALU.is_ge, ALU.mult))
                link(nc.vector.tensor_tensor(cand[:, :, 0:EXP0].rearrange("p t (g e) -> p t g e", g=4),
                                             biased[:, :, :].rearrange("p (t g) e -> p t g e", t=TB),
                                             gpen[:, :].rearrange("p (t g) -> p t g", t=TB).unsqueeze(3).to_broadcast([P, TB, 4, 4]),
                                             ALU.add))

            def route_experts(b):
                for t in range(TB):
                    last = nc.vector.max(best8[:, t, :], cand[:, t, 0:EXP0])
                link(last)
                link(nc.vector.memset(best8[:, :, TOPK:8], SENT))
                for t in range(TB):
                    last = nc.vector.match_replace(struck[:, t, :], best8[:, t, :], cand[:, t, :], STRUCK)
                link(last)
                link(nc.vector.tensor_scalar(wts[:, :, :], struck[:, :, 0:EXP0], STRUCK, None, ALU.is_equal))
                link(nc.vector.tensor_tensor(wts[:, :, :], wts[:, :, :], score[:, :, :], ALU.mult))
                link(nc.vector.reduce_sum(wsum[:, :], wts[:, :, :], AX.X))
                link(nc.vector.tensor_scalar(wsum[:, :], wsum[:, :], 1e-20, None, ALU.add))
                link(nc.vector.reciprocal(wrec[:, :], wsum[:, :]))
                nc.vector.tensor_tensor(wts[:, :, :], wts[:, :, :], wrec[:, :].unsqueeze(2).to_broadcast([P, TB, EXP0]),
                                        ALU.mult).then_inc(w_ok, 1)

            def beside(b, o):
                ts = tiles_of(b)
                if o == 2:
                    for qc in range(C):
                        wait_filled(dve, f"out_tp{qc}", b)
                        o4 = bank_of(f"out_tp{qc}", b)[:, :].rearrange("p (h w) -> p h w", w=32)
                        link(nc.vector.reciprocal(orec[:, qc, :], o4[:, :, D0]))
                        done_reading(nc.vector.tensor_tensor(
                            attn[:, qc, :].rearrange("p (h d) -> p h d", h=H0), o4[:, :, 0:D0],
                            orec[:, qc, :].unsqueeze(2).to_broadcast([P, H0, D0]), ALU.mult), f"out_tp{qc}", b)
                if o == 4:
                    wait_filled(dve, "attn_proj", b)
                    dve.wait_ge(xbias_ok, 1)
                    done_reading(nc.vector.scalar_tensor_tensor(
                        x[:, ts, :], bank_of("attn_proj", b)[:, 0:C * E].rearrange("p (c e) -> p c e", c=C), tg[:, 0:1],
                        x[:, ts, :], ALU.mult, ALU.add), "attn_proj", b)
                    wait_read(dve, "attn_proj", b)
                    ln_stats(1, ts)
                for norm, at in ((1, 5), (2, 16), (3, 31)):
                    if o == at:
                        ln_apply(norm, ts, b)
                if o == 8:
                    route_groups(b)
                if o == 9:
                    route_experts(b)
                k = gu_at(o)
                if k is not None:
                    dve.wait_ge(th_ok, b * HC + k + 1)
                    done_reading(nc.vector.scalar_tensor_tensor(sil[:, k % 2, :], th[:, k % 2, :], 1.0,
                                                                bank_of(f"gu{k}", b)[:, 0:S], ALU.add, ALU.mult), f"gu{k}", b)
                if o in (11, 14):
                    r = (o - 11) // 3
                    wait_filled(dve, f"comb{r}", b)
                    dve.wait_ge(hid_ok, b * HC + SC + 2 * r + 2)
                    h2 = hid[:, 2 * r:2 * r + 2, :].rearrange("p c s -> p (c s)")
                    done_reading(nc.vector.tensor_tensor(h2, h2, bank_of(f"comb{r}", b)[:, :], ALU.mult), f"comb{r}", b)
                if o == 15:
                    wait_filled(dve, "down", b)
                    done_reading(nc.vector.scalar_tensor_tensor(
                        x[:, ts, :], bank_of("down", b)[:, 0:C * E].rearrange("p (c e) -> p c e", c=C), tg_half[:, :],
                        x[:, ts, :], ALU.mult, ALU.add), "down", b)
                    wait_read(dve, "down", b)
                    ln_stats(2, ts)
                if o == 18:
                    wait_filled(dve, "gram", b)
                    for r in range(C):
                        t = C * b + r
                        last = nc.vector.tensor_tensor_reduce(out=junk[:, :], in0=bank_of("gram", b)[:, r * P:(r + 1) * P],
                                                              in1=xn[:, t, :], scale=1.0, scalar=EPS, op0=ALU.mult,
                                                              op1=ALU.add, accum_out=qvar[:, t:t + 1])
                        if r < C - 1:
                            link(last)
                    done_reading(last, "gram", b)
                if o in (19, 20):
                    r = o - 19
                    t = C * b + r
                    dve.wait_ge(qr_ok, b + 1)
                    wait_filled(dve, f"q{r}", b)
                    done_reading(nc.vector.scalar_tensor_tensor(z[:, r, :, :].rearrange("p h d -> p (h d)"),
                                                                bank_of(f"q{r}", b)[:, :], qrstd[:, t:t + 1], lnq_b[:, :],
                                                                ALU.mult, ALU.add), f"q{r}", b)
                    wait_read(dve, f"q{r}", b)
                    nc.vector.tensor_reduce(zmx[:, r, :], z[:, r, :, :], AX.X, ALU.max).then_inc(z_ok, 1)
                if o in (23, 27):
                    r = (o - 23) // 4
                    t = C * b + r
                    halves = [(f"oa{r}", 0), (f"ob{r}", 1)]
                    for stage, q in halves:
                        wait_filled(dve, stage, b)
                        ob = bank_of(stage, b)[:, 0:4 * (D1 + 1)].rearrange("p (h e) -> p h e", h=4)
                        last = nc.vector.tensor_scalar(osum[:, r, 4 * q:4 * q + 4], ob[:, :, D1], 1.0 / SCALE1, None, ALU.mult)
                    link(last)
                    link(nc.vector.reciprocal(osum[:, r, :], osum[:, r, :]))
                    for stage, q in halves:
                        ob = bank_of(stage, b)[:, 0:4 * (D1 + 1)].rearrange("p (h e) -> p h e", h=4)
                        done_reading(nc.vector.tensor_tensor(
                            on[:, r, q * 256:(q + 1) * 256].rearrange("p (h e) -> p h e", h=4), ob[:, :, 0:D1],
                            osum[:, r, 4 * q:4 * q + 4].unsqueeze(2).to_broadcast([P, 4, D1]), ALU.mult), stage, b)
                    wait_read(dve, f"oa{r}", b)
                    wait_read(dve, f"ob{r}", b)
                    link(nc.vector.bn_stats(ostat[:, t, :], on[:, r, :]))
                    link(nc.vector.bn_aggr(omv[:, t, :], ostat[:, t, :]))
                    last = nc.vector.tensor_scalar(ove[:, t:t + 1], omv[:, t, 1:2], EPS, None, ALU.add)
                    if r == C - 1:
                        last.then_inc(ov_ok, 1)
                if o == 30:
                    wait_filled(dve, "proj1", b)
                    dve.wait_ge(or_ok, b + 1)
                    dve.wait_ge(xb3_ok, b + 1)
                    for r in range(C):
                        t = C * b + r
                        last = nc.vector.scalar_tensor_tensor(x[:, t, :], bank_of("proj1", b)[:, r * E:(r + 1) * E],
                                                              orstd[:, t:t + 1], x[:, t, :], ALU.mult, ALU.add)
                    done_reading(last, "proj1", b)
                    wait_read(dve, "proj1", b)
                    ln_stats(3, ts)
                if o == 33:
                    wait_filled(dve, "ffn", b)
                    done_reading(nc.vector.tensor_tensor(
                        fh[:, :, :], bank_of("ffn", b)[:, 0:C * E].rearrange("p (t e) -> p t e", t=C),
                        fb_row[:, :].unsqueeze(1).to_broadcast([P, C, E]), ALU.add), "ffn", b)
                if o == 34:
                    dve.wait_ge(ft_ok, b + 1)
                    nc.vector.scalar_tensor_tensor(x[:, ts, :], fh[:, :, :], tg[:, 3:4], x[:, ts, :], ALU.mult,
                                                   ALU.add).then_inc(x4_ok, 1)

            for i in ALL_STEPS:
                if i < B * H0:
                    b, h, s, p0 = head(i)
                    g = i // GH
                    dve.wait_ge(s_mm, i + 1)
                    if g >= 2 and i % GH == 0:
                        wait_filled(dve, "max_tp", g - 2)
                    nc.vector.tensor_reduce(mx[:, g % 2, h % 2, :, s % (GH // 2)],
                                            bankS[i % 2][:, :].rearrange("p (c s) -> p c s", c=C),
                                            AX.X, ALU.max).then_inc(s_max, 1)
                j = i - LAG
                if 0 <= j < B * H0:
                    dve.wait_ge(t_mm, j + 1)
                    if j >= 2:
                        dve.wait_ge(t_exp, j - 1)
                    if j % H0 == 0 and j:
                        dve.wait_ge(adjmT_ok, j // H0 + 1)
                    nc.vector.tensor_tensor(sc_t[:, j % 2, :], bankT[j % 2][:, :],
                                            adjmT[:, j // H0].rearrange("p c s -> p (c s)"),
                                            ALU.add).then_inc(t_add, 1)
                prepare(i)
                if i == H0 * 2:
                    loaded(dve, "moe", "ffn")
                for b, o in offsets(i):
                    beside(b, o)

        @block.tensor
        def _(pe):
            mm = nc.tensor.matmul

            def k1_transpose(u):
                pe.wait_ge(k1exp, u + 1)
                if u >= 2:
                    pe.wait_ge(k1n, u - 1)
                for k in range(4):
                    last = nc.tensor.transpose(banks[4 + u % 2][:, k * P:(k + 1) * P], kE[:, u % 2, k * P:(k + 1) * P],
                                               ident[:, :])
                last.then_inc(k1tp, 1)

            loaded(pe, "ctx", "wk")
            for half in range(2):
                mm(banks[4 + half][:, :], w_kT[:, :], ctxT[:, half * HALF:(half + 1) * HALF],
                   start=True, stop=True).then_inc(kproj, 1)
            for u in range(2 * PR):
                c, half = divmod(u, 2)
                if u == 0:
                    loaded(pe, "w1k")
                if u >= 2:
                    pe.wait_ge(k1exp, u - 1)
                mm(banks[u % 2][:, :], w1kv[:, c * P:(c + 1) * P], ctxT[:, half * HALF:(half + 1) * HALF],
                   start=True, stop=True).then_inc(k1mm, 1)
                if u == 0:
                    loaded(pe, "w1v")
                if u >= 2:
                    pe.wait_ge(v1_ok, u - 1)
                mm(banks[2 + u % 2][:, :], ctxT[:, u * P:(u + 1) * P], w1kv[:, I1:2 * I1],
                   start=True, stop=True).then_inc(v1mm, 1)
                if u == 0:
                    loaded(pe, "id")
                    for half in range(2):
                        pe.wait_ge(ln_xn[0], half + 1)
                        for k in range(HT):
                            last = nc.tensor.transpose(banks[6 + half][:, k * P:(k + 1) * P], xn[:, half * HT + k, :], ident[:, :])
                        last.then_inc(tp0, 1)
                if u == 1:
                    loaded(pe, "wq")
                    for half in range(2):
                        pe.wait_ge(xT0, half + 1)
                        mm(banks[6 + half][:, :], w_qT[:, :], xnT[:, half * HALF:(half + 1) * HALF],
                           start=True, stop=True).then_inc(qproj, 1)
                if u == 4:
                    loaded(pe, "wv")
                    pe.wait_ge(qf_ok, 2)
                    for t in range(NT):
                        last = mm(banks[6 + t // HT][:, (t % HT) * E:(t % HT + 1) * E], ctxT[:, t * P:(t + 1) * P],
                                  w_vT[:, :], start=True, stop=True)
                        if t % HT == HT - 1:
                            last.then_inc(vproj, 1)
                if u >= 1:
                    if u == 1:
                        pe.wait_ge(k1_ok, 2)
                    k1_transpose(u - 1)
            k1_transpose(2 * PR - 1)

            def prepare(i):
                if i == 0:
                    loaded(pe, "ffn", "l1")
                    pe.wait_ge(k1n, 2 * PR)
                    mm(banks[4][:, 0:E], fa1_T[:, :], fa2[:, :], start=True, stop=True).then_inc(fa12_mm, 1)
                    pe.wait_ge(wqc_ok, 1)
                    for k in range(PR):
                        last = nc.tensor.transpose(banks[5][:, k * P:(k + 1) * P], wq_c[:, k * P:(k + 1) * P], ident[:, :])
                    last.then_inc(wqT_mm, 1)
                if i == 2:
                    pe.wait_ge(fa12_ok, 1)
                    mm(banks[4][:, 0:E], fw_T[:, :], fa12[:, :], start=True, stop=True).then_inc(w3_mm, 1)
                    pe.wait_ge(wqT_ok, 1)
                    for c in range(PR):
                        ws = wq_cT[:, c * P:(c + 1) * P]
                        last = mm(banks[5][:, 0:P], ws, ws, start=(c == 0), stop=(c == PR - 1))
                    last.then_inc(gram_mm, 1)
                if 3 <= i < 3 + B:
                    b = i - 3
                    if b == 0:
                        pe.wait_ge(v1_ok, 2 * PR)
                    for c in range(PR):
                        for k in range(C):
                            t = b * C + k
                            last = mm(banks[b][:, c * P:(c + 1) * P], kEn[:, t, c * P:(c + 1) * P],
                                      v1[:, t, c * P:(c + 1) * P], start=(k == 0), stop=(k == C - 1))
                    last.then_inc(c1mm, 1)
                if i == 7:
                    pe.wait_ge(wog_ok, 1)
                    pe.wait_ge(lnb_ok, 1)
                    pe.wait_ge(w3_ok, 1)
                    pe.wait_ge(consts_ok, 1)
                    for c in range(PR):
                        mm(banks[4][:, 0:E], ones_mean[:, :], wo_g[:, c, :], start=(c == 0), stop=(c == PR - 1))
                    for c in range(PR):
                        last = mm(banks[4][:, E:2 * E], lnb_bc[:, c, :], w1out[:, c, :], start=(c == 0), stop=(c == PR - 1))
                    last.then_inc(wmean_mm, 1)

            pe.wait_ge(kst_ld, 16 * 2 * len(K_RUNS))
            loaded(pe, "ones")

            def transposes(stage, b, srcs):
                bank = take_bank(pe, stage, b)
                for k, src in enumerate(srcs):
                    last = nc.tensor.transpose(bank[0:src.shape[1], k * P:(k + 1) * P], src, ident[:, :])
                fill(last, stage, b)

            def beside(b, stage):
                tt = [C * b + r for r in range(C)]
                bank = None
                if stage[:6] == "out_tp":
                    qc = int(stage[6])
                    wait_read(pe, "values", SH * b + SH - 1)
                    transposes(stage, b, [outT[:, n, qc * P:(qc + 1) * P] for n in range(SH)])
                elif stage == "attn_tp":
                    wait_read(pe, "out_tp0", b)
                    wait_read(pe, "out_tp1", b)
                    transposes(stage, b, [attn[:, qc, :] for qc in range(C)])
                elif stage == "attn_proj":
                    bank = take_bank(pe, stage, b)
                    wait_read(pe, "attn_tp", b)
                    for qc in range(C):
                        last = mm(bank[:, qc * E:(qc + 1) * E], attnT[:, qc * P:(qc + 1) * P], w_oT[:, :], start=True, stop=True)
                elif stage[:2] == "tp":
                    pe.wait_ge(ln_xn[int(stage[2])], b + 1)
                    transposes(stage, b, [xn[:, t, :] for t in tt])
                elif stage == "logits":
                    bank = take_bank(pe, stage, b)
                    wait_read(pe, "tp1", b)
                    for r, t in enumerate(tt):
                        last = mm(bank[:, r * EXP0:(r + 1) * EXP0], xnT[:, t * P:(t + 1) * P], w_router[:, :], start=True, stop=True)
                elif stage[:2] == "gu":
                    bank = take_bank(pe, stage, b)
                    c = GU[int(stage[2])]
                    mm(bank[:, 0:S], w_gate[:, c, :], xnT[:, toks(b)], start=True, stop=True)
                    last = mm(bank[:, S:2 * S], w_up[:, c, :], xnT[:, toks(b)], start=True, stop=True)
                elif stage == "wts_tp":
                    pe.wait_ge(w_ok, b + 1)
                    transposes(stage, b, [wts[:, r, :] for r in range(C)])
                elif stage[:4] == "comb":
                    bank = take_bank(pe, stage, b)
                    wait_read(pe, "wts_tp", b)
                    for k in range(2):
                        last = mm(bank[:, k * S:(k + 1) * S], expand[:, 2 * int(stage[4]) + k, :], combT[:, :], start=True, stop=True)
                elif stage == "down":
                    bank = take_bank(pe, stage, b)
                    pe.wait_ge(hid_ok, (b + 1) * HC)
                    wait_read(pe, "comb1", b)
                    for r in range(C):
                        for n, c in enumerate(GU):
                            last = mm(bank[:, r * E:(r + 1) * E], hid[:, c, r * P:(r + 1) * P], w_down[:, c, :],
                                      start=(n == 0), stop=(n == HC - 1))
                elif stage == "gram":
                    bank = take_bank(pe, stage, b)
                    wait_read(pe, "tp2", b)
                    for r, t in enumerate(tt):
                        last = mm(bank[:, r * P:(r + 1) * P], xnT[:, t * P:(t + 1) * P], gram[:, :], start=True, stop=True)
                elif stage in ("q0", "q1"):
                    bank = take_bank(pe, stage, b)
                    t = tt[int(stage[1])]
                    last = mm(bank[:, :], xnT[:, t * P:(t + 1) * P], wq_g[:, :], start=True, stop=True)
                elif stage[:4] == "e_tp":
                    r = int(stage[4])
                    pe.wait_ge(qe_ok, C * b + r + 1)
                    transposes(stage, b, [qE[:, r, c * P:(c + 1) * P] for c in range(PR)])
                elif stage[:2] in ("oa", "ob"):
                    r = int(stage[2])
                    bank = take_bank(pe, stage, b)
                    wait_read(pe, f"e_tp{r}", b)
                    for k in range(2):
                        c = 2 * "ab".index(stage[1]) + k
                        last = mm(bank[:, k * 2 * (D1 + 1):(k + 1) * 2 * (D1 + 1)], qET[:, r, c, :], ctx_bd[:, b * PR + c, :],
                                  start=True, stop=True)
                elif stage[:4] == "n_tp":
                    r = int(stage[4])
                    wait_read(pe, f"oa{r}", b)
                    wait_read(pe, f"ob{r}", b)
                    transposes(stage, b, [on[:, r, c * P:(c + 1) * P] for c in range(PR)])
                elif stage == "proj1":
                    bank = take_bank(pe, stage, b)
                    wait_read(pe, "n_tp1", b)
                    for r in range(C):
                        for c in range(PR):
                            last = mm(bank[:, r * E:(r + 1) * E], onT[:, r, c, :], wo_c[:, c, :], start=(c == 0), stop=(c == PR - 1))
                elif stage == "ffn":
                    bank = take_bank(pe, stage, b)
                    wait_read(pe, "tp3", b)
                    for r, t in enumerate(tt):
                        last = mm(bank[:, r * E:(r + 1) * E], xnT[:, t * P:(t + 1) * P], w3[:, :], start=True, stop=True)
                if bank is not None:
                    fill(last, stage, b)

            for i in ALL_STEPS:
                if i == 0:
                    pe.wait_ge(vaug_ok, 2)
                if i % (2 * H0) == 0 and i < B * H0:
                    pe.wait_ge(qst_ld[i // (2 * H0)], 16 * 2 * len(Q_RUNS))
                if i == GH + 1:
                    pe.wait_ge(c1read, B)
                    pe.wait_ge(bw_ok, 1)
                    pe.wait_ge(gram_ok, 1)
                if i == H0 * 2 + 2:
                    loaded(pe, "moe")
                    pe.wait_ge(ctx_ok, 1)
                if i < B * H0:
                    b, h, s, p0 = head(i)
                    if i >= 2:
                        pe.wait_ge(s_max, i - 1)
                    if h == 0:
                        pe.wait_ge(adjm_ok, b + 1)
                    mm(bankS[i % 2][:, :], identb[:, :], adjm[:, b, :, :].rearrange("p c s -> p (c s)"),
                       start=True, stop=False)
                    for qc in range(C):
                        last = mm(bankS[i % 2][:, qc * S:(qc + 1) * S],
                                  qst[p0:p0 + KROWS, s, b * S + qc * P:b * S + (qc + 1) * P],
                                  kst[p0:p0 + KROWS, s, toks(b)], start=False, stop=(qc == C - 1))
                    last.then_inc(s_mm, 1)
                prepare(i)
                j = i - LAG
                if 0 <= j < B * H0:
                    b, h, s, p0 = head(j)
                    if j >= 2:
                        pe.wait_ge(t_add, j - 1)
                    if j % GH == 0:
                        g = j // GH
                        pe.wait_ge(m_ld[g % 2], 64 * (g // 2 + 1))
                    for kc in range(C):
                        last = mm(bankT[j % 2][:, kc * S:(kc + 1) * S],
                                  kst[p0:p0 + KROWS + 1, s, b * S + kc * P:b * S + (kc + 1) * P],
                                  qst[p0:p0 + KROWS + 1, s, toks(b)], start=True, stop=True)
                    last.then_inc(t_mm, 1)
                if i % GH == 1 and 1 <= i // GH <= 2 * B:
                    g = i // GH - 1
                    pe.wait_ge(s_max, (g + 1) * GH)
                    transposes("max_tp", g, [mx[:, g % 2, :, :, :].rearrange("p a c s -> p (a c s)")])
                n = v_set(i)
                if n is not None:
                    bank = take_bank(pe, "values", n)
                    pe.wait_ge(t_exp, (n + 1) * SH)
                    b = n // (H0 // SH)
                    for kc in range(C):
                        for k in range(SH):
                            h = (n * SH + k) % H0
                            last = mm(bank[32 * k:32 * k + 32, 0:S], vaug[:, b * C + kc, h * AW:h * AW + 32],
                                      et[:, (n * SH + k) % (2 * SH), kc, :], start=(kc == 0), stop=(kc == C - 1))
                    fill(last, "values", n)
                for b, o in offsets(i):
                    for stage, _ in STAGES.get(o, []):
                        beside(b, stage)


def kernel(**inputs):
    import numpy as np
    import concourse.bacc as bacc
    from ml_dtypes import bfloat16 as bf16
    from concourse.bass_utils import run_bass_kernel_spmd as run

    I = {k: np.asarray(v) for k, v in inputs.items()}

    def rows(v):
        return np.broadcast_to(v.reshape(1, -1), (P, v.size))

    def tiles(v):
        return v.reshape(-1, P, v.shape[-1]).transpose(1, 0, 2)

    order = np.arange(E).reshape(SLOTS, 2, D0).transpose(1, 2, 0).reshape(-1)
    mask = I["mask_Bx1xSxS2_ik1"][:, 0]
    lay = {
        "x": tiles(I["x"].reshape(N, E)),
        "ctxT": I["ctx_1024"].reshape(N, E).T,
        "wkT": I["L0_xattn_Wk"].T[:, order], "wqT": I["L0_xattn_Wq"].T[:, order],
        "wvT": I["L0_xattn_Wv"].T, "woT": I["L0_xattn_Wo"].T,
        "bq": I["L0_xattn_bq"][order].reshape(P, 1), "bk": I["L0_xattn_bk"][order].reshape(P, 1),
        "bv": rows(I["L0_xattn_bv"]), "bo": rows(I["L0_xattn_bo"]),
        "gates": rows(np.concatenate([I["g_xattn"], I["g_ffn"]])),
        "ident": np.eye(P, dtype=np.float32), "identb": np.eye(P).astype(bf16),
        "ones": np.ones((2, SLOTS, N), bf16),
        "tri": np.broadcast_to(np.tril(np.ones((4, 4), np.float32), -1), (P, 4, 4)),
        "expand": np.repeat(np.eye(EXP0, dtype=np.float32), HID, 1).reshape(EXP0, RC, P),
        "adj": tiles(I["L0_xattn_adj"]), "adjT": tiles(I["L0_xattn_adj"].T),
        "mask": mask.reshape(B, C, P, S).transpose(2, 0, 1, 3),
        "maskT": mask.transpose(0, 2, 1).reshape(B, C, P, S).transpose(2, 0, 1, 3),
        "router_w": I["L0_ffn_router_w"].T, "cb": rows(I["L0_ffn_correction_bias"]),
        "gate_w": I["L0_ffn_gate_w"].transpose(1, 0, 2).reshape(P, RC, P),
        "up_w": I["L0_ffn_up_w"].transpose(1, 0, 2).reshape(P, RC, P),
        "down_w": tiles(I["L0_ffn_down_w"].reshape(EXP0 * HID, E)),
        "sgate_w": I["L0_ffn_shared_gate_w"].T.reshape(P, SC, P), "sup_w": I["L0_ffn_shared_up_w"].T.reshape(P, SC, P),
        "sdown_w": tiles(I["L0_ffn_shared_down_w"].T),
        "w1q": I["L1_xattn_Wq"], "w1kv": I["L1_xattn_Wkv"], "w1out": tiles(I["L1_xattn_Wout"]),
        "nullk": np.concatenate([I["L1_xattn_null_kv"][0]] * 2).reshape(P, 1), "nullv": rows(I["L1_xattn_null_kv"][1]),
        "lnq_g": rows(I["L1_xattn_ln_q_g"]), "lnq_b": rows(I["L1_xattn_ln_q_b"]),
        "lno_g": I["L1_xattn_ln_out_g"].reshape(PR, P).T, "lno_b": I["L1_xattn_ln_out_b"].reshape(PR, P).T,
        "fwT": I["L1_ffn_weight"].T, "fa1T": I["L1_ffn_aux_weight1"].T, "fa2": I["L1_ffn_aux_weight2"],
        "fb": rows(I["L1_ffn_bias"]),
    }
    nc = bacc.Bacc("TRN2", target_bir_lowering=False, num_devices=1)
    arrays, A = {}, {}
    for name, a in lay.items():
        a = np.ascontiguousarray(a)
        arrays[f"in_{name}"] = a
        A[name] = nc.dram_tensor(f"in_{name}", a.shape, mybir.dt.from_np(a.dtype), kind="ExternalInput").ap()
    out = nc.dram_tensor("out", (P, NT, E), F32, kind="ExternalOutput").ap()
    build(nc, A, out)
    r = run(nc, [arrays], core_ids=[0])
    return r.results[0]["out"].transpose(1, 0, 2).reshape(B, S, E)
```

```python
from contextlib import ExitStack

import concourse.bass as bass
from concourse import mybir

F32 = mybir.dt.float32
BF16 = mybir.dt.bfloat16
I32 = mybir.dt.int32
ALU = mybir.AluOpType
ACT = mybir.ActivationFunctionType
AX = mybir.AxisListType

P = 128
B, S, E = 4, 256, 128
N = B * S
NT = N // P
HALF = N // 2
HT = NT // 2
H0, D0 = 16, 8
C = S // P
TERMS = [(0, 0), (0, 1), (0, 2), (1, 0), (1, 1), (2, 0)]
Q_RUNS = [(0, 1, 3), (1, 1, 2), (2, 1, 1)]
K_RUNS = [(0, 3, 1), (0, 2, 1), (0, 1, 1)]
KROWS = len(TERMS) * D0
SLOTS = H0 // 2
SH = 4
GH = 8
SC_RING = 3
LAG = 2 * GH
NEG = -1.0e30
LOWEST = -3.0e38
EXP0, HID = 16, 32
RC = EXP0 * HID // P
SC = 256 // P
HC = RC + SC
TOPG, TOPK = 2, 4
H1, D1 = 8, 64
I1 = H1 * D1
PR = I1 // P
SCALE1 = 8.0
EPS = 1e-5
AW = D0 + 1
GU = [RC, RC + 1, 0, 1, 2, 3]
MAIN = H0 * (B + 1) + 2

CONTEXTS = {2: [0], 3: [1], 4: [2, 3]}

STAGES = {
    3: [("out_tp0", "X"), ("out_tp1", "M")], 5: [("attn_tp", "X")], 7: [("attn_proj", "M")], 10: [("tp1", "X")],
    12: [("logits", "Y")], 14: [("gu0", "M"), ("gu1", "O")], 15: [("gu2", "Y")], 16: [("gu3", "X")],
    20: [("gu4", "Y"), ("gu5", "M")], 21: [("wts_tp", "Y")], 22: [("comb0", "O"), ("comb1", "Y")],
    24: [("down", "X")], 28: [("tp2", "M")], 31: [("gram", "O")], 36: [("q0", "O")],
    40: [("e_tp0", "O"), ("q1", "Y")], 41: [("oa0", "Y")], 42: [("ob0", "M")], 43: [("e_tp1", "X")],
    49: [("oa1", "Y"), ("ob1", "X")], 51: [("n_tp1", "Y")], 54: [("n_tp0", "X")], 60: [("proj1", "X"), ("tp3", "O")],
    63: [("ffn", "M")],
}
DVE_AT = {
    3: ["norm0"], 7: ["x1"], 14: ["rg0"], 15: ["re0"], 22: ["cm0", "cm1"], 24: ["x2"], 32: ["qvar0"], 36: ["z0"],
    40: ["z1"], 43: ["on0"], 49: ["on1"], 60: ["x3"], 66: ["x4"],
}
ACT_AT = {
    5: ["attnT0"], 10: ["xT1"], 12: ["elog0"], 14: ["th0", "th1"], 15: ["th2"], 16: ["th3"], 20: ["th4", "th5"],
    21: ["combT0"], 28: ["xT2"], 38: ["qe0"], 40: ["qET0"], 41: ["qe1"], 43: ["qET1"], 51: ["onT1"], 55: ["onT0"],
    60: ["xT3"], 64: ["fh0"],
}
POOL_AT = {
    7: ["ap1"], 14: ["hid0"], 16: ["hid1"], 17: ["wsplit0"], 18: ["hid2"], 19: ["hid3"], 20: ["hid4", "hid5"],
    26: ["ap2"], 36: ["qr0"], 37: ["zs0"], 41: ["zs1"], 57: ["or0"], 60: ["ap3"],
}

TAIL_PE = [
    (3, "out_tp1", "O"), (2, "gu4", "M"), (2, "gu5", "X"), (3, "out_tp0", "Y"), (2, "wts_tp", "S"), (1, "q0", "T"),
    (1, "q1", "U"), (3, "attn_tp", "V"), (2, "comb1", "M"), (2, "comb0", "X"), (3, "attn_proj", "O"),
    (0, "n_tp0", "Y"), (0, "n_tp1", "S"), (2, "down", "V"), (1, "e_tp0", "T"), (3, "tp1", "X"), (0, "proj1", "M"),
    (3, "gu0", "Y"), (3, "gu1", "S"), (3, "logits", "O"), (3, "gu2", "U"), (3, "gu3", "T"), (3, "gu4", "X"),
    (3, "gu5", "V"), (2, "tp2", "M"), (1, "e_tp1", "Y"), (1, "oa0", "O"), (1, "ob0", "S"), (2, "q0", "U"),
    (3, "wts_tp", "T"), (2, "gram", "M"), (2, "q1", "X"), (3, "comb0", "V"), (3, "comb1", "T"), (1, "oa1", "Y"),
    (3, "down", "O"), (1, "ob1", "S"), (2, "e_tp0", "M"), (1, "n_tp0", "V"), (2, "oa0", "T"), (2, "ob0", "U"),
    (3, "tp2", "X"), (2, "e_tp1", "O"), (3, "gram", "M"), (3, "q0", "V"), (2, "oa1", "Y"), (3, "q1", "S"),
    (1, "n_tp1", "X"), (2, "ob1", "O"), (2, "n_tp0", "T"), (1, "proj1", "U"), (3, "e_tp0", "M"), (3, "e_tp1", "V"),
    (3, "oa0", "X"), (3, "ob0", "S"), (3, "oa1", "O"), (3, "ob1", "Y"), (2, "n_tp1", "M"), (0, "tp3", "V"),
    (2, "proj1", "T"), (3, "n_tp0", "U"), (3, "n_tp1", "M"), (1, "tp3", "V"), (0, "ffn", "X"), (3, "proj1", "S"),
    (1, "ffn", "O"), (2, "tp3", "Y"), (2, "ffn", "U"), (3, "tp3", "T"), (3, "ffn", "M"),
]
TAIL_DVE = [
    (3, "norm0"), (1, "z0"), (2, "cm0"), (2, "cm1"), (3, "x1"), (1, "z1"), (3, "ap1"), (2, "x2"), (2, "ap2"),
    (0, "x3"), (3, "rg0"), (3, "re0"), (3, "wsplit0"), (1, "on0"), (2, "qvar0"), (3, "cm0"), (3, "cm1"), (2, "z0"),
    (2, "z1"), (3, "x2"), (1, "on1"), (3, "ap2"), (2, "on0"), (3, "qvar0"), (0, "ap3"), (3, "z0"), (3, "z1"),
    (2, "on1"), (1, "x3"), (3, "on0"), (3, "on1"), (1, "ap3"), (2, "x3"), (2, "ap3"), (0, "x4"), (3, "x3"), (1, "x4"),
    (3, "ap3"), (2, "x4"), (3, "x4"),
]
TAIL_ACT = [
    (2, "th4"), (2, "th5"), (2, "combT0"), (3, "attnT0"), (0, "onT0"), (1, "qe0"), (0, "onT1"), (1, "qET0"),
    (3, "xT1"), (1, "qe1"), (3, "th0"), (3, "elog0"), (3, "th1"), (3, "th2"), (3, "th3"), (2, "xT2"), (3, "th4"),
    (3, "th5"), (3, "combT0"), (1, "qET1"), (2, "qe0"), (2, "qe1"), (2, "qET0"), (1, "onT0"), (3, "xT2"), (2, "qET1"),
    (1, "onT1"), (3, "qe0"), (3, "qe1"), (3, "qET0"), (3, "qET1"), (2, "onT0"), (2, "onT1"), (0, "xT3"), (3, "onT0"),
    (3, "onT1"), (1, "xT3"), (0, "fh0"), (2, "xT3"), (1, "fh0"), (2, "fh0"), (3, "xT3"), (3, "fh0"),
]
TAIL_POOL = [
    (2, "hid2"), (2, "hid3"), (1, "qr0"), (2, "hid4"), (2, "hid5"), (1, "zs0"), (0, "or0"), (3, "pw1"), (1, "zs1"),
    (2, "pw2"), (2, "xb2"), (3, "hid0"), (3, "hid1"), (3, "hid2"), (3, "hid3"), (3, "hid4"), (3, "hid5"), (2, "qr0"),
    (0, "pw3"), (2, "zs0"), (2, "zs1"), (3, "pw2"), (1, "or0"), (3, "xb2"), (3, "qr0"), (3, "zs0"), (3, "zs1"),
    (2, "or0"), (1, "pw3"), (3, "or0"), (2, "pw3"), (3, "pw3"),
]


def offsets(i):
    return [(b, i - H0 * (b + 2)) for b in range(B) if i >= H0 * (b + 2)]


def bank_turns():
    turns, filled = {}, dict.fromkeys("OMXYSTUV", 0)

    def take(stage, key, bank):
        turns[stage, key] = (bank, filled[bank])
        filled[bank] += 1

    for i in range(MAIN):
        if i % GH == 1 and 1 <= i // GH <= 2 * B:
            take("max_tp", i // GH - 1, "M")
        j = i - LAG
        if j >= SH + 1 and (j - SH - 1) % SH == 0 and (j - SH - 1) // SH < B * H0 // SH:
            take("values", (j - SH - 1) // SH, "O")
        for b, o in offsets(i):
            for stage, bank in STAGES.get(o, []):
                take(stage, b, bank)
    for b, stage, bank in TAIL_PE:
        take(stage, b, bank)
    return turns


SENT = -2.0e38
STRUCK = 1.0e38


def build(nc, A, out):
    ctx = ExitStack()
    with ctx:
        def sb(name, shape, dt=F32):
            return ctx.enter_context(nc.sbuf_tensor(name, shape, dt))

        def sem(name):
            return ctx.enter_context(nc.semaphore(name))

        banks = [ctx.enter_context(nc.psum_tensor(f"bank{i}", [P, 512], F32)) for i in range(8)]
        bankS = banks[6:8]
        bankT = banks[0:2]
        shared = dict(zip("OMXYSTUV", banks[2:6] + bankS + bankT))

        x = sb("x", [P, NT, E])
        ctxT = sb("ctxT", [P, N])
        w_kT, w_vT, w_qT, w_oT = (sb(n, [P, E]) for n in ("w_kT", "w_vT", "w_qT", "w_oT"))
        bq_col, bk_col = sb("bq_col", [P, 1]), sb("bk_col", [P, 1])
        bv_row, bo_row = sb("bv_row", [P, E]), sb("bo_row", [P, E])
        gates = sb("gates", [P, 4])
        ident = sb("ident", [P, P])
        identb = sb("identb", [P, P], BF16)
        adj = sb("adj", [P, C, S])
        adjT = sb("adjT", [P, C, S])
        mask = sb("mask", [P, 2, C, S], I32)
        maskT = sb("maskT", [P, B, C, S], I32)
        w_router = sb("w_router", [P, EXP0])
        cb_row = sb("cb_row", [P, EXP0])
        w_gate = sb("w_gate", [P, HC, P])
        w_up = sb("w_up", [P, HC, P])
        w_down = sb("w_down", [P, HC, E])
        expand = sb("expand", [3 * EXP0, RC, P], BF16)
        tri = sb("tri", [P, 4, 4])
        w1q = sb("w1q", [P, I1])
        w1kv = sb("w1kv", [P, 2 * I1])
        w1out = sb("w1out", [P, PR, E])
        nullk = sb("nullk", [P, 1])
        nullv = sb("nullv", [P, D1])
        lnq_g, lnq_b = sb("lnq_g", [P, I1]), sb("lnq_b", [P, I1])
        lno_g, lno_b = sb("lno_g", [P, PR]), sb("lno_b", [P, PR])
        fw_T, fa1_T, fa2 = sb("fw_T", [P, E]), sb("fa1_T", [P, E]), sb("fa2", [P, E])
        fb_row = sb("fb_row", [P, E])

        tg = sb("tg", [P, 4])
        tg_half = sb("tg_half", [P, 1])
        half_neg = sb("half_neg", [P, 8])
        stats = sb("stats", [P, NT, 6])
        mv = sb("mv", [P, NT, 2])
        vare = sb("vare", [P, NT])
        rstd = sb("rstd", [P, NT])
        xn = sb("xn", [P, NT, E])
        xnT = sb("xnT", [P, N])
        kf = sb("kf", [P, N])
        kr = sb("kr", [P, N])
        kparts = sb("kparts", [P, 3, N], BF16)
        qf = sb("qf", [P, N])
        qr = sb("qr", [P, N])
        qparts = sb("qparts", [P, 3, N], BF16)
        qst = sb("qst", [P, SLOTS, N], BF16)
        kst = sb("kst", [P, SLOTS, N], BF16)
        vaug = sb("vaug", [P, NT, H0 * AW + 32 - AW])
        vheads = vaug[:, :, 0:H0 * AW].rearrange("p t (h w) -> p t h w", h=H0)
        adjm = sb("adjm", [P, B, C, S], BF16)
        adjmT = maskT[:, :, :, :].bitcast(F32)
        unread = kparts[:, 0:2, 0:HALF].rearrange("p r (c s) -> p r c s", c=C)
        mx = sb("mx", [P, 2, 2, C, GH // 2])
        mrow = sb("mrow", [2 * C * GH // 2, 2, P], BF16)
        sc_t = qparts[:, :, :].bitcast(F32)
        et = sb("et", [P, 2 * SH, C, S])
        outT = qr[:, :].rearrange("p (n s) -> p n s", n=SH)
        orec = sb("orec", [P, C, H0])
        attn = sb("attn", [P, C, E])
        attnT = sb("attnT", [P, C * P])
        tgbo = sb("tgbo", [P, E])

        kmx = sb("kmx", [P, B, PR])
        ksum = sb("ksum", [P, B, PR])
        ek0 = sb("ek0", [P, B, PR])
        kden = sb("kden", [P, B, PR])
        krec = sb("krec", [P, B, PR])
        kEn = sb("kEn", [P, NT, I1])
        v1 = sb("v1", [P, NT, I1])
        early = et[:, :, :, :].rearrange("p r c s -> p (r c s)")
        nkv = early[:, 0:B * PR * D1].rearrange("p (n e) -> p n e", e=D1)
        kE = early[:, 2 * B * PR * D1:2 * B * PR * D1 + N].rearrange("p (r n) -> p r n", r=2)
        ctx_t = early[:, B * PR * D1:2 * B * PR * D1].rearrange("p (n e) -> p n e", e=D1)
        ctx_bd = sb("ctx_bd", [P, B * PR, 2 * (D1 + 1)])
        w3 = sb("w3", [P, E])
        fa12 = sb("fa12", [P, E])
        wq_mean = sb("wq_mean", [P, 1])
        wq_c = w1q
        wq_cT = sb("wq_cT", [P, PR * P])
        wq_g = lnq_g
        gram = sb("gram", [P, P])
        wo_g = sb("wo_g", [P, PR, E])
        wo_c = wo_g
        ones_mean = sb("ones_mean", [P, P])
        lnb_bc = sb("lnb_bc", [P, PR, P])
        tgbw = sb("tgbw", [P, E])

        spent = kEn[:, :, :].rearrange("p t n -> p (t n)")
        hid = spent[:, 0:HC * S].rearrange("p (c s) -> p c s", c=HC)
        sil = spent[:, HC * S:(HC + 2) * S].rearrange("p (r s) -> p r s", r=2)
        up = spent[:, (HC + 2) * S:(HC + 4) * S].rearrange("p (r s) -> p r s", r=2)
        th = spent[:, (HC + 4) * S:(HC + 6) * S].rearrange("p (r s) -> p r s", r=2)
        gate = spent[:, (HC + 6) * S:(HC + 8) * S].rearrange("p (r s) -> p r s", r=2)
        TB = C
        elog = sb("elog", [P, TB * EXP0])
        score = sb("score", [P, TB, EXP0])
        biased = sb("biased", [P, TB * 4, 4])
        pairs = sb("pairs", [P, TB * 4, 6])
        gscore = sb("gscore", [P, TB, 4])
        gcmp = sb("gcmp", [P, TB, 4, 4])
        geq = sb("geq", [P, TB, 4, 4])
        grank = sb("grank", [P, TB * 4])
        gpen = sb("gpen", [P, TB * 4])
        cand = sb("cand", [P, TB, EXP0 + 4])
        best8 = sb("best8", [P, TB, 8])
        struck = sb("struck", [P, TB, EXP0 + 4])
        wts = sb("wts", [P, TB, EXP0])
        wsum = sb("wsum", [P, TB])
        wrec = sb("wrec", [P, TB])
        wrest = sb("wrest", [P, TB, EXP0])
        wparts = sb("wparts", [P, TB, 3, EXP0], BF16)
        combT = sb("combT", [3 * EXP0, S], BF16)

        qvar = sb("qvar", [P, NT])
        qrstd = sb("qrstd", [P, NT])
        junk = sb("junk", [P, E])
        late = v1[:, :, :].rearrange("p (k r) n -> p k r n", k=4)
        z = late[:, 0].rearrange("p r (h d) -> p r h d", h=H1)
        zmx = sb("zmx", [P, 2, H1])
        zs = late[:, 1].rearrange("p r (h d) -> p r h d", h=H1)
        qE = late[:, 2]
        qET = late[:, 3].rearrange("p r (c m) -> p r c m", c=PR)
        osum = sb("osum", [P, 2, H1])
        on = kf[:, :].rearrange("p (r n) -> p r n", r=2)
        onT = kr[:, :].rearrange("p (r c m) -> p r c m", r=2, c=PR)
        ostat = sb("ostat", [P, NT, 6])
        omv = sb("omv", [P, NT, 2])
        ove = sb("ove", [P, NT])
        orstd = sb("orstd", [P, NT])
        fh = qf[:, 0:C * E].rearrange("p (t e) -> p t e", t=C)

        k_scr = nc.dram_tensor("k_scr", [2, 3, D0 * SLOTS, N], BF16, kind="Internal").ap()
        q_scr = nc.dram_tensor("q_scr", [2, 3, D0 * SLOTS, N], BF16, kind="Internal").ap()

        LOADS = dict(x=1, ctx=1, wk=1, w1k=1, w1v=1, wv=1, wq=2, small=5, adj=1, adjT=2, moe=10, l1=7, ffn=4, id=2,
                     ones=1)
        ld = {n: sem(f"ld_{n}") for n in LOADS}
        ld_maskq = [sem(f"ld_maskq{i}") for i in range(2)]

        def load(eng, group, dst, src):
            eng.dma_start(dst, src).then_inc(ld[group], 16)

        def loaded(eng, *groups):
            for group in groups:
                eng.wait_ge(ld[group], 16 * LOADS[group])

        own_dve, own_act, own_pool = sem("own_dve"), sem("own_act"), sem("own_pool")
        gates_ok, nullk_ld, consts_ok = sem("gates_ok"), sem("nullk_ld"), sem("consts_ok")
        kproj, vproj, qproj = sem("kproj"), sem("vproj"), sem("qproj")
        k1_ok, kparts_ok, qf_ok, qparts_ok = (sem(n) for n in ("k1_ok", "kparts_ok", "qf_ok", "qparts_ok"))
        kspill, qspill = sem("kspill"), sem("qspill")
        kst_ld, qst_ld = ([sem(f"{n}{i}") for i in range(2)] for n in ("kst_ld", "qst_ld"))
        vaug_ok, adjm_ok, adjmT_ok, xbias_ok = sem("vaug_ok"), sem("adjm_ok"), sem("adjmT_ok"), sem("xbias_ok")
        tp0, xT0 = sem("tp0"), sem("xT0")
        ln_var = [sem(f"ln_var{i}") for i in range(4)]
        rstd_ok = sem("rstd_ok")
        tail_rstd = [sem(f"tail_rstd{i}") for i in range(4)]
        ln_xn = [sem(f"ln_xn{i}") for i in range(4)]
        fa12_mm, fa12_ok, w3_mm, w3_ok = sem("fa12_mm"), sem("fa12_ok"), sem("w3_mm"), sem("w3_ok")
        wqm_ok, wqc_ok, wqg_ok, wqT_mm, wqT_ok = (sem(n) for n in ("wqm_ok", "wqc_ok", "wqg_ok", "wqT_mm", "wqT_ok"))
        gram_mm, gram_ok, wog_ok, lnb_ok, wmean_mm, bw_ok = (
            sem(n) for n in ("gram_mm", "gram_ok", "wog_ok", "lnb_ok", "wmean_mm", "bw_ok"))
        k1mm, k1max, k1exp, k1tp, k1n, v1mm, v1_ok = (sem(n) for n in ("k1mm", "k1max", "k1exp", "k1tp", "k1n", "v1mm", "v1_ok"))
        c1mm, c1read, ctx_ok = sem("c1mm"), sem("c1read"), sem("ctx_ok")
        s_mm, s_max, t_mm, t_add, t_exp = (sem(n) for n in ("s_mm", "s_max", "t_mm", "t_add", "t_exp"))
        m_ld = [sem(f"m_ld{i}") for i in range(2)]
        filled = {k: sem(f"filled_{k}") for k in "OMXYSTUV"}
        read = {k: sem(f"read_{k}") for k in "OMXYSTUV"}
        th_ok, hid_ok, w_ok, wparts_ok = (sem(n) for n in ("th_ok", "hid_ok", "w_ok", "wparts_ok"))
        qr_ok, z_ok, zs_ok, qe_ok, on_ok, ov_ok, or_ok, xb3_ok = (
            sem(n) for n in ("qr_ok", "z_ok", "zs_ok", "qe_ok", "on_ok", "ov_ok", "or_ok", "xb3_ok"))
        x4_ok, stored = sem("x4_ok"), sem("stored")

        turns = bank_turns()

        def bank_of(stage, key):
            return shared[turns[stage, key][0]]

        def take_bank(pe, stage, key):
            name, turn = turns[stage, key]
            if turn:
                pe.wait_ge(read[name], turn)
            return shared[name]

        def fill(ins, stage, key):
            ins.then_inc(filled[turns[stage, key][0]], 1)

        def wait_filled(eng, stage, key):
            name, turn = turns[stage, key]
            eng.wait_ge(filled[name], turn + 1)

        def done_reading(ins, stage, key):
            ins.then_inc(read[turns[stage, key][0]], 1)

        def wait_read(eng, stage, key):
            name, turn = turns[stage, key]
            eng.wait_ge(read[name], turn + 1)

        def head(i):
            b, h = divmod(i, H0)
            return b, h, h // 2, 64 * (h % 2)

        def tiles_of(b):
            return slice(b * C, (b + 1) * C)

        def toks(b):
            return slice(b * S, (b + 1) * S)

        def v_set(i):
            j = i - LAG - SH - 1
            return j // SH if j >= 0 and j % SH == 0 and j // SH < B * H0 // SH else None

        ALL_STEPS = range(MAIN)
        block = ctx.enter_context(nc.Block())

        @block.sync
        def _(sp):
            load(sp, "ctx", ctxT[:, :], A["ctxT"])
            load(sp, "wk", w_kT[:, :], A["wkT"])
            load(sp, "w1k", w1kv[:, 0:I1], A["w1kv"][:, 0:I1])
            load(sp, "wv", w_vT[:, :], A["wvT"])
            load(sp, "w1v", w1kv[:, I1:2 * I1], A["w1kv"][:, I1:2 * I1])
            load(sp, "wq", w_qT[:, :], A["wqT"])
            load(sp, "wq", w_oT[:, :], A["woT"])
            load(sp, "ones", kst[KROWS:KROWS + 65:64, :, :], A["ones"])
            load(sp, "l1", w1q[:, :], A["w1q"])
            load(sp, "l1", w1out[:, :, :], A["w1out"])
            load(sp, "l1", nullv[:, :], A["nullv"])
            load(sp, "l1", lnq_g[:, :], A["lnq_g"])
            load(sp, "l1", lnq_b[:, :], A["lnq_b"])
            load(sp, "l1", lno_g[:, :], A["lno_g"])
            load(sp, "l1", lno_b[:, :], A["lno_b"])
            load(sp, "ffn", fw_T[:, :], A["fwT"])
            load(sp, "ffn", fa1_T[:, :], A["fa1T"])
            load(sp, "ffn", fa2[:, :], A["fa2"])
            load(sp, "ffn", fb_row[:, :], A["fb"])
            load(sp, "adj", adj[:, :, :], A["adj"])
            sp.dma_start(mask[:, 0, :, :], A["mask"][:, 0]).then_inc(ld_maskq[0], 16)

            def spill(parts, scr, half, ready, spilled):
                cols = slice(half * HALF, (half + 1) * HALF)
                sp.wait_ge(ready, half + 1)
                for c in range(3):
                    sp.dma_start(scr[:, c, :, cols], parts[:, c, cols]).then_inc(spilled, 16)

            def restack(scr, stack, cols, landed, runs):
                for par in range(2):
                    term = 0
                    for part, count, repeats in runs:
                        r0 = 64 * par + term * D0
                        rows = count * repeats * D0
                        src = scr[par, part:part + count, :, cols].rearrange("c (d s) n -> (c d) s n", d=D0)
                        if repeats > 1:
                            src = src.unsqueeze(0).to_broadcast([repeats, D0, SLOTS, cols.stop - cols.start])
                        sp.dma_start(stack[r0:r0 + rows, :, cols], src).then_inc(landed, 16)
                        term += count * repeats

            for half in range(2):
                cols = slice(half * HALF, (half + 1) * HALF)
                spill(kparts, k_scr, half, kparts_ok, kspill)
                spill(qparts, q_scr, half, qparts_ok, qspill)
                sp.wait_ge(kspill, 16 * 3 * (half + 1))
                restack(k_scr, kst, cols, kst_ld[half], K_RUNS)
                sp.wait_ge(qspill, 16 * 3 * (half + 1))
                restack(q_scr, qst, cols, qst_ld[half], Q_RUNS)
                if half == 0:
                    load(sp, "adjT", adjT[:, :, :], A["adjT"])
                    load(sp, "adjT", maskT[:, :, :, :], A["maskT"])
                    sp.dma_start(mask[:, 1, :, :], A["mask"][:, 1]).then_inc(ld_maskq[1], 16)
            load(sp, "moe", w_router[:, :], A["router_w"])
            load(sp, "moe", cb_row[:, :], A["cb"])
            load(sp, "moe", expand[:, :, :], A["expand"])
            load(sp, "moe", tri[:, :, :], A["tri"])
            load(sp, "moe", w_gate[:, 0:RC, :], A["gate_w"])
            load(sp, "moe", w_gate[:, RC:HC, :], A["sgate_w"])
            load(sp, "moe", w_up[:, 0:RC, :], A["up_w"])
            load(sp, "moe", w_up[:, RC:HC, :], A["sup_w"])
            load(sp, "moe", w_down[:, 0:RC, :], A["down_w"])
            load(sp, "moe", w_down[:, RC:HC, :], A["sdown_w"])
            for g in range(2 * B):
                b, s0 = g // 2, (g % 2) * GH // 2
                wait_read(sp, "max_tp", g)
                for par in range(2):
                    for qc in range(C):
                        r0 = (par * C + qc) * GH // 2
                        t0 = b * S + qc * P
                        sp.dma_start(qst[64 * par + KROWS:64 * par + KROWS + 1, s0:s0 + GH // 2, t0:t0 + P],
                                     mrow[r0:r0 + GH // 2, g % 2, :]).then_inc(m_ld[g % 2], 16)
                if g in (1, 3):
                    nb = 2 + g // 2
                    sp.wait_ge(adjm_ok, nb - 1)
                    sp.dma_start(mask[:, nb % 2, :, :], A["mask"][:, nb]).then_inc(ld_maskq[nb % 2], 16)
            for b in range(B):
                sp.wait_ge(x4_ok, b + 1)
                sp.dma_start(out[:, tiles_of(b)], x[:, tiles_of(b), :]).then_inc(stored, 16)
            sp.wait_ge(stored, 16 * B)

        @block.gpsimd
        def _(pool):
            steps = [0]

            def link(ins):
                steps[0] += 1
                ins.then_inc(own_pool, 1)
                pool.wait_ge(own_pool, steps[0])

            def power(dst, src, n, ready):
                nc.gpsimd.tensor_tensor(dst, src, half_neg[:, 0:n], ALU.pow).then_inc(ready, 1)

            link(nc.gpsimd.memset(half_neg[:, :], -0.5))
            for half in range(2):
                pool.wait_ge(ln_var[0], half + 1)
                power(rstd[:, half * HT:(half + 1) * HT], vare[:, half * HT:(half + 1) * HT], HT, rstd_ok)
            link(nc.gpsimd.memset(ones_mean[:, :], 1.0 / I1))
            nc.gpsimd.memset(vaug[:, :, :], 1.0).then_inc(consts_ok, 1)
            cols = slice(HALF, N)
            pool.wait_ge(k1_ok, 2)
            link(nc.gpsimd.tensor_tensor(kr[:, cols], kf[:, cols], kparts[:, 0, cols], ALU.subtract))
            link(nc.gpsimd.tensor_copy(kparts[:, 1, cols], kr[:, cols]))
            pool.wait_ge(kparts_ok, 1)
            nc.gpsimd.tensor_tensor(kparts[:, 2, cols], kr[:, cols], kparts[:, 1, cols], ALU.subtract).then_inc(kparts_ok, 1)
            loaded(pool, "adj")
            pool.wait_ge(ld_maskq[0], 16)
            link(nc.gpsimd.tensor_scalar(mask[:, 0].bitcast(F32), mask[:, 0], 0.0, NEG, ALU.is_equal, ALU.mult))
            nc.gpsimd.tensor_tensor(adjm[:, 0], mask[:, 0].bitcast(F32), adj[:, :, :], ALU.add).then_inc(adjm_ok, 1)
            pool.wait_ge(wqm_ok, 1)
            nc.gpsimd.tensor_scalar(wq_c[:, :], w1q[:, :], wq_mean[:, :], None, ALU.subtract).then_inc(wqc_ok, 1)
            pool.wait_ge(wqc_ok, 1)
            nc.gpsimd.tensor_tensor(wq_g[:, :], wq_c[:, :], lnq_g[:, :], ALU.mult).then_inc(wqg_ok, 1)
            loaded(pool, "adjT")
            link(nc.gpsimd.tensor_scalar(adjmT[:, 0], maskT[:, 0], 0.0, NEG, ALU.is_equal, ALU.mult))
            nc.gpsimd.tensor_tensor(adjmT[:, 0], adjmT[:, 0], adjT[:, :, :], ALU.add).then_inc(adjmT_ok, 1)
            nc.gpsimd.tensor_tensor(wo_g[:, :, :], w1out[:, :, :], lno_g[:, :].unsqueeze(2).to_broadcast([P, PR, E]),
                                    ALU.mult).then_inc(wog_ok, 1)
            nc.gpsimd.tensor_copy(lnb_bc[:, :, :], lno_b[:, :].unsqueeze(2).to_broadcast([P, PR, P])).then_inc(lnb_ok, 1)
            pool.wait_ge(gates_ok, 1)
            loaded(pool, "small")
            link(nc.gpsimd.tensor_scalar(tgbo[:, :], bo_row[:, :], tg[:, 0:1], None, ALU.mult))
            pool.wait_ge(ln_xn[0], 2)
            nc.gpsimd.tensor_tensor(x[:, :, :], x[:, :, :],
                                    tgbo[:, :].unsqueeze(1).to_broadcast([P, NT, E]), ALU.add).then_inc(xbias_ok, 1)
            link(nc.gpsimd.memset(ctx_bd[:, :, :], 0.0))
            link(nc.gpsimd.memset(ctx_bd[0:D1, :, D1:D1 + 1], 1.0))
            link(nc.gpsimd.memset(ctx_bd[D1:P, :, 2 * D1 + 1:2 * D1 + 2], 1.0))
            nc.gpsimd.memset(cand[:, :, EXP0:EXP0 + 4], SENT).then_inc(consts_ok, 1)

            def beside(b, step):
                ts = tiles_of(b)
                tt = range(b * C, (b + 1) * C)
                n = int(step[-1])
                if step[:2] == "ap":
                    pool.wait_ge(ln_var[n], b + 1)
                    link(nc.gpsimd.tensor_tensor(rstd[:, ts], vare[:, ts], half_neg[:, 0:C], ALU.pow))
                    for t in tt:
                        last = nc.gpsimd.tensor_scalar(xn[:, t, :], x[:, t, :], mv[:, t, 0:1], rstd[:, t:t + 1],
                                                       ALU.subtract, ALU.mult)
                    last.then_inc(ln_xn[n], 1)
                    if n == 2:
                        beside(b, "xb2")
                elif step == "xb2":
                    pool.wait_ge(ln_xn[2], b + 1)
                    nc.gpsimd.tensor_tensor(x[:, ts, :], x[:, ts, :], tgbw[:, :].unsqueeze(1).to_broadcast([P, C, E]),
                                            ALU.add).then_inc(xb3_ok, 1)
                elif step[:2] == "pw":
                    pool.wait_ge(ln_var[n], b + 1)
                    power(rstd[:, ts], vare[:, ts], C, tail_rstd[n])
                elif step[:3] == "hid":
                    pool.wait_ge(th_ok, b * HC + n + 1)
                    if n == 0 and b:
                        wait_filled(pool, "down", b - 1)
                    link(nc.gpsimd.tensor_tensor(sil[:, n % 2, :], th[:, n % 2, :], gate[:, n % 2, :], ALU.mult))
                    nc.gpsimd.tensor_tensor(hid[:, GU[n], :], sil[:, n % 2, :], up[:, n % 2, :],
                                            ALU.mult).then_inc(hid_ok, 1)
                elif step == "wsplit0":
                    pool.wait_ge(w_ok, b + 1)
                    if b:
                        wait_filled(pool, "wts_tp", b - 1)
                    link(nc.gpsimd.tensor_copy(wparts[:, :, 0, :], wts[:, :, :]))
                    link(nc.gpsimd.tensor_tensor(wrest[:, :, :], wts[:, :, :], wparts[:, :, 0, :], ALU.subtract))
                    link(nc.gpsimd.tensor_copy(wparts[:, :, 1, :], wrest[:, :, :]))
                    nc.gpsimd.tensor_tensor(wparts[:, :, 2, :], wrest[:, :, :], wparts[:, :, 1, :],
                                            ALU.subtract).then_inc(wparts_ok, 1)
                elif step == "qr0":
                    wait_read(pool, "gram", b)
                    power(qrstd[:, ts], qvar[:, ts], C, qr_ok)
                elif step[:2] == "zs":
                    pool.wait_ge(z_ok, C * b + n + 1)
                    if b:
                        pool.wait_ge(qe_ok, C * (b - 1) + n + 1)
                    nc.gpsimd.tensor_tensor(zs[:, n, :, :], z[:, n, :, :],
                                            zmx[:, n, :].unsqueeze(2).to_broadcast([P, H1, D1]),
                                            ALU.subtract).then_inc(zs_ok, 1)
                elif step == "or0":
                    pool.wait_ge(ov_ok, b + 1)
                    link(nc.gpsimd.tensor_tensor(orstd[:, ts], ove[:, ts], half_neg[:, 0:C], ALU.pow))
                    nc.gpsimd.tensor_scalar(orstd[:, ts], orstd[:, ts], tg[:, 1:2], None, ALU.mult).then_inc(or_ok, 1)

            for i in ALL_STEPS:
                nb, k = i // H0 + 1, i % H0
                if nb < B and k in (1, 3, 11, 13):
                    if k == 1:
                        pool.wait_ge(ld_maskq[nb % 2], 16 * (nb // 2 + 1))
                        link(nc.gpsimd.tensor_scalar(mask[:, nb % 2].bitcast(F32), mask[:, nb % 2], 0.0, NEG,
                                                     ALU.is_equal, ALU.mult))
                    if k == 3:
                        nc.gpsimd.tensor_tensor(adjm[:, nb], mask[:, nb % 2].bitcast(F32), adj[:, :, :],
                                                ALU.add).then_inc(adjm_ok, 1)
                    if k == 11:
                        link(nc.gpsimd.tensor_scalar(adjmT[:, nb], maskT[:, nb], 0.0, NEG, ALU.is_equal, ALU.mult))
                    if k == 13:
                        nc.gpsimd.tensor_tensor(adjmT[:, nb], adjmT[:, nb], adjT[:, :, :], ALU.add).then_inc(adjmT_ok, 1)
                if i == 9:
                    pool.wait_ge(c1read, B)
                    kb = krec[:, :, :].rearrange("p b c -> p (b c)").unsqueeze(2).to_broadcast([P, B * PR, D1])
                    link(nc.gpsimd.tensor_tensor(ctx_bd[0:D1, :, 0:D1], ctx_t[0:D1, :, :], kb[0:D1], ALU.mult))
                    nc.gpsimd.tensor_tensor(ctx_bd[D1:P, :, D1 + 1:2 * D1 + 1], ctx_t[D1:P, :, :], kb[D1:P],
                                            ALU.mult).then_inc(ctx_ok, 1)
                    pool.wait_ge(ctx_ok, 1)
                for b, o in offsets(i):
                    for step in POOL_AT.get(o, []):
                        beside(b, step)
            for b, step in TAIL_POOL:
                beside(b, step)

        def k1_evac(act, u):
            c, half = divmod(u, 2)
            act.wait_ge(k1tp, u + 1)
            nc.scalar.copy(kEn[:, half * HT:(half + 1) * HT, c * P:(c + 1) * P],
                           banks[4 + u % 2][:, :].rearrange("p (t c) -> p t c", t=HT)).then_inc(k1n, 1)

        @block.scalar
        def _(act):
            steps = [0]

            def link(ins):
                steps[0] += 1
                ins.then_inc(own_act, 1)
                act.wait_ge(own_act, steps[0])

            def evac(dst, src, stage, b):
                wait_filled(act, stage, b)
                done_reading(nc.scalar.copy(dst, src), stage, b)

            load(act, "x", x[:, :, :], A["x"])
            load(act, "small", bk_col[:, :], A["bk"])
            load(act, "small", gates[:, :], A["gates"])
            load(act, "small", bq_col[:, :], A["bq"])
            load(act, "small", bv_row[:, :], A["bv"])
            load(act, "small", bo_row[:, :], A["bo"])
            load(act, "id", ident[:, :], A["ident"])
            load(act, "id", identb[:, :], A["identb"])
            act.dma_start(nullk[:, :], A["nullk"]).then_inc(nullk_ld, 16)
            loaded(act, "small")
            nc.scalar.activation(tg[:, :], gates[:, :], ACT.Tanh).then_inc(gates_ok, 1)
            for half in range(2):
                cols = slice(half * HALF, (half + 1) * HALF)
                act.wait_ge(kproj, half + 1)
                link(nc.scalar.activation(kf[:, cols], banks[4 + half][:, :], ACT.Identity, bias=bk_col[:, :]))
                nc.scalar.copy(kparts[:, 0, cols], kf[:, cols]).then_inc(k1_ok, 1)
            for half in range(2):
                act.wait_ge(tp0, half + 1)
                nc.scalar.copy(xnT[:, half * HALF:(half + 1) * HALF], banks[6 + half][:, :]).then_inc(xT0, 1)
            act.wait_ge(nullk_ld, 16)
            for u in range(2 * PR):
                c, half = divmod(u, 2)
                act.wait_ge(v1mm, u + 1)
                nc.scalar.copy(v1[:, u, :], banks[2 + u % 2][:, :]).then_inc(v1_ok, 1)
                if u >= 2:
                    act.wait_ge(k1tp, u - 1)
                act.wait_ge(k1max, u + 1)
                for k in range(2):
                    b = 2 * half + k
                    nc.scalar.activation(kE[:, u % 2, k * S:(k + 1) * S], banks[u % 2][:, k * S:(k + 1) * S], ACT.Exp,
                                         bias=kmx[:, b, c:c + 1], accum_out=ksum[:, b, c:c + 1])
                    last = nc.scalar.activation(ek0[:, b, c:c + 1], nullk[:, :], ACT.Exp, bias=kmx[:, b, c:c + 1])
                last.then_inc(k1exp, 1)
                if u >= 1:
                    k1_evac(act, u - 1)
            k1_evac(act, 2 * PR - 1)

            def beside(b, step):
                n = int(step[-1])
                if step == "attnT0":
                    evac(attnT[:, :], bank_of("attn_tp", b)[:, 0:C * P], "attn_tp", b)
                elif step[:2] == "xT":
                    evac(xnT[:, toks(b)], bank_of(f"tp{n}", b)[:, 0:S], f"tp{n}", b)
                elif step == "elog0":
                    if b:
                        act.wait_ge(w_ok, b)
                    wait_filled(act, "logits", b)
                    done_reading(nc.scalar.activation(elog[:, :], bank_of("logits", b)[:, 0:C * EXP0], ACT.Exp,
                                                      scale=-1.0), "logits", b)
                elif step[:2] == "th":
                    wait_filled(act, f"gu{n}", b)
                    gu = bank_of(f"gu{n}", b)
                    if b * HC + n >= 2:
                        act.wait_ge(hid_ok, b * HC + n - 1)
                    nc.scalar.copy(up[:, n % 2, :], gu[:, S:2 * S])
                    nc.scalar.copy(gate[:, n % 2, :], gu[:, 0:S])
                    done_reading(nc.scalar.activation(th[:, n % 2, :], gu[:, 0:S], ACT.Tanh, scale=0.5), f"gu{n}", b)
                    wait_read(act, f"gu{n}", b)
                    nc.scalar.activation(th[:, n % 2, :], th[:, n % 2, :], ACT.Copy, bias=1.0).then_inc(th_ok, 1)
                elif step == "combT0":
                    if b:
                        wait_filled(act, "comb0", b - 1)
                        wait_filled(act, "comb1", b - 1)
                    evac(combT[:, :], bank_of("wts_tp", b).bitcast(BF16)[0:3 * EXP0, 0:S], "wts_tp", b)
                elif step[:2] == "qe":
                    act.wait_ge(zs_ok, C * b + n + 1)
                    if b:
                        wait_filled(act, f"e_tp{n}", b - 1)
                    nc.scalar.activation(qE[:, n, :], zs[:, n, :, :].rearrange("p h d -> p (h d)"),
                                         ACT.Exp).then_inc(qe_ok, 1)
                elif step[:3] == "qET":
                    if b:
                        wait_filled(act, f"oa{n}", b - 1)
                        wait_filled(act, f"ob{n}", b - 1)
                    evac(qET[:, n, :, :].rearrange("p c s -> p (c s)"), bank_of(f"e_tp{n}", b)[:, :], f"e_tp{n}", b)
                elif step[:3] == "onT":
                    if b:
                        wait_filled(act, "proj1", b - 1)
                    evac(onT[:, n, :, :].rearrange("p c s -> p (c s)"), bank_of(f"n_tp{n}", b)[:, :], f"n_tp{n}", b)
                elif step == "fh0":
                    wait_filled(act, "ffn", b)
                    if b:
                        act.wait_ge(x4_ok, b)
                    done_reading(nc.scalar.activation(fh[:, :, :].rearrange("p t e -> p (t e)"),
                                                      bank_of("ffn", b)[:, 0:C * E], ACT.Tanh), "ffn", b)

            act.wait_ge(fa12_mm, 1)
            nc.scalar.copy(fa12[:, :], banks[4][:, 0:E]).then_inc(fa12_ok, 1)
            act.wait_ge(wqT_mm, 1)
            nc.scalar.copy(wq_cT[:, :], banks[5][:, :]).then_inc(wqT_ok, 1)
            act.wait_ge(w3_mm, 1)
            nc.scalar.copy(w3[:, :], banks[4][:, 0:E]).then_inc(w3_ok, 1)
            act.wait_ge(gram_mm, 1)
            nc.scalar.mul(gram[:, :], banks[5][:, 0:P], 1.0 / I1).then_inc(gram_ok, 1)

            for i in ALL_STEPS:
                j = i - LAG
                if 0 <= j < B * H0:
                    act.wait_ge(t_add, j + 1)
                    if j == 0:
                        act.wait_ge(ctx_ok, 1)
                    if j >= 2 * SH:
                        wait_filled(act, "values", j // SH - 2)
                    nc.scalar.activation(et[:, j % (2 * SH), :, :].rearrange("p c s -> p (c s)"), sc_t[:, j % SC_RING, :],
                                         ACT.Exp).then_inc(t_exp, 1)
                if i % GH == 1 and 1 <= i // GH <= 2 * B:
                    g = i // GH - 1
                    wait_filled(act, "max_tp", g)
                    if g >= 2:
                        act.wait_ge(m_ld[g % 2], 64 * (g // 2))
                    done_reading(nc.scalar.mul(mrow[:, g % 2, :], bank_of("max_tp", g)[0:16, 0:P], -1.0), "max_tp", g)
                n = v_set(i)
                if n is not None:
                    evac(outT[:, n % SH, :], bank_of("values", n)[:, 0:S], "values", n)
                for b, o in offsets(i):
                    for step in ACT_AT.get(o, []):
                        beside(b, step)
            for b, step in TAIL_ACT:
                beside(b, step)

        @block.vector
        def _(dve):
            steps = [0]

            def link(ins):
                steps[0] += 1
                ins.then_inc(own_dve, 1)
                dve.wait_ge(own_dve, steps[0])

            def ln_stats(i, ts):
                for t in range(ts.start, ts.stop):
                    last = nc.vector.bn_stats(stats[:, t, :], x[:, t, :])
                link(last)
                for t in range(ts.start, ts.stop):
                    last = nc.vector.bn_aggr(mv[:, t, :], stats[:, t, :])
                link(last)
                nc.vector.tensor_scalar(vare[:, ts], mv[:, ts, 1], EPS, None, ALU.add).then_inc(ln_var[i], 1)

            def ln_apply(half):
                dve.wait_ge(rstd_ok, half + 1)
                for t in range(half * HT, (half + 1) * HT):
                    last = nc.vector.tensor_scalar(xn[:, t, :], x[:, t, :], mv[:, t, 0:1], rstd[:, t:t + 1],
                                                   ALU.subtract, ALU.mult)
                last.then_inc(ln_xn[0], 1)

            def k1_max(u):
                c, half = divmod(u, 2)
                dve.wait_ge(k1mm, u + 1)
                m = kmx[:, 2 * half:2 * half + 2, c]
                link(nc.vector.tensor_reduce(m, banks[u % 2][:, :].rearrange("p (b s) -> p b s", b=2), AX.X, ALU.max))
                nc.vector.tensor_scalar(m, m, nullk[:, :], -1.0, ALU.max, ALU.mult).then_inc(k1max, 1)

            def split(dst, full, rest, half, ready):
                cols = slice(half * HALF, (half + 1) * HALF)
                link(nc.vector.tensor_tensor(rest[:, cols], full[:, cols], dst[:, 0, cols], ALU.subtract))
                link(nc.vector.tensor_copy(dst[:, 1, cols], rest[:, cols]))
                nc.vector.tensor_tensor(dst[:, 2, cols], rest[:, cols], dst[:, 1, cols], ALU.subtract).then_inc(ready, 1)

            def k_split(half):
                dve.wait_ge(k1_ok, half + 1)
                split(kparts, kf, kr, half, kparts_ok)

            def q_split(half):
                cols = slice(half * HALF, (half + 1) * HALF)
                dve.wait_ge(qproj, half + 1)
                nc.vector.tensor_scalar(qf[:, cols], banks[6 + half][:, :], bq_col[:, :], float(D0) ** -0.5,
                                        ALU.add, ALU.mult).then_inc(qf_ok, 1)
                dve.wait_ge(qf_ok, half + 1)
                link(nc.vector.tensor_copy(qparts[:, 0, cols], qf[:, cols]))
                split(qparts, qf, qr, half, qparts_ok)

            def v_bias(half):
                dve.wait_ge(vproj, half + 1)
                nc.vector.tensor_tensor(
                    vheads[:, half * HT:(half + 1) * HT, :, 0:D0],
                    banks[2 + half][:, :].rearrange("p (t h d) -> p t h d", t=HT, h=H0),
                    bv_row[:, :].rearrange("p (h d) -> p h d", h=H0).unsqueeze(1).to_broadcast([P, HT, H0, D0]),
                    ALU.add).then_inc(vaug_ok, 1)

            loaded(dve, "x")
            for half in range(2):
                ln_stats(0, slice(half * HT, (half + 1) * HT))
            for half in range(2):
                ln_apply(half)
            dve.wait_ge(nullk_ld, 16)
            loaded(dve, "small")
            k1_max(0)
            k_split(0)
            k1_max(1)
            q_split(0)
            k1_max(2)
            k1_max(3)
            q_split(1)
            for u in range(4, 2 * PR):
                k1_max(u)
            loaded(dve, "l1")
            link(nc.vector.reduce_sum(wq_mean[:, :], w1q[:, :], AX.X))
            nc.vector.tensor_scalar(wq_mean[:, :], wq_mean[:, :], 1.0 / I1, None, ALU.mult).then_inc(wqm_ok, 1)
            dve.wait_ge(gates_ok, 1)
            nc.vector.tensor_scalar(tg_half[:, :], tg[:, 2:3], 0.5, None, ALU.mult)

            def prepare(i):
                if i == 1:
                    dve.wait_ge(consts_ok, 1)
                    v_bias(0)
                    v_bias(1)
                if i == 2:
                    dve.wait_ge(k1exp, 2 * PR)
                    link(nc.vector.tensor_tensor(kden[:, :, :], ksum[:, :, :], ek0[:, :, :], ALU.add))
                    link(nc.vector.reciprocal(krec[:, :, :], kden[:, :, :]))
                    link(nc.vector.tensor_tensor(nkv[:, :, :], nullv[:, :].unsqueeze(1).to_broadcast([P, B * PR, D1]),
                                                 ek0[:, :, :].rearrange("p b c -> p (b c)").unsqueeze(2).to_broadcast([P, B * PR, D1]),
                                                 ALU.mult))
                for b in CONTEXTS.get(i - 1, []):
                    dve.wait_ge(c1mm, b + 1)
                    pr = slice(b * PR, (b + 1) * PR)
                    nc.vector.tensor_tensor(ctx_t[:, pr, :], banks[b][:, 0:PR * D1].rearrange("p (c e) -> p c e", c=PR),
                                            nkv[:, pr, :], ALU.add).then_inc(c1read, 1)
                if i == 6:
                    dve.wait_ge(wmean_mm, 1)
                    nc.vector.tensor_tensor(wo_c[:, :, :], wo_g[:, :, :],
                                            banks[4][:, 0:E].unsqueeze(1).to_broadcast([P, PR, E]), ALU.subtract)
                    nc.vector.tensor_scalar(tgbw[:, :], banks[4][:, E:2 * E], tg[:, 1:2], None, ALU.mult).then_inc(bw_ok, 1)
            def route_groups(b):
                wait_read(dve, "logits", b)
                link(nc.vector.tensor_scalar(elog[:, :], elog[:, :], 1.0, None, ALU.add))
                link(nc.vector.reciprocal(score[:, :, :].rearrange("p t e -> p (t e)"), elog[:, :]))
                link(nc.vector.tensor_tensor(biased[:, :, :].rearrange("p (t g) e -> p t (g e)", t=TB), score[:, :, :],
                                             cb_row[:, :].unsqueeze(1).to_broadcast([P, TB, EXP0]), ALU.add))
                nc.vector.tensor_tensor(pairs[:, :, 0:3], biased[:, :, 0:3], biased[:, :, 1:4], ALU.add)
                nc.vector.tensor_tensor(pairs[:, :, 3:5], biased[:, :, 0:2], biased[:, :, 2:4], ALU.add)
                link(nc.vector.tensor_tensor(pairs[:, :, 5:6], biased[:, :, 0:1], biased[:, :, 3:4], ALU.add))
                link(nc.vector.tensor_reduce(gscore[:, :, :].rearrange("p t g -> p (t g)"), pairs[:, :, :], AX.X, ALU.max))
                other = gscore[:, :, :].unsqueeze(2).to_broadcast([P, TB, 4, 4])
                mine = gscore[:, :, :].unsqueeze(3).to_broadcast([P, TB, 4, 4])
                nc.vector.tensor_tensor(gcmp[:, :, :, :], other, mine, ALU.is_gt)
                link(nc.vector.tensor_tensor(geq[:, :, :, :], other, mine, ALU.is_equal))
                link(nc.vector.tensor_tensor(geq[:, :, :, :], geq[:, :, :, :],
                                             tri[:, :, :].unsqueeze(1).to_broadcast([P, TB, 4, 4]), ALU.mult))
                link(nc.vector.tensor_tensor(gcmp[:, :, :, :], gcmp[:, :, :, :], geq[:, :, :, :], ALU.add))
                link(nc.vector.reduce_sum(grank[:, :], gcmp[:, :, :, :].rearrange("p t g h -> p (t g) h"), AX.X))
                link(nc.vector.tensor_scalar(gpen[:, :], grank[:, :], float(TOPG), NEG, ALU.is_ge, ALU.mult))
                link(nc.vector.tensor_tensor(cand[:, :, 0:EXP0].rearrange("p t (g e) -> p t g e", g=4),
                                             biased[:, :, :].rearrange("p (t g) e -> p t g e", t=TB),
                                             gpen[:, :].rearrange("p (t g) -> p t g", t=TB).unsqueeze(3).to_broadcast([P, TB, 4, 4]),
                                             ALU.add))

            def route_experts(b):
                for t in range(TB):
                    last = nc.vector.max(best8[:, t, :], cand[:, t, 0:EXP0])
                link(last)
                link(nc.vector.memset(best8[:, :, TOPK:8], SENT))
                for t in range(TB):
                    last = nc.vector.match_replace(struck[:, t, :], best8[:, t, :], cand[:, t, :], STRUCK)
                link(last)
                link(nc.vector.tensor_scalar(wts[:, :, :], struck[:, :, 0:EXP0], STRUCK, None, ALU.is_equal))
                link(nc.vector.tensor_tensor(wts[:, :, :], wts[:, :, :], score[:, :, :], ALU.mult))
                link(nc.vector.reduce_sum(wsum[:, :], wts[:, :, :], AX.X))
                link(nc.vector.tensor_scalar(wsum[:, :], wsum[:, :], 1e-20, None, ALU.add))
                link(nc.vector.reciprocal(wrec[:, :], wsum[:, :]))
                nc.vector.tensor_tensor(wts[:, :, :], wts[:, :, :], wrec[:, :].unsqueeze(2).to_broadcast([P, TB, EXP0]),
                                        ALU.mult).then_inc(w_ok, 1)

            def beside(b, step):
                ts = tiles_of(b)
                n = int(step[-1])
                if step[:2] == "ap":
                    first = min(k for k, name in TAIL_DVE if name == step)
                    dve.wait_ge(tail_rstd[n], b - first + 1)
                    dve.wait_ge(ln_xn[n], b)
                    for t in range(b * C, (b + 1) * C):
                        last = nc.vector.tensor_scalar(xn[:, t, :], x[:, t, :], mv[:, t, 0:1], rstd[:, t:t + 1],
                                                       ALU.subtract, ALU.mult)
                    last.then_inc(ln_xn[n], 1)
                elif step == "wsplit0":
                    dve.wait_ge(w_ok, b + 1)
                    dve.wait_ge(wparts_ok, b)
                    wait_filled(dve, "wts_tp", b - 1)
                    link(nc.vector.tensor_copy(wparts[:, :, 0, :], wts[:, :, :]))
                    link(nc.vector.tensor_tensor(wrest[:, :, :], wts[:, :, :], wparts[:, :, 0, :], ALU.subtract))
                    link(nc.vector.tensor_copy(wparts[:, :, 1, :], wrest[:, :, :]))
                    nc.vector.tensor_tensor(wparts[:, :, 2, :], wrest[:, :, :], wparts[:, :, 1, :],
                                            ALU.subtract).then_inc(wparts_ok, 1)
                elif step == "norm0":
                    for qc in range(C):
                        wait_filled(dve, f"out_tp{qc}", b)
                        o4 = bank_of(f"out_tp{qc}", b)[:, :].rearrange("p (h w) -> p h w", w=32)
                        link(nc.vector.reciprocal(orec[:, qc, :], o4[:, :, D0]))
                        done_reading(nc.vector.tensor_tensor(
                            attn[:, qc, :].rearrange("p (h d) -> p h d", h=H0), o4[:, :, 0:D0],
                            orec[:, qc, :].unsqueeze(2).to_broadcast([P, H0, D0]), ALU.mult), f"out_tp{qc}", b)
                elif step == "x1":
                    wait_filled(dve, "attn_proj", b)
                    dve.wait_ge(xbias_ok, 1)
                    done_reading(nc.vector.scalar_tensor_tensor(
                        x[:, ts, :], bank_of("attn_proj", b)[:, 0:C * E].rearrange("p (c e) -> p c e", c=C), tg[:, 0:1],
                        x[:, ts, :], ALU.mult, ALU.add), "attn_proj", b)
                    wait_read(dve, "attn_proj", b)
                    ln_stats(1, ts)
                elif step == "rg0":
                    route_groups(b)
                elif step == "re0":
                    if b:
                        dve.wait_ge(wparts_ok, b)
                    route_experts(b)
                elif step[:2] == "cm":
                    r = n
                    wait_filled(dve, f"comb{r}", b)
                    dve.wait_ge(hid_ok, b * HC + SC + 2 * r + 2)
                    h2 = hid[:, 2 * r:2 * r + 2, :].rearrange("p c s -> p (c s)")
                    done_reading(nc.vector.tensor_tensor(h2, h2, bank_of(f"comb{r}", b)[:, :], ALU.mult), f"comb{r}", b)
                elif step == "x2":
                    wait_filled(dve, "down", b)
                    done_reading(nc.vector.scalar_tensor_tensor(
                        x[:, ts, :], bank_of("down", b)[:, 0:C * E].rearrange("p (c e) -> p c e", c=C), tg_half[:, :],
                        x[:, ts, :], ALU.mult, ALU.add), "down", b)
                    wait_read(dve, "down", b)
                    ln_stats(2, ts)
                elif step == "qvar0":
                    wait_filled(dve, "gram", b)
                    for r in range(C):
                        t = C * b + r
                        last = nc.vector.tensor_tensor_reduce(out=junk[:, :], in0=bank_of("gram", b)[:, r * P:(r + 1) * P],
                                                              in1=xn[:, t, :], scale=1.0, scalar=EPS, op0=ALU.mult,
                                                              op1=ALU.add, accum_out=qvar[:, t:t + 1])
                        if r < C - 1:
                            link(last)
                    done_reading(last, "gram", b)
                elif step in ("z0", "z1"):
                    r = n
                    t = C * b + r
                    dve.wait_ge(qr_ok, b + 1)
                    if b:
                        dve.wait_ge(zs_ok, C * (b - 1) + n + 1)
                    wait_filled(dve, f"q{r}", b)
                    done_reading(nc.vector.scalar_tensor_tensor(z[:, r, :, :].rearrange("p h d -> p (h d)"),
                                                                bank_of(f"q{r}", b)[:, :], qrstd[:, t:t + 1], lnq_b[:, :],
                                                                ALU.mult, ALU.add), f"q{r}", b)
                    wait_read(dve, f"q{r}", b)
                    nc.vector.tensor_reduce(zmx[:, r, :], z[:, r, :, :], AX.X, ALU.max).then_inc(z_ok, 1)
                elif step[:2] == "on":
                    r = n
                    t = C * b + r
                    halves = [(f"oa{r}", 0), (f"ob{r}", 1)]
                    if b:
                        wait_filled(dve, f"n_tp{r}", b - 1)
                    for stage, q in halves:
                        wait_filled(dve, stage, b)
                        ob = bank_of(stage, b)[:, 0:4 * (D1 + 1)].rearrange("p (h e) -> p h e", h=4)
                        last = nc.vector.tensor_scalar(osum[:, r, 4 * q:4 * q + 4], ob[:, :, D1], 1.0 / SCALE1, None, ALU.mult)
                    link(last)
                    link(nc.vector.reciprocal(osum[:, r, :], osum[:, r, :]))
                    for stage, q in halves:
                        ob = bank_of(stage, b)[:, 0:4 * (D1 + 1)].rearrange("p (h e) -> p h e", h=4)
                        done_reading(nc.vector.tensor_tensor(
                            on[:, r, q * 256:(q + 1) * 256].rearrange("p (h e) -> p h e", h=4), ob[:, :, 0:D1],
                            osum[:, r, 4 * q:4 * q + 4].unsqueeze(2).to_broadcast([P, 4, D1]), ALU.mult), stage, b)
                    wait_read(dve, f"oa{r}", b)
                    wait_read(dve, f"ob{r}", b)
                    link(nc.vector.bn_stats(ostat[:, t, :], on[:, r, :]))
                    link(nc.vector.bn_aggr(omv[:, t, :], ostat[:, t, :]))
                    last = nc.vector.tensor_scalar(ove[:, t:t + 1], omv[:, t, 1:2], EPS, None, ALU.add)
                    if r == C - 1:
                        last.then_inc(ov_ok, 1)
                elif step == "x3":
                    wait_filled(dve, "proj1", b)
                    dve.wait_ge(or_ok, b + 1)
                    dve.wait_ge(xb3_ok, b + 1)
                    for r in range(C):
                        t = C * b + r
                        last = nc.vector.scalar_tensor_tensor(x[:, t, :], bank_of("proj1", b)[:, r * E:(r + 1) * E],
                                                              orstd[:, t:t + 1], x[:, t, :], ALU.mult, ALU.add)
                    done_reading(last, "proj1", b)
                    wait_read(dve, "proj1", b)
                    ln_stats(3, ts)
                elif step == "x4":
                    wait_read(dve, "ffn", b)
                    nc.vector.scalar_tensor_tensor(x[:, ts, :], fh[:, :, :], tg[:, 3:4], x[:, ts, :], ALU.mult,
                                                   ALU.add).then_inc(x4_ok, 1)

            for i in ALL_STEPS:
                if i < B * H0:
                    b, h, s, p0 = head(i)
                    g = i // GH
                    dve.wait_ge(s_mm, i + 1)
                    if g >= 2 and i % GH == 0:
                        wait_filled(dve, "max_tp", g - 2)
                    if h == 0:
                        dve.wait_ge(adjm_ok, b + 1)
                    if i >= 2:
                        dve.wait_ge(s_max, i - 1)
                    for qc in range(C):
                        last = nc.vector.tensor_tensor_reduce(
                            out=unread[:, i % 2, qc, :], in0=bankS[i % 2][:, qc * S:(qc + 1) * S], in1=adjm[:, b, qc, :], scale=1.0,
                            scalar=LOWEST, op0=ALU.add, op1=ALU.max,
                            accum_out=mx[:, g % 2, h % 2, qc, s % (GH // 2):s % (GH // 2) + 1])
                    last.then_inc(s_max, 1)
                j = i - LAG
                if 0 <= j < B * H0:
                    dve.wait_ge(t_mm, j + 1)
                    if j == 0:
                        dve.wait_ge(qspill, 16 * 6)
                    if j >= SC_RING:
                        dve.wait_ge(t_exp, j - SC_RING + 1)
                    if j % H0 == 0 and j:
                        dve.wait_ge(adjmT_ok, j // H0 + 1)
                    nc.vector.tensor_tensor(sc_t[:, j % SC_RING, :], bankT[j % 2][:, :],
                                            adjmT[:, j // H0].rearrange("p c s -> p (c s)"),
                                            ALU.add).then_inc(t_add, 1)
                prepare(i)
                if i == H0 * 2:
                    loaded(dve, "moe", "ffn")
                for b, o in offsets(i):
                    for step in DVE_AT.get(o, []):
                        beside(b, step)
            for b, step in TAIL_DVE:
                beside(b, step)

        @block.tensor
        def _(pe):
            mm = nc.tensor.matmul

            def k1_transpose(u):
                pe.wait_ge(k1exp, u + 1)
                if u >= 2:
                    pe.wait_ge(k1n, u - 1)
                for k in range(4):
                    last = nc.tensor.transpose(banks[4 + u % 2][:, k * P:(k + 1) * P], kE[:, u % 2, k * P:(k + 1) * P],
                                               ident[:, :])
                last.then_inc(k1tp, 1)

            loaded(pe, "ctx", "wk")
            for half in range(2):
                mm(banks[4 + half][:, :], w_kT[:, :], ctxT[:, half * HALF:(half + 1) * HALF],
                   start=True, stop=True).then_inc(kproj, 1)

            def k1_unit(u):
                c, half = divmod(u, 2)
                if u == 0:
                    loaded(pe, "w1k")
                if u >= 2:
                    pe.wait_ge(k1exp, u - 1)
                mm(banks[u % 2][:, :], w1kv[:, c * P:(c + 1) * P], ctxT[:, half * HALF:(half + 1) * HALF],
                   start=True, stop=True).then_inc(k1mm, 1)
                if u == 0:
                    loaded(pe, "w1v")
                if u >= 2:
                    pe.wait_ge(v1_ok, u - 1)
                mm(banks[2 + u % 2][:, :], ctxT[:, u * P:(u + 1) * P], w1kv[:, I1:2 * I1],
                   start=True, stop=True).then_inc(v1mm, 1)
                if u == 0:
                    loaded(pe, "id")
                    for half in range(2):
                        pe.wait_ge(ln_xn[0], half + 1)
                        for k in range(HT):
                            last = nc.tensor.transpose(banks[6 + half][:, k * P:(k + 1) * P], xn[:, half * HT + k, :], ident[:, :])
                        last.then_inc(tp0, 1)
                if u == 1:
                    loaded(pe, "wq")
                    for half in range(2):
                        pe.wait_ge(xT0, half + 1)
                        mm(banks[6 + half][:, :], w_qT[:, :], xnT[:, half * HALF:(half + 1) * HALF],
                           start=True, stop=True).then_inc(qproj, 1)
                if u >= 1:
                    if u == 1:
                        pe.wait_ge(k1_ok, 2)
                    k1_transpose(u - 1)
            for u in range(2 * PR):
                k1_unit(u)

            def prepare(i):
                if i == 0:
                    k1_transpose(2 * PR - 1)
                    loaded(pe, "wv")
                    pe.wait_ge(v1_ok, 2 * PR)
                    for t in range(NT):
                        last = mm(banks[2 + t // HT][:, (t % HT) * E:(t % HT + 1) * E], ctxT[:, t * P:(t + 1) * P],
                                  w_vT[:, :], start=True, stop=True)
                        if t % HT == HT - 1:
                            last.then_inc(vproj, 1)
                if i == 1:
                    loaded(pe, "ffn", "l1")
                    pe.wait_ge(k1n, 2 * PR)
                    mm(banks[4][:, 0:E], fa1_T[:, :], fa2[:, :], start=True, stop=True).then_inc(fa12_mm, 1)
                    pe.wait_ge(wqc_ok, 1)
                    for k in range(PR):
                        last = nc.tensor.transpose(banks[5][:, k * P:(k + 1) * P], wq_c[:, k * P:(k + 1) * P], ident[:, :])
                    last.then_inc(wqT_mm, 1)
                if i == 3:
                    pe.wait_ge(fa12_ok, 1)
                    mm(banks[4][:, 0:E], fw_T[:, :], fa12[:, :], start=True, stop=True).then_inc(w3_mm, 1)
                    pe.wait_ge(wqT_ok, 1)
                    for c in range(PR):
                        ws = wq_cT[:, c * P:(c + 1) * P]
                        last = mm(banks[5][:, 0:P], ws, ws, start=(c == 0), stop=(c == PR - 1))
                    last.then_inc(gram_mm, 1)
                for b in CONTEXTS.get(i, []):
                    if b == 2:
                        pe.wait_ge(vaug_ok, 2)
                    for c in range(PR):
                        for k in range(C):
                            t = b * C + k
                            for par in range(2):
                                of_head = slice(c * P + D1 * par, c * P + D1 * (par + 1))
                                last = mm(banks[b][D1 * par:D1 * (par + 1), c * D1:(c + 1) * D1], kEn[:, t, of_head],
                                          v1[:, t, of_head], start=(k == 0), stop=(k == C - 1))
                    last.then_inc(c1mm, 1)
                if i == 5:
                    pe.wait_ge(wog_ok, 1)
                    pe.wait_ge(lnb_ok, 1)
                    pe.wait_ge(w3_ok, 1)
                    pe.wait_ge(consts_ok, 1)
                    for c in range(PR):
                        mm(banks[4][:, 0:E], ones_mean[:, :], wo_g[:, c, :], start=(c == 0), stop=(c == PR - 1))
                    for c in range(PR):
                        last = mm(banks[4][:, E:2 * E], lnb_bc[:, c, :], w1out[:, c, :], start=(c == 0), stop=(c == PR - 1))
                    last.then_inc(wmean_mm, 1)

            loaded(pe, "ones")

            def transposes(stage, b, srcs):
                bank = take_bank(pe, stage, b)
                for k, src in enumerate(srcs):
                    last = nc.tensor.transpose(bank[0:src.shape[1], k * P:(k + 1) * P], src, ident[:, :])
                fill(last, stage, b)

            def beside(b, stage):
                tt = [C * b + r for r in range(C)]
                bank = None
                if stage[:6] == "out_tp":
                    qc = int(stage[6])
                    wait_read(pe, "values", SH * b + SH - 1)
                    transposes(stage, b, [outT[:, n, qc * P:(qc + 1) * P] for n in range(SH)])
                elif stage == "attn_tp":
                    wait_read(pe, "out_tp0", b)
                    wait_read(pe, "out_tp1", b)
                    transposes(stage, b, [attn[:, qc, :] for qc in range(C)])
                elif stage == "attn_proj":
                    bank = take_bank(pe, stage, b)
                    wait_read(pe, "attn_tp", b)
                    for qc in range(C):
                        last = mm(bank[:, qc * E:(qc + 1) * E], attnT[:, qc * P:(qc + 1) * P], w_oT[:, :], start=True, stop=True)
                elif stage[:2] == "tp":
                    pe.wait_ge(ln_xn[int(stage[2])], b + 1)
                    transposes(stage, b, [xn[:, t, :] for t in tt])
                elif stage == "logits":
                    bank = take_bank(pe, stage, b)
                    wait_read(pe, "tp1", b)
                    for r, t in enumerate(tt):
                        last = mm(bank[:, r * EXP0:(r + 1) * EXP0], xnT[:, t * P:(t + 1) * P], w_router[:, :], start=True, stop=True)
                elif stage[:2] == "gu":
                    bank = take_bank(pe, stage, b)
                    wait_read(pe, "tp1", b)
                    c = GU[int(stage[2])]
                    mm(bank[:, 0:S], w_gate[:, c, :], xnT[:, toks(b)], start=True, stop=True)
                    last = mm(bank[:, S:2 * S], w_up[:, c, :], xnT[:, toks(b)], start=True, stop=True)
                elif stage == "wts_tp":
                    bank = take_bank(pe, stage, b)
                    pe.wait_ge(wparts_ok, b + 1)
                    for r in range(C):
                        last = nc.tensor.transpose(bank.bitcast(BF16)[0:3 * EXP0, r * P:(r + 1) * P],
                                                   wparts[:, r, :, :].rearrange("p k e -> p (k e)"), identb[:, :])
                elif stage[:4] == "comb":
                    bank = take_bank(pe, stage, b)
                    wait_read(pe, "wts_tp", b)
                    for k in range(2):
                        last = mm(bank[:, k * S:(k + 1) * S], expand[:, 2 * int(stage[4]) + k, :], combT[:, :], start=True, stop=True)
                elif stage == "down":
                    bank = take_bank(pe, stage, b)
                    pe.wait_ge(hid_ok, (b + 1) * HC)
                    for r in range(C):
                        for n, c in enumerate(GU):
                            if r == 0 and n >= SC and n % 2 == 0:
                                wait_read(pe, f"comb{n // 2 - 1}", b)
                            last = mm(bank[:, r * E:(r + 1) * E], hid[:, c, r * P:(r + 1) * P], w_down[:, c, :],
                                      start=(n == 0), stop=(n == HC - 1))
                elif stage == "gram":
                    bank = take_bank(pe, stage, b)
                    wait_read(pe, "tp2", b)
                    for r, t in enumerate(tt):
                        last = mm(bank[:, r * P:(r + 1) * P], xnT[:, t * P:(t + 1) * P], gram[:, :], start=True, stop=True)
                elif stage in ("q0", "q1"):
                    bank = take_bank(pe, stage, b)
                    wait_read(pe, "tp2", b)
                    t = tt[int(stage[1])]
                    last = mm(bank[:, :], xnT[:, t * P:(t + 1) * P], wq_g[:, :], start=True, stop=True)
                elif stage[:4] == "e_tp":
                    r = int(stage[4])
                    pe.wait_ge(qe_ok, C * b + r + 1)
                    transposes(stage, b, [qE[:, r, c * P:(c + 1) * P] for c in range(PR)])
                elif stage[:2] in ("oa", "ob"):
                    r = int(stage[2])
                    bank = take_bank(pe, stage, b)
                    wait_read(pe, f"e_tp{r}", b)
                    for k in range(2):
                        c = 2 * "ab".index(stage[1]) + k
                        last = mm(bank[:, k * 2 * (D1 + 1):(k + 1) * 2 * (D1 + 1)], qET[:, r, c, :], ctx_bd[:, b * PR + c, :],
                                  start=True, stop=True)
                elif stage[:4] == "n_tp":
                    r = int(stage[4])
                    wait_read(pe, f"oa{r}", b)
                    wait_read(pe, f"ob{r}", b)
                    transposes(stage, b, [on[:, r, c * P:(c + 1) * P] for c in range(PR)])
                elif stage == "proj1":
                    bank = take_bank(pe, stage, b)
                    for r in range(C):
                        wait_read(pe, f"n_tp{r}", b)
                        for c in range(PR):
                            last = mm(bank[:, r * E:(r + 1) * E], onT[:, r, c, :], wo_c[:, c, :], start=(c == 0), stop=(c == PR - 1))
                elif stage == "ffn":
                    bank = take_bank(pe, stage, b)
                    wait_read(pe, "tp3", b)
                    for r, t in enumerate(tt):
                        mm(bank[:, r * E:(r + 1) * E], xnT[:, t * P:(t + 1) * P], w3[:, :], start=True, stop=False)
                        last = mm(bank[:, r * E:(r + 1) * E], ident[:, :], fb_row[:, :], start=False, stop=True)
                if bank is not None:
                    fill(last, stage, b)

            for i in ALL_STEPS:
                if i == 0:
                    pe.wait_ge(qf_ok, 2)
                if i % (2 * H0) == 0 and i < B * H0:
                    pe.wait_ge(kst_ld[i // (2 * H0)], 16 * 2 * len(K_RUNS))
                    pe.wait_ge(qst_ld[i // (2 * H0)], 16 * 2 * len(Q_RUNS))
                if i == GH + 1:
                    pe.wait_ge(c1read, B)
                if i == 2 * H0:
                    pe.wait_ge(bw_ok, 1)
                    pe.wait_ge(gram_ok, 1)
                if i == H0 * 2 + 2:
                    loaded(pe, "moe")
                    pe.wait_ge(ctx_ok, 1)
                if i < B * H0:
                    b, h, s, p0 = head(i)
                    if i >= 2:
                        pe.wait_ge(s_max, i - 1)
                    for qc in range(C):
                        last = mm(bankS[i % 2][:, qc * S:(qc + 1) * S],
                                  qst[p0:p0 + KROWS, s, b * S + qc * P:b * S + (qc + 1) * P],
                                  kst[p0:p0 + KROWS, s, toks(b)], start=True, stop=True)
                    last.then_inc(s_mm, 1)
                prepare(i)
                j = i - LAG
                if 0 <= j < B * H0:
                    b, h, s, p0 = head(j)
                    if j >= 2:
                        pe.wait_ge(t_add, j - 1)
                    if j % GH == 0:
                        g = j // GH
                        pe.wait_ge(m_ld[g % 2], 64 * (g // 2 + 1))
                    for kc in range(C):
                        last = mm(bankT[j % 2][:, kc * S:(kc + 1) * S],
                                  kst[p0:p0 + KROWS + 1, s, b * S + kc * P:b * S + (kc + 1) * P],
                                  qst[p0:p0 + KROWS + 1, s, toks(b)], start=True, stop=True)
                    last.then_inc(t_mm, 1)
                if i % GH == 1 and 1 <= i // GH <= 2 * B:
                    g = i // GH - 1
                    pe.wait_ge(s_max, (g + 1) * GH)
                    transposes("max_tp", g, [mx[:, g % 2, :, :, :].rearrange("p a c s -> p (a c s)")])
                n = v_set(i)
                if n is not None:
                    bank = take_bank(pe, "values", n)
                    pe.wait_ge(t_exp, (n + 1) * SH)
                    b = n // (H0 // SH)
                    for kc in range(C):
                        for k in range(SH):
                            h = (n * SH + k) % H0
                            last = mm(bank[32 * k:32 * k + 32, 0:S], vaug[:, b * C + kc, h * AW:h * AW + 32],
                                      et[:, (n * SH + k) % (2 * SH), kc, :], start=(kc == 0), stop=(kc == C - 1))
                    fill(last, "values", n)
                for b, o in offsets(i):
                    for stage, _ in STAGES.get(o, []):
                        beside(b, stage)
            pe.wait_ge(s_max, B * H0)
            pe.wait_ge(t_add, B * H0)
            for b, stage, _ in TAIL_PE:
                beside(b, stage)


def kernel(**inputs):
    import numpy as np
    import concourse.bacc as bacc
    from ml_dtypes import bfloat16 as bf16
    from concourse.bass_utils import run_bass_kernel_spmd as run

    I = {k: np.asarray(v) for k, v in inputs.items()}

    def rows(v):
        return np.broadcast_to(v.reshape(1, -1), (P, v.size))

    def tiles(v):
        return v.reshape(-1, P, v.shape[-1]).transpose(1, 0, 2)

    order = np.arange(E).reshape(SLOTS, 2, D0).transpose(1, 2, 0).reshape(-1)
    mask = I["mask_Bx1xSxS2_ik1"][:, 0]
    lay = {
        "x": tiles(I["x"].reshape(N, E)),
        "ctxT": I["ctx_1024"].reshape(N, E).T,
        "wkT": I["L0_xattn_Wk"].T[:, order], "wqT": I["L0_xattn_Wq"].T[:, order],
        "wvT": I["L0_xattn_Wv"].T, "woT": I["L0_xattn_Wo"].T,
        "bq": I["L0_xattn_bq"][order].reshape(P, 1), "bk": I["L0_xattn_bk"][order].reshape(P, 1),
        "bv": rows(I["L0_xattn_bv"]), "bo": rows(I["L0_xattn_bo"]),
        "gates": rows(np.concatenate([I["g_xattn"], I["g_ffn"]])),
        "ident": np.eye(P, dtype=np.float32), "identb": np.eye(P).astype(bf16),
        "ones": np.ones((2, SLOTS, N), bf16),
        "tri": np.broadcast_to(np.tril(np.ones((4, 4), np.float32), -1), (P, 4, 4)),
        "expand": np.tile(np.repeat(np.eye(EXP0), HID, 1), (3, 1)).astype(bf16).reshape(3 * EXP0, RC, P),
        "adj": tiles(I["L0_xattn_adj"]), "adjT": tiles(I["L0_xattn_adj"].T),
        "mask": mask.reshape(B, C, P, S).transpose(2, 0, 1, 3),
        "maskT": mask.transpose(0, 2, 1).reshape(B, C, P, S).transpose(2, 0, 1, 3),
        "router_w": I["L0_ffn_router_w"].T, "cb": rows(I["L0_ffn_correction_bias"]),
        "gate_w": I["L0_ffn_gate_w"].transpose(1, 0, 2).reshape(P, RC, P),
        "up_w": I["L0_ffn_up_w"].transpose(1, 0, 2).reshape(P, RC, P),
        "down_w": tiles(I["L0_ffn_down_w"].reshape(EXP0 * HID, E)),
        "sgate_w": I["L0_ffn_shared_gate_w"].T.reshape(P, SC, P), "sup_w": I["L0_ffn_shared_up_w"].T.reshape(P, SC, P),
        "sdown_w": tiles(I["L0_ffn_shared_down_w"].T),
        "w1q": I["L1_xattn_Wq"], "w1kv": I["L1_xattn_Wkv"], "w1out": tiles(I["L1_xattn_Wout"]),
        "nullk": np.concatenate([I["L1_xattn_null_kv"][0]] * 2).reshape(P, 1), "nullv": rows(I["L1_xattn_null_kv"][1]),
        "lnq_g": rows(I["L1_xattn_ln_q_g"]), "lnq_b": rows(I["L1_xattn_ln_q_b"]),
        "lno_g": I["L1_xattn_ln_out_g"].reshape(PR, P).T, "lno_b": I["L1_xattn_ln_out_b"].reshape(PR, P).T,
        "fwT": I["L1_ffn_weight"].T, "fa1T": I["L1_ffn_aux_weight1"].T, "fa2": I["L1_ffn_aux_weight2"],
        "fb": rows(I["L1_ffn_bias"]),
    }
    nc = bacc.Bacc("TRN2", target_bir_lowering=False, num_devices=1)
    arrays, A = {}, {}
    for name, a in lay.items():
        a = np.ascontiguousarray(a)
        arrays[f"in_{name}"] = a
        A[name] = nc.dram_tensor(f"in_{name}", a.shape, mybir.dt.from_np(a.dtype), kind="ExternalInput").ap()
    out = nc.dram_tensor("out", (P, NT, E), F32, kind="ExternalOutput").ap()
    build(nc, A, out)
    r = run(nc, [arrays], core_ids=[0])
    return r.results[0]["out"].transpose(1, 0, 2).reshape(B, S, E)
```
